# Optimizing a Trainium2 kernel written in Bass

```python
import numpy as np
import jax
import jax.numpy as jnp

def _softmax(x, axis=-1):
    return jax.nn.softmax(x, axis=axis)

def _gelu(x):
    return jax.nn.gelu(x, approximate=True)

def _silu(x):
    return jax.nn.silu(x)

def _sigmoid(x):
    return jax.nn.sigmoid(x)

def _layernorm(x, axis=-1, eps=1e-05):
    m = jnp.mean(x, axis=axis, keepdims=True)
    v = jnp.var(x, axis=axis, keepdims=True)
    return (x - m) / jnp.sqrt(v + eps)

def _scatter_add(tgt, idx, src, axis=0):
    return tgt.at[idx].add(src)

def _segment_sum(src, seg, n):
    return jax.ops.segment_sum(src, seg, n)
kernel_name = 'mk_hybrid_d1_jaxref_r4_08202f'

def setup_inputs(seed: int=0):
    np.random.seed(seed)
    _w = jnp.asarray

    def _L0_attn_a_setup():
        import jax, jax.numpy as jnp
        import numpy as np
        B, S, D, H = (2, 512, 256, 16)
        HD = D // H
        key = jax.random.key(seed)
        k1, k2, k3 = jax.random.split(key, 3)
        x = jax.random.normal(k1, (B, S, D), dtype=jnp.float32)
        c_attn_kernel = 0.02 * jax.random.normal(k2, (3 * D, D), dtype=jnp.float32)
        c_attn_bias = jnp.zeros((3 * D,), dtype=jnp.float32)
        c_proj_kernel = 0.02 * jax.random.normal(k3, (D, D), dtype=jnp.float32)
        c_proj_bias = jnp.zeros((D,), dtype=jnp.float32)
        return {'hidden_states': x, 'c_attn_kernel': c_attn_kernel, 'c_attn_bias': c_attn_bias, 'c_proj_kernel': c_proj_kernel, 'c_proj_bias': c_proj_bias}
    _L0_attn_a_in = _L0_attn_a_setup()

    def _L0_attn_b_setup():
        import jax, jax.numpy as jnp
        import numpy as np
        B, T, D, H = (2, 512, 256, 16)
        HD = D // H
        key = jax.random.key(seed)
        ks = jax.random.split(key, 9)
        w = lambda k, shp: jax.random.normal(k, shp, jnp.float32) * 0.02
        return {'x': jax.random.normal(ks[0], (B, T, D), jnp.float32), 'Wq': w(ks[1], (D, D)), 'bq': jnp.zeros((D,), jnp.float32), 'Wk': w(ks[2], (D, D)), 'bk': jnp.zeros((D,), jnp.float32), 'Wv': w(ks[3], (D, D)), 'bv': jnp.zeros((D,), jnp.float32), 'Wo': w(ks[4], (D, D)), 'bo': jnp.zeros((D,), jnp.float32), 'Wqs': w(ks[5], (3, HD)), 'bqs': jnp.zeros((3,), jnp.float32), 'Wks': w(ks[6], (3, HD)), 'bks': jnp.zeros((3,), jnp.float32), 'Wvs': w(ks[7], (3, HD)), 'bvs': jnp.zeros((3,), jnp.float32), 'temp': jnp.float32(1.0)}
    _L0_attn_b_in = _L0_attn_b_setup()

    def _L0_ffn_setup():
        import jax, jax.numpy as jnp
        import numpy as np
        D = 256
        H = 512
        E = 8
        TOP_K = 2
        N_SHARED = 1
        B, S = (2, 256)
        key = jax.random.key(seed)
        ks = jax.random.split(key, 12)
        sc = 0.02
        return {'hidden': jax.random.normal(ks[0], (B, S, D), jnp.float32), 'router_w': jax.random.normal(ks[1], (D, E), jnp.float32) * sc, 'router_b': jnp.zeros((E,), jnp.float32), 'sw1': jax.random.normal(ks[2], (D, H), jnp.float32) * sc, 'sb1': jnp.zeros((H,), jnp.float32), 'sw2': jax.random.normal(ks[3], (H, D), jnp.float32) * sc, 'sb2': jnp.zeros((D,), jnp.float32), 'rw1': jax.random.normal(ks[4], (E, D, H), jnp.float32) * sc, 'rb1': jnp.zeros((E, H), jnp.float32), 'rw2': jax.random.normal(ks[5], (E, H, D), jnp.float32) * sc, 'rb2': jnp.zeros((E, D), jnp.float32)}
    _L0_ffn_in = _L0_ffn_setup()
    _d = {'L0_attn_a_hidden_states': _L0_attn_a_in['hidden_states'], 'L0_attn_a_c_attn_kernel': _L0_attn_a_in['c_attn_kernel'], 'L0_attn_a_c_attn_bias': _L0_attn_a_in['c_attn_bias'], 'L0_attn_a_c_proj_kernel': _L0_attn_a_in['c_proj_kernel'], 'L0_attn_a_c_proj_bias': _L0_attn_a_in['c_proj_bias'], 'L0_attn_b_Wq': _L0_attn_b_in['Wq'], 'L0_attn_b_bq': _L0_attn_b_in['bq'], 'L0_attn_b_Wk': _L0_attn_b_in['Wk'], 'L0_attn_b_bk': _L0_attn_b_in['bk'], 'L0_attn_b_Wv': _L0_attn_b_in['Wv'], 'L0_attn_b_bv': _L0_attn_b_in['bv'], 'L0_attn_b_Wo': _L0_attn_b_in['Wo'], 'L0_attn_b_bo': _L0_attn_b_in['bo'], 'L0_attn_b_Wqs': _L0_attn_b_in['Wqs'], 'L0_attn_b_bqs': _L0_attn_b_in['bqs'], 'L0_attn_b_Wks': _L0_attn_b_in['Wks'], 'L0_attn_b_bks': _L0_attn_b_in['bks'], 'L0_attn_b_Wvs': _L0_attn_b_in['Wvs'], 'L0_attn_b_bvs': _L0_attn_b_in['bvs'], 'L0_attn_b_temp': _L0_attn_b_in['temp'], 'L0_ffn_router_w': _L0_ffn_in['router_w'], 'L0_ffn_router_b': _L0_ffn_in['router_b'], 'L0_ffn_sw1': _L0_ffn_in['sw1'], 'L0_ffn_sb1': _L0_ffn_in['sb1'], 'L0_ffn_sw2': _L0_ffn_in['sw2'], 'L0_ffn_sb2': _L0_ffn_in['sb2'], 'L0_ffn_rw1': _L0_ffn_in['rw1'], 'L0_ffn_rb1': _L0_ffn_in['rb1'], 'L0_ffn_rw2': _L0_ffn_in['rw2'], 'L0_ffn_rb2': _L0_ffn_in['rb2']}
    _x0 = _d['L0_attn_a_hidden_states']
    _d['L0_attn_a_hidden_states'] = jax.random.normal(jax.random.fold_in(jax.random.key(seed), 1), (2, 2048, 256), dtype=_x0.dtype)
    del _x0
    return _d

def reference(L0_attn_a_hidden_states, L0_attn_a_c_attn_kernel, L0_attn_a_c_attn_bias, L0_attn_a_c_proj_kernel, L0_attn_a_c_proj_bias, L0_attn_b_Wq, L0_attn_b_bq, L0_attn_b_Wk, L0_attn_b_bk, L0_attn_b_Wv, L0_attn_b_bv, L0_attn_b_Wo, L0_attn_b_bo, L0_attn_b_Wqs, L0_attn_b_bqs, L0_attn_b_Wks, L0_attn_b_bks, L0_attn_b_Wvs, L0_attn_b_bvs, L0_attn_b_temp, L0_ffn_router_w, L0_ffn_router_b, L0_ffn_sw1, L0_ffn_sb1, L0_ffn_sw2, L0_ffn_sb2, L0_ffn_rw1, L0_ffn_rb1, L0_ffn_rw2, L0_ffn_rb2):

    def _L0_attn_a_ref(hidden_states, c_attn_kernel, c_attn_bias, c_proj_kernel, c_proj_bias):
        import jax, jax.numpy as jnp
        import numpy as np
        B, S, D, H = (2, 512, 256, 16)
        HD = D // H
        b, s, d = hidden_states.shape
        qkv = hidden_states @ c_attn_kernel.T + c_attn_bias
        q, k, v = jnp.split(qkv, 3, axis=2)
        q = q.reshape(b, s, H, HD)
        k = k.reshape(b, s, H, HD)
        v = v.reshape(b, s, H, HD)
        causal = jnp.tril(jnp.ones((s, s), dtype=bool))
        neg = jnp.finfo(jnp.float32).min
        bias = jnp.where(causal, 0.0, neg).astype(jnp.float32)
        scale = 1.0 / jnp.sqrt(jnp.float32(HD))
        scores = jnp.einsum('bqhd,bkhd->bhqk', q * scale, k) + bias
        attn_weights = jax.nn.softmax(scores, axis=-1)
        attn_output = jnp.einsum('bhqk,bkhd->bqhd', attn_weights, v)
        attn_output = attn_output.reshape(b, s, d)
        out = attn_output @ c_proj_kernel.T + c_proj_bias
        return out

    def _L0_attn_b_ref(x, Wq, bq, Wk, bk, Wv, bv, Wo, bo, Wqs, bqs, Wks, bks, Wvs, bvs, temp):
        import jax, jax.numpy as jnp
        import numpy as np
        B, T, D, H = (2, 512, 256, 16)
        HD = D // H
        Bx, Tx, Dx = x.shape
        split = lambda y: y.reshape(Bx, Tx, H, HD).transpose(0, 2, 1, 3)
        q = split(x @ Wq.T + bq)
        k = split(x @ Wk.T + bk)
        v = split(x @ Wv.T + bv)
        q_stp = q @ Wqs.T + bqs
        k3 = k @ Wks.T + bks
        v3 = v @ Wvs.T + bvs
        cross_kv = jnp.cross(k3, v3, axis=-1)
        scores = (jnp.einsum('bhqd,bhkd->bhqk', q, k) + jnp.einsum('bhqc,bhkc->bhqk', q_stp, cross_kv)) * temp
        attn = jax.nn.softmax(scores, axis=-1)
        out = jnp.einsum('bhqk,bhkd->bhqd', attn, v)
        out = out.transpose(0, 2, 1, 3).reshape(Bx, Tx, Dx)
        return out @ Wo.T + bo

    def _L0_ffn_ref(hidden, router_w, router_b, sw1, sb1, sw2, sb2, rw1, rb1, rw2, rb2):
        import jax, jax.numpy as jnp
        import numpy as np
        D = 256
        H = 512
        E = 8
        TOP_K = 2
        N_SHARED = 1
        B, S = (2, 256)
        b, s, d = hidden.shape
        T = b * s
        flat = hidden.reshape(T, d)
        router_logits = flat @ router_w + router_b
        router_probs = jax.nn.softmax(router_logits, axis=-1)
        topk_probs, topk_idx = jax.lax.top_k(router_probs, TOP_K)
        weights = jnp.zeros_like(router_probs).at[jnp.arange(T)[:, None], topk_idx].add(topk_probs)
        sh = jax.nn.gelu(flat @ sw1 + sb1, approximate=False)
        shared_out = (sh @ sw2 + sb2) / N_SHARED
        h1 = jax.nn.gelu(jnp.einsum('td,edh->teh', flat, rw1) + rb1[None], approximate=False)
        expert_out = jnp.einsum('teh,ehd->ted', h1, rw2) + rb2[None]
        mixed = jnp.einsum('ted,te->td', expert_out, weights)
        return (shared_out + mixed).reshape(b, s, d)
    x = L0_attn_a_hidden_states
    x = x + _L0_attn_a_ref(_layernorm(x, axis=-1), L0_attn_a_c_attn_kernel, L0_attn_a_c_attn_bias, L0_attn_a_c_proj_kernel, L0_attn_a_c_proj_bias)
    x = x + _L0_ffn_ref(_layernorm(x, axis=-1), L0_ffn_router_w, L0_ffn_router_b, L0_ffn_sw1, L0_ffn_sb1, L0_ffn_sw2, L0_ffn_sb2, L0_ffn_rw1, L0_ffn_rb1, L0_ffn_rw2, L0_ffn_rb2)
    x = x + _L0_attn_b_ref(_layernorm(x, axis=-1), L0_attn_b_Wq, L0_attn_b_bq, L0_attn_b_Wk, L0_attn_b_bk, L0_attn_b_Wv, L0_attn_b_bv, L0_attn_b_Wo, L0_attn_b_bo, L0_attn_b_Wqs, L0_attn_b_bqs, L0_attn_b_Wks, L0_attn_b_bks, L0_attn_b_Wvs, L0_attn_b_bvs, L0_attn_b_temp)
    x = x + _L0_ffn_ref(_layernorm(x, axis=-1), L0_ffn_router_w, L0_ffn_router_b, L0_ffn_sw1, L0_ffn_sb1, L0_ffn_sw2, L0_ffn_sb2, L0_ffn_rw1, L0_ffn_rb1, L0_ffn_rw2, L0_ffn_rb2)
    return x

_drawn_inputs = setup_inputs


def setup_inputs(seed=0):
    import zlib

    import numpy as np

    out = dict(_drawn_inputs(seed))
    spreads = {'L0_attn_a_c_attn_bias': (0.0, 0.1),
     'L0_attn_a_c_proj_bias': (0.0, 0.1),
     'L0_attn_b_bq': (0.0, 0.8),
     'L0_attn_b_bk': (0.0, 0.8),
     'L0_attn_b_bv': (0.0, 0.1),
     'L0_attn_b_bo': (0.0, 0.1),
     'L0_attn_b_bqs': (0.0, 0.8),
     'L0_attn_b_bks': (0.0, 0.8),
     'L0_attn_b_bvs': (0.0, 0.8),
     'L0_ffn_router_b': (0.0, 0.345),
     'L0_ffn_sb1': (0.0, 0.1),
     'L0_ffn_sb2': (0.0, 0.1),
     'L0_ffn_rb1': (0.0, 0.652),
     'L0_ffn_rb2': (0.0, 0.1)}
    factors = {'L0_attn_a_c_attn_kernel': 8.0,
     'L0_attn_b_Wq': 8.0,
     'L0_attn_b_Wk': 8.0,
     'L0_attn_b_Wv': 3.322,
     'L0_attn_b_Wqs': 8.0,
     'L0_attn_b_Wks': 8.0,
     'L0_attn_b_Wvs': 8.0}
    for name, (base, spread) in spreads.items():
        noise = np.random.default_rng([zlib.crc32(name.encode()), seed]).standard_normal(out[name].shape)
        drawn = base * np.exp(spread * noise) if base else spread * noise
        out[name] = jnp.asarray(drawn.astype(out[name].dtype))
    for name, factor in factors.items():
        out[name] = (out[name] * factor).astype(out[name].dtype)
    return out
```

```python
from contextlib import ExitStack

import concourse.bass as bass
from concourse import mybir

F32 = mybir.dt.float32
BF16 = mybir.dt.bfloat16
ALU = mybir.AluOpType
ACT = mybir.ActivationFunctionType
AX = mybir.AxisListType

P = 128
B, S, D = 2, 2048, 256
T = B * S
NT = T // P
H, HD = 16, 16
U = B * H
KT = S // P
KD = D // P
G = 512
NG = T // G
GT = G // P
NE, HID = 8, 512
EX = NE + 1
SH = NE
HT = HID // P
C3 = 3
XR = H * C3
EPS = 1e-5
NEG = -1e30
LOWEST = -3e38

Q_RUNS = [(0, 1, 3), (1, 1, 2), (2, 1, 1)]
K_RUNS = [(0, 3, 1), (0, 2, 1), (0, 1, 1)]


def build(nc, io, out):
    ctx = ExitStack()
    with ctx:
        def sb(name, shape, dt=F32, at=ctx):
            return at.enter_context(nc.sbuf_tensor(name, shape, dt))

        def pb(name, shape, at, dt=F32):
            return at.enter_context(nc.psum_tensor(name, shape, dt))

        def sem(name):
            return ctx.enter_context(nc.semaphore(name))

        scratch = {}
        for side in "qk":
            scratch[side] = nc.dram_tensor(f"{side}_pieces", [B, 3, D, S], BF16, kind="Internal").ap()
            scratch[side + "x"] = nc.dram_tensor(f"{side}x_pieces", [B, 3, XR, S], BF16, kind="Internal").ap()

        big = dict(
            X=sb("X", [P, NT * D]),
            w1=sb("w1", [P, EX, KD, HID]),
            w2=sb("w2", [P, EX, HT, D]),
            b1=sb("b1", [P, EX, HT]),
            b2=sb("b2", [EX, D]),
            rw=sb("rw", [P, KD, NE]),
            rb=sb("rb", [P, NE]),
            WT=sb("WT", [P, KD, 8 * D]),
            bcolA=sb("bcolA", [P, 6]),
            bcolB=sb("bcolB", [P, 6]),
            scolA=sb("scolA", [P, 1]),
            scolB=sb("scolB", [P, 1]),
            vbA=sb("vbA", [P, D]), vbB=sb("vbB", [P, D]),
            obA=sb("obA", [P, D]), obB=sb("obB", [P, D]),
            XW=sb("XW", [P, KD, 5, XR]),
            xb=sb("xb", [P, 3]),
            identF=sb("identF", [P, P]),
            identB=sb("identB", [P, P], BF16),
            maskK=sb("maskK", [P, P], BF16),
            maskQ=sb("maskQ", [P, P], BF16),
            mv=sb("mv", [P, NT, 2]), std=sb("std", [P, NT]), rstd=sb("rstd", [P, NT]),
            eps=sb("eps", [P, 1]),
        )
        ffn_loaded = sem("ffn_loaded")
        setup(nc, io, big, sb, pb, sem, ffn_loaded)
        attention(nc, "A", True, big, scratch, sb, pb, sem)
        experts(nc, "A", big, sb, pb, sem, ffn_loaded)
        attention(nc, "B", False, big, scratch, sb, pb, sem)
        experts(nc, "B", big, sb, pb, sem, ffn_loaded)
        finish(nc, out, big, sem)


def chain(eng, sem, base=0):
    n = [0]

    def link(ins):
        n[0] += 1
        ins.then_inc(sem, 1)
        eng.wait_ge(sem, base + n[0])
    link.count = n
    return link


def setup(nc, io, big, sb, pb, sem, ffn_loaded):
    with ExitStack() as st:
        natural = sb("natural", [P, 16, D], F32, st)
        wcol = sb("wcol", [P, 3, C3], F32, st)
        blockdiag = sb("blockdiag", [P, 5, 2, H, C3], F32, st)
        xb_in = sb("xb_in", [P, 3], F32, st)
        banks = [pb(f"setup_ps{i}", [P, 512], st) for i in range(8)]
        X = big["X"]
        x_loaded, w_loaded, small_loaded = sem("x_loaded"), sem("w_loaded"), sem("small_loaded")
        ident_made, masks_made, bd_link = sem("ident_made"), sem("masks_made"), sem("bd_link")
        turned, turned_out, comp_done, comp_out = sem("turned"), sem("turned_out"), sem("comp_done"), sem("comp_out")
        zeroed = sem("zeroed")
        block = st.enter_context(nc.Block())
        sets = [(0, 0), (1, 1), (1, 2), (2, 2), (2, 1)]
        small = []

        x_view = io["L0_attn_a_hidden_states"].rearrange("b (t p) d -> p (b t) d", p=P)
        X3 = X[:, :].rearrange("p (t d) -> p t d", d=D)

        @block.sync
        def _(sp):
            names = [("L0_attn_a_c_attn_kernel", 0, 6), ("L0_attn_a_c_proj_kernel", 6, 2), ("L0_attn_b_Wq", 8, 2),
                     ("L0_attn_b_Wk", 10, 2), ("L0_attn_b_Wv", 12, 2), ("L0_attn_b_Wo", 14, 2)]
            for name, at, n in names:
                sp.dma_start(natural[:, at:at + n, :], io[name].rearrange("(m p) d -> p m d", p=P)).then_inc(w_loaded, 16)
            for g in range(NG):
                sp.dma_start(X3[:, g * GT:(g + 1) * GT, :], x_view[:, g * GT:(g + 1) * GT, :]).then_inc(x_loaded, 16)
            for e in range(EX):
                src = io["L0_ffn_sw1"] if e == SH else io["L0_ffn_rw1"][e]
                sp.dma_start(big["w1"][:, e, :, :], src.rearrange("(k p) h -> p k h", p=P)).then_inc(ffn_loaded, 16)
                src = io["L0_ffn_sw2"] if e == SH else io["L0_ffn_rw2"][e]
                sp.dma_start(big["w2"][:, e, :, :], src.rearrange("(k p) d -> p k d", p=P)).then_inc(ffn_loaded, 16)
            sp.wait_ge(x_loaded, 16 * NG)

        @block.scalar
        def _(act):
            def load(dst, src):
                act.dma_start(dst, src, allow_slow_non_contiguous=True).then_inc(small_loaded, 16)
                small.append(1)
            for i, n in enumerate(("L0_attn_b_Wqs", "L0_attn_b_Wks", "L0_attn_b_Wvs")):
                for r in range(P // HD):
                    load(wcol[r * HD:(r + 1) * HD, i, :], io[n].rearrange("c d -> d c"))
            load(big["bcolA"][:, :], io["L0_attn_a_c_attn_bias"].rearrange("(m p) -> p m", p=P))
            for i, n in enumerate(("L0_attn_b_bq", "L0_attn_b_bk", "L0_attn_b_bv")):
                load(big["bcolB"][:, 2 * i:2 * i + 2], io[n].rearrange("(m p) -> p m", p=P))
            load(big["scolB"][:, :], io["L0_attn_b_temp"].partition_broadcast(P))
            load(big["vbA"][:, :], io["L0_attn_a_c_attn_bias"][2 * D:3 * D].partition_broadcast(P))
            load(big["obA"][:, :], io["L0_attn_a_c_proj_bias"].partition_broadcast(P))
            load(big["vbB"][:, :], io["L0_attn_b_bv"].partition_broadcast(P))
            load(big["obB"][:, :], io["L0_attn_b_bo"].partition_broadcast(P))
            load(big["rb"][:, :], io["L0_ffn_router_b"].partition_broadcast(P))
            load(big["rw"][:, :, :], io["L0_ffn_router_w"].rearrange("(k p) e -> p k e", p=P))
            load(big["b1"][:, 0:NE, :], io["L0_ffn_rb1"].rearrange("e (m p) -> p e m", p=P))
            load(big["b1"][:, SH, :], io["L0_ffn_sb1"].rearrange("(m p) -> p m", p=P))
            load(big["b2"][0:NE, :], io["L0_ffn_rb2"])
            load(big["b2"][SH:SH + 1, :], io["L0_ffn_sb2"].rearrange("(a d) -> a d", a=1))
            for (src, rot), (row, col) in zip(sets, [(0, 0), (0, 1), (64, 1), (0, 2), (64, 2)]):
                b = io[("L0_attn_b_bqs", "L0_attn_b_bks", "L0_attn_b_bvs")[src]]
                for c in range(C3):
                    f = (c + rot) % C3
                    load(xb_in[row + c:row + c + 3 * (H - 1) + 1:3, col:col + 1],
                         b[f:f + 1].partition_broadcast(H))

        @block.gpsimd
        def _(pool):
            pool.memset(big["identF"][:, :], 0.0).then_inc(zeroed, 1)
            pool.memset(big["identB"][:, :], 0.0).then_inc(zeroed, 1)
            pool.memset(big["maskK"][:, :], 0.0).then_inc(zeroed, 1)
            pool.memset(big["maskQ"][:, :], 0.0).then_inc(zeroed, 1)
            pool.memset(big["scolA"][:, :], HD ** -0.5).then_inc(zeroed, 1)
            pool.memset(big["eps"][:, :], EPS).then_inc(zeroed, 1)
            pool.wait_ge(zeroed, 6)
            for m in ("identF", "identB"):
                pool.affine_select(out=big[m][:, :], in_=big[m][:, :], compare_op=ALU.not_equal, fill=1.0, base=0,
                                   pattern=[[-1, P]], channel_multiplier=1).then_inc(ident_made, 1)
            pool.affine_select(out=big["maskK"][:, :], in_=big["maskK"][:, :], compare_op=ALU.is_ge, fill=NEG, base=0,
                               pattern=[[1, P]], channel_multiplier=-1).then_inc(masks_made, 1)
            pool.affine_select(out=big["maskQ"][:, :], in_=big["maskQ"][:, :], compare_op=ALU.is_ge, fill=NEG, base=0,
                               pattern=[[-1, P]], channel_multiplier=1).then_inc(masks_made, 1)
            pool.wait_ge(small_loaded, 16 * len(small))
            for s, (src, rot) in enumerate(sets):
                for c in range(C3):
                    f = (c + rot) % C3
                    pool.tensor_copy(blockdiag[:, s, :, :, c],
                                     wcol[:, src, f:f + 1].unsqueeze(2).to_broadcast([P, 2, H])).then_inc(bd_link, 1)
            n = 15
            pool.wait_ge(bd_link, n)
            pool.affine_select(out=blockdiag[:, :, :, :, :], in_=blockdiag[:, :, :, :, :], compare_op=ALU.is_ge,
                               fill=0.0, base=0, pattern=[[0, 5], [P, 2], [-HD, H], [0, C3]],
                               channel_multiplier=1).then_inc(bd_link, 1)
            pool.wait_ge(bd_link, n + 1)
            pool.affine_select(out=blockdiag[:, :, :, :, :], in_=blockdiag[:, :, :, :, :], compare_op=ALU.is_ge,
                               fill=0.0, base=HD - 1, pattern=[[0, 5], [-P, 2], [HD, H], [0, C3]],
                               channel_multiplier=-1).then_inc(bd_link, 1)

        @block.tensor
        def _(pe):
            pe.wait_ge(ident_made, 1)
            pe.wait_ge(w_loaded, 16 * 6)
            for n in range(8):
                kk, m0 = n // 4, 4 * (n % 4)
                if n >= 4:
                    pe.wait_ge(turned_out, n - 3)
                for j in range(4):
                    last = nc.tensor.transpose(banks[n % 4][:, j * P:(j + 1) * P],
                                               natural[:, m0 + j, kk * P:(kk + 1) * P], big["identF"][:, :])
                last.then_inc(turned, 1)
            pe.wait_ge(bd_link, 17)
            for kk in range(KD):
                for s, (src, _rot) in enumerate(sets):
                    at = (kk * 5 + s) * XR
                    for half in range(2):
                        last = nc.tensor.matmul(banks[4][:, at:at + XR],
                                                natural[:, 8 + 2 * src + half, kk * P:(kk + 1) * P],
                                                blockdiag[:, s, half, :, :].rearrange("p h c -> p (h c)"),
                                                start=half == 0, stop=half == 1)
            last.then_inc(comp_done, 1)
            for (s, (src, _rot)), (row, col) in zip(enumerate(sets), [(0, 0), (0, 1), (64, 1), (0, 2), (64, 2)]):
                for half in range(2):
                    last = nc.tensor.matmul(banks[5][row:row + XR, col:col + 1],
                                            blockdiag[:, s, half, :, :].rearrange("p h c -> p (h c)"),
                                            big["bcolB"][:, 2 * src + half:2 * src + half + 1],
                                            start=half == 0, stop=half == 1)
            last.then_inc(comp_done, 1)

        @block.vector
        def _(dve):
            for n in range(8):
                dve.wait_ge(turned, n + 1)
                kk, m0 = n // 4, 4 * (n % 4)
                nc.vector.tensor_copy(big["WT"][:, kk, m0 * P:(m0 + 4) * P], banks[n % 4][:, :]).then_inc(turned_out, 1)
            dve.wait_ge(comp_done, 1)
            nc.vector.tensor_copy(big["XW"][:, :, :, :].rearrange("p k s r -> p (k s r)"),
                                  banks[4][:, 0:10 * XR]).then_inc(comp_out, 1)
            dve.wait_ge(comp_done, 2)
            dve.wait_ge(small_loaded, 16 * len(small))
            for row, cols in ((0, slice(0, 3)), (64, slice(1, 3))):
                nc.vector.tensor_tensor(big["xb"][row:row + XR, cols], banks[5][row:row + XR, cols],
                                        xb_in[row:row + XR, cols], ALU.add).then_inc(comp_out, 1)


def norm_stats(nc, dve, link, big, stats):
    X = big["X"]
    for t in range(NT):
        last = nc.vector.bn_stats(stats[:, t, :], X[:, t * D:(t + 1) * D])
    link(last)
    for t in range(NT):
        last = nc.vector.bn_aggr(big["mv"][:, t, :], stats[:, t, :])
    link(last)


def attention(nc, tag, causal, big, scratch, sb, pb, sem):
    with ExitStack() as st:
        V = sb(f"V{tag}", [P, NT * D], F32, st)
        project(nc, tag, causal, big, scratch, V, sb, pb, sem)
        units(nc, tag, causal, big, scratch, V, sb, pb, sem)
        combine(nc, tag, big, V, sb, pb, sem)


def project(nc, tag, causal, big, scratch, V, sb, pb, sem):
    extra = not causal
    NI = 6 if extra else 4
    NPC = 4
    NPQ = 5 if extra else 4
    w0 = 0 if causal else 4 * D
    bcol = big["bcolA"] if causal else big["bcolB"]
    scol = big["scolA"] if causal else big["scolB"]
    vb = big["vbA"] if causal else big["vbB"]
    X = big["X"]
    with ExitStack() as st:
        stats = sb(f"stats{tag}", [P, NT, 6], F32, st)
        XN = [sb(f"XN{tag}{i}", [P, GT, D], F32, st) for i in range(2)]
        xT = [sb(f"xT{tag}{i}", [P, KD, G], F32, st) for i in range(2)]
        Y = [sb(f"Y{tag}{i}", [P, G], F32, st) for i in range(2)]
        R = [sb(f"R{tag}{i}", [P, G], F32, st) for i in range(2)]
        PC = [sb(f"PC{tag}{i}", [P, 3, G], BF16, st) for i in range(NPC)]
        if extra:
            V1V2 = sb(f"V1V2{tag}", [P, G], F32, st)
            prodA = sb(f"prodA{tag}", [XR, G], F32, st)
            prodB = sb(f"prodB{tag}", [XR, G], F32, st)
        qbias = sb(f"qbias{tag}", [P, 3], F32, st)
        TP = [pb(f"TP{tag}{i}", [P, G], st) for i in range(2)]
        PQ = [pb(f"PQ{tag}{i}", [P, G], st) for i in range(2)]
        PV = [pb(f"PV{tag}{i}", [P, G], st) for i in range(2)]
        PE_ = [pb(f"PE{tag}{i}", [P, G], st) for i in range(2)] if extra else None
        s = {n: sem(f"{n}{tag}") for n in (
            "ln_link", "root_done", "rstd_done", "xn_ready", "turned", "xT_ready", "qk_ready", "qk_read", "y_ready",
            "r_ready", "p1_ready", "p2_ready", "v_ready", "v_read", "ex_ready", "vv_ready", "prod_link", "cross_ready")}
        stored = [sem(f"stored{tag}{i}") for i in range(NPC)]

        def pieces_free(eng, i, k):
            eng.wait_ge(stored[k % NPC], 16 * (i * (2 * NI // NPC) + k // NPC))

        block = st.enter_context(nc.Block())

        def groups(eng):
            with eng.Fori(0, NG // 2) as i:
                for par in range(2):
                    yield i, par, 2 * i + par

        @block.vector
        def _(dve):
            link = chain(dve, s["ln_link"])
            norm_stats(nc, dve, link, big, stats)
            dve.wait_ge(s["root_done"], 1)
            nc.vector.reciprocal(big["rstd"][:, :], big["std"][:, :]).then_inc(s["rstd_done"], 1)
            for m in range(2):
                nc.vector.tensor_tensor(qbias[:, m:m + 1], bcol[:, m:m + 1], scol[:, :], ALU.mult).then_inc(s["rstd_done"], 1)
            nc.vector.tensor_tensor(qbias[0:XR, 2:3], big["xb"][0:XR, 0:1], scol[0:XR, :], ALU.mult)\
                .then_inc(s["rstd_done"], 1)
            dve.wait_ge(s["rstd_done"], 4)
            for i, par, g in groups(dve):
                dve.wait_ge(s["turned"], 2 * KD * i)
                for t in range(GT):
                    nc.vector.tensor_scalar(XN[par][:, t, :], X[:, bass.ds((g * GT + t) * D, D)],
                                            big["mv"][:, bass.ds(g * GT + t, 1), 0], big["rstd"][:, bass.ds(g * GT + t, 1)],
                                            ALU.subtract, ALU.mult).then_inc(s["xn_ready"], 1)

                def remainder(n, first):
                    rows = P if n < 4 else XR
                    k = par * NI + n
                    if n < NPQ:
                        dve.wait_ge(s["qk_read"], 2 * i * NPQ + par * NPQ + n + 1 + 2)
                    else:
                        dve.wait_ge(s["y_ready"], g + 1)
                    dve.wait_ge(s["p1_ready"], 2 * i * NI + k + 1)
                    dve.wait_ge(s["p2_ready"], 2 * i * NI + (par * NI if first or n == 1 else k - 1))
                    nc.vector.tensor_tensor(R[k % 2][0:rows, :], Y[k % 2][0:rows, :], PC[k % NPC][0:rows, 0, :],
                                            ALU.subtract).then_inc(s["r_ready"], 1)

                def last_piece(n):
                    rows = P if n < 4 else XR
                    k = par * NI + n
                    dve.wait_ge(s["p1_ready"], 2 * i * NI + k + 1 + 2)
                    dve.wait_ge(s["r_ready"], 2 * i * NI + k + 1)
                    nc.vector.tensor_tensor(PC[k % NPC][0:rows, 2, :], R[k % 2][0:rows, :], PC[k % NPC][0:rows, 1, :],
                                            ALU.subtract).then_inc(s["p2_ready"], 1)

                for n in range(NI):
                    if n == 5:
                        dve.wait_ge(s["ex_ready"], 2 * (g + 1))
                        dve.wait_ge(s["vv_ready"], 2 * (g + 1))
                        for dst, row in ((prodA, 0), (prodB, 64)):
                            nc.vector.scalar_tensor_tensor(
                                dst[:, :], PE_[0][row:row + XR, :], big["xb"][row:row + XR, 1:2],
                                V1V2[row:row + XR, :], ALU.add, ALU.mult).then_inc(s["prod_link"], 1)
                        dve.wait_ge(s["prod_link"], 2 * (g + 1))
                        nc.vector.tensor_tensor(Y[(par * NI + n) % 2][0:XR, :], prodA[:, :], prodB[:, :],
                                                ALU.subtract).then_inc(s["cross_ready"], 1)
                    remainder(n, n == 0)
                    if n >= 1:
                        last_piece(n - 1)
                last_piece(NI - 1)
                for pair in range(2):
                    dve.wait_ge(s["v_ready"], 2 * g + pair + 1 + 2)
                    nc.vector.tensor_tensor(
                        V[:, bass.ds((g * GT + 2 * pair) * D, 2 * D)].rearrange("p (t d) -> p t d", d=D),
                        PV[pair][:, :].rearrange("p (t d) -> p t d", d=D),
                        vb[:, :].unsqueeze(1).to_broadcast([P, 2, D]), ALU.add).then_inc(s["v_read"], 1)

        @block.scalar
        def _(act):
            act.wait_ge(s["ln_link"], 2)
            nc.scalar.activation(big["std"][:, :], big["mv"][:, :, 1], ACT.Sqrt, bias=big["eps"][:, :])\
                .then_inc(s["root_done"], 1)
            act.sem_inc(s["qk_read"], 2)
            act.sem_inc(s["p1_ready"], 2)
            act.wait_ge(s["rstd_done"], 4)
            for i, par, g in groups(act):
                act.wait_ge(s["v_ready"], 2 * (g - 1) + 2)
                for kk in range(KD):
                    act.wait_ge(s["turned"], KD * g + kk + 1)
                    nc.scalar.copy(xT[par][:, kk, :], TP[kk][:, :]).then_inc(s["xT_ready"], 1)

                def middle(n):
                    rows = P if n < 4 else XR
                    k = par * NI + n
                    act.wait_ge(s["r_ready"], 2 * i * NI + k + 1)
                    nc.scalar.copy(PC[k % NPC][0:rows, 1, :], R[k % 2][0:rows, :]).then_inc(s["p1_ready"], 1)

                for n in range(NI):
                    k = par * NI + n
                    y, rows = Y[k % 2], (P if n < 4 else XR)
                    pieces_free(act, i, k)
                    if extra and n == 5:
                        act.wait_ge(s["ex_ready"], 2 * (g + 1))
                        act.wait_ge(s["cross_ready"], g)
                        for row in (0, 64):
                            nc.scalar.activation(V1V2[row:row + XR, :], PE_[1][row:row + XR, :], ACT.Identity,
                                                 bias=big["xb"][row:row + XR, 2:3]).then_inc(s["vv_ready"], 1)
                        middle(n - 1)
                        act.wait_ge(s["cross_ready"], g + 1)
                        nc.scalar.copy(PC[k % NPC][0:rows, 0, :], y[0:rows, :]).then_inc(s["y_ready"], 1)
                        continue
                    q = par * NPQ + n
                    act.wait_ge(s["qk_ready"], 2 * i * NPQ + q + 1)
                    if k >= 2:
                        act.wait_ge(s["r_ready"], 2 * i * NI + k - 1)
                    else:
                        act.wait_ge(s["r_ready"], 2 * i * NI)
                    for dst in (y[0:rows, :], PC[k % NPC][0:rows, 0, :]):
                        if n < 2:
                            last = nc.scalar.activation(dst, PQ[q % 2][:, :], ACT.Identity, bias=qbias[:, n:n + 1],
                                                        scale=scol[:, :])
                        elif n < 4:
                            last = nc.scalar.activation(dst, PQ[q % 2][:, :], ACT.Identity, bias=bcol[:, n:n + 1])
                        else:
                            last = nc.scalar.activation(dst, PQ[q % 2][0:XR, :], ACT.Identity,
                                                        bias=qbias[0:XR, 2:3], scale=scol[0:XR, :])
                    last.then_inc(s["qk_read"], 1)
                    if n >= 1:
                        middle(n - 1)
                middle(NI - 1)

        @block.tensor
        def _(pe):
            pe.sem_inc(s["v_ready"], 2)
            for i, par, g in groups(pe):
                pe.wait_ge(s["xT_ready"], KD * g)
                for kk in range(KD):
                    for t in range(GT):
                        if kk == 0:
                            pe.wait_ge(s["xn_ready"], GT * g + t + 1)
                        last = nc.tensor.transpose(TP[kk][:, t * P:(t + 1) * P],
                                                   XN[par][:, t, kk * P:(kk + 1) * P], big["identF"][:, :])
                    last.then_inc(s["turned"], 1)
                pe.wait_ge(s["xT_ready"], KD * (g + 1))
                for n in range(NPQ):
                    q = par * NPQ + n
                    pe.wait_ge(s["qk_read"], 2 * i * NPQ + q + 1)
                    for kk in range(KD):
                        if n < 4:
                            last = nc.tensor.matmul(PQ[q % 2][:, :], big["WT"][:, kk, w0 + n * P:w0 + (n + 1) * P],
                                                    xT[par][:, kk, :], start=kk == 0, stop=kk == KD - 1)
                        else:
                            last = nc.tensor.matmul(PQ[q % 2][0:XR, :], big["XW"][:, kk, 0, :], xT[par][:, kk, :],
                                                    start=kk == 0, stop=kk == KD - 1)
                    last.then_inc(s["qk_ready"], 1)
                if extra:
                    pe.wait_ge(s["cross_ready"], g)
                    for b, sets in ((0, (1, 2)), (1, (3, 4))):
                        for kk in range(KD):
                            for row, j in zip((0, 64), sets):
                                last = nc.tensor.matmul(PE_[b][row:row + XR, :], big["XW"][:, kk, j, :],
                                                        xT[par][:, kk, :], start=kk == 0, stop=kk == KD - 1)
                        last.then_inc(s["ex_ready"], 1)
                for pair in range(2):
                    pe.wait_ge(s["v_read"], 2 * g)
                    for t in (2 * pair, 2 * pair + 1):
                        for kk in range(KD):
                            last = nc.tensor.matmul(PV[pair][:, (t % 2) * D:(t % 2 + 1) * D],
                                                    xT[par][:, kk, t * P:(t + 1) * P],
                                                    big["WT"][:, kk, w0 + 2 * D:w0 + 3 * D],
                                                    start=kk == 0, stop=kk == KD - 1)
                    last.then_inc(s["v_ready"], 1)

        @block.sync
        def _(sp):
            for i, par, g in groups(sp):
                b, t0 = g // (NG // B), (g % (NG // B)) * G
                for n in range(NI):
                    k = par * NI + n
                    sp.wait_ge(s["p2_ready"], 2 * i * NI + k + 1)
                    if n < 4:
                        dst = scratch["q" if n < 2 else "k"][bass.ds(b, 1), :, (n % 2) * P:(n % 2 + 1) * P, bass.ds(t0, G)]
                        rows = P
                    else:
                        dst = scratch["qx" if n == 4 else "kx"][bass.ds(b, 1), :, :, bass.ds(t0, G)]
                        rows = XR
                    sp.dma_start(dst.rearrange("b k r t -> r (b k) t"), PC[k % NPC][0:rows, :, :]).then_inc(stored[k % NPC], 16)
            for n in range(NPC):
                sp.wait_ge(stored[n], 16 * NI * NG // NPC)


def plan_units(causal):
    HALF = S // 2
    order = [1, 0]
    steps = []
    for hf in order:
        for kt in range(KT):
            lo = max(0, kt * P - hf * HALF) if causal else 0
            if lo < HALF:
                steps.append((hf, kt, lo))
    chunks = []
    for hf in order:
        for qt in range(8 * hf, 8 * hf + 8):
            keys = (qt + 1) * P if causal else S
            for c in range((keys + G - 1) // G):
                chunks.append((hf, qt, c, min(G, keys - c * G)))
    shift = 4 if causal else 6
    n = len(steps)
    weight = [(HALF - lo) // P + 2 for _, _, lo in steps]
    cyc = [(shift + j) % n for j in range(n)]
    total = sum(weight)
    total_c = sum(w + P for *_, w in chunks)
    at = [[] for _ in range(n)]
    acc = 0
    j = 0
    donew = 0
    for pos, stp in enumerate(cyc):
        acc += weight[stp]
        while j < len(chunks) and (donew + chunks[j][3] / 2) / total_c <= acc / total or (pos == n - 1 and j < len(chunks)):
            at[pos].append(j)
            donew += chunks[j][3] + P
            j += 1
    return order, steps, chunks, shift, cyc, at


def units(nc, tag, causal, big, scratch, V, sb, pb, sem):
    extra = not causal
    NR = 6 * HD + (6 * C3 if extra else 0)
    NM = 2
    HALF = S // 2
    order, steps, chunks, shift, cyc, at = plan_units(causal)
    NS, NC, NP = len(steps), len(chunks), 4
    assert NS % NP == 0 and NC % 2 == 0
    H1 = sum(1 for x in steps if x[0] == order[0])
    per_half = {hf: sum(1 for c in chunks if c[0] == hf) for hf in order}
    z1 = next(p for p in range(NS) if at[p] and at[p][-1] >= per_half[order[0]] - 1)
    O_PREV, O_THIS = 3, H1 + 3
    M_SECOND = shift + 1
    M_FIRST = shift + z1 + 2
    assert M_FIRST < NS and len({O_PREV, O_THIS, M_SECOND, M_FIRST}) == 4 and M_SECOND < H1
    with ExitStack() as st:
        QS = [sb(f"QS{tag}{i}", [P, S], BF16, st) for i in range(2)]
        KS = [sb(f"KS{tag}{i}", [P, S], BF16, st) for i in range(2)]
        Vh = [sb(f"Vh{tag}{i}", [P, KT, 32], F32, st) for i in range(2)]
        PR = [sb(f"PR{tag}{i}", [P, HALF], F32, st) for i in range(NP)]
        Osb = sb(f"Osb{tag}", [P, D], F32, st)
        mx = [sb(f"mx{tag}{i}", [P, KT, 4], F32, st) for i in range(2)]
        nm = sb(f"nm{tag}", [P, 8], F32, st)
        nm0 = sb(f"nm0{tag}", [P, 8], BF16, st)
        nmp = [sb(f"nmp{tag}{i}", [P, 2, 8], F32, st) for i in range(2)]
        nmT = [sb(f"nmT{tag}{i}", [16, P], BF16, st) for i in range(2)]
        rec = sb(f"rec{tag}", [P, 2, 4], F32, st)
        ones = sb(f"ones{tag}", [NM, S], BF16, st)
        SP_ = [pb(f"S{tag}{i}", [P, HALF], st) for i in range(2)]
        MP = [pb(f"M{tag}{i}", [P, G], st) for i in range(2)]
        OP = pb(f"O{tag}", [P, G], st)
        TB = pb(f"T{tag}", [P, G], st)
        s = {n: sem(f"{n}{tag}") for n in (
            "ones_made", "ones_in", "vh_preset", "mx_preset", "vh_ready", "scores_ready", "exp_done", "max_ready", "max_read", "pv_done",
            "o_copied", "o_turned", "nm_link", "nm_made", "nm_turned", "nmT_made", "ao_link", "bias_added")}
        loaded = [sem(f"qk_loaded{tag}{i}") for i in range(2)]
        nm_in = [sem(f"nm_in{tag}{i}") for i in range(2)]
        nload = 6 + (6 if extra else 0)
        block = st.enter_context(nc.Block())

        def unit_loop(eng, emit):
            emit(0, 0, False, True)
            with eng.Fori(0, (U - 2) // 2) as i:
                emit(2 * i + 1, 1, True, True)
                emit(2 * i + 2, 0, True, True)
            emit(U - 1, 1, True, False)

        def max_part(u, st_, nxt):
            pos = (st_ - shift) % NS
            if st_ < shift:
                return [(u, j, True) for j in at[pos]]
            return [(u + 1, j, False) for j in at[pos]] if nxt else []

        @block.gpsimd
        def _(pool):
            for i in range(2):
                pool.memset(Vh[i][:, :, HD:], 0.0).then_inc(s["vh_preset"], 1)
            pool.memset(ones[:, :], 1.0).then_inc(s["ones_made"], 1)
            pool.wait_ge(s["vh_preset"], 2)
            for i in range(2):
                pool.memset(Vh[i][:, :, HD:HD + 1], 1.0).then_inc(s["vh_preset"], 1)
            pool.wait_ge(s["vh_preset"], 4)

            def copy_values(u, par, _prev, _nxt):
                if not (isinstance(u, int) and u < 2):
                    pool.wait_ge(s["pv_done"], (u - 1) * NS + NP)
                b, h = u // H, u % H
                src = V[:, :].rearrange("p (b k c) -> p b k c", b=B, k=KT)
                nc.gpsimd.tensor_copy(Vh[par][:, :, 0:HD], src[:, bass.ds(b, 1), :, bass.ds(h * HD, HD)]
                                      .rearrange("p b k c -> p (b k) c")).then_inc(s["vh_ready"], 1)

            unit_loop(pool, copy_values)
            ob = big["obA"] if causal else big["obB"]
            with pool.Fori(0, NT) as t:
                nc.gpsimd.tensor_tensor(big["X"][:, bass.ds(t * D, D)], big["X"][:, bass.ds(t * D, D)], ob[:, :],
                                        ALU.add).then_inc(s["bias_added"], 1)

        def load_unit(sp, u, par):
            b, h = u // H, u % H
            for side, buf, runs in (("q", QS, Q_RUNS), ("k", KS, K_RUNS)):
                for scr, width, row in [(scratch[side], HD, 0)] + ([(scratch[side + "x"], C3, 6 * HD)] if extra else []):
                    for first, pieces, copies in runs:
                        n = pieces * copies * width
                        src = scr[bass.ds(b, 1), first:first + pieces, bass.ds(h * width, width), :]\
                            .rearrange("b k r t -> (b k) r t")
                        if copies > 1:
                            src = src.to_broadcast([copies, width, S])
                        sp.dma_start(buf[par][row:row + n, :], src).then_inc(loaded[par], 16)
                        row += n

        def put_max(sp, k, pos, par):
            hf = order[pos]
            sp.wait_ge(s["nmT_made"], k)
            for piece in range(NM):
                dst = QS[par][NR + piece:NR + piece + 1, hf * HALF:(hf + 1) * HALF].rearrange("r (q c) -> r q c", c=P)
                sp.dma_start(dst, nmT[pos][piece * 8:piece * 8 + 8, :]).then_inc(nm_in[pos], 16)

        @block.sync
        def _(sp):
            sp.wait_ge(s["ones_made"], 1)
            for i in range(2):
                sp.dma_start(KS[i][NR:NR + NM, :], ones[:, :]).then_inc(s["ones_in"], 16)
            load_unit(sp, 0, 0)
            put_max(sp, 1, 0, 0)

            def emit(u, par, _prev, nxt):
                if nxt:
                    sp.wait_ge(s["scores_ready"], u * NS)
                    load_unit(sp, u + 1, 1 - par)
                put_max(sp, 2 * u + 2, 1, par)
                if nxt:
                    put_max(sp, 2 * u + 3, 0, 1 - par)

            unit_loop(sp, emit)

        @block.tensor
        def _(pe):
            pe.sem_inc(s["pv_done"], NP)

            def maxima(u, par, j):
                hf, qt, c, w = chunks[j]
                if j == 0:
                    pe.wait_ge(loaded[par], (u // 2 + 1) * 16 * nload)
                pe.wait_ge(s["max_read"], u * NC + j + 1)
                diag = causal and c == qt // 4
                last = nc.tensor.matmul(MP[j % 2][:, 0:w], QS[par][0:NR, qt * P:(qt + 1) * P],
                                        KS[par][0:NR, c * G:c * G + w], start=True, stop=not diag)
                if diag:
                    last = nc.tensor.matmul(MP[j % 2][:, w - P:w], big["identB"][:, :], big["maskQ"][:, :],
                                            start=False, stop=True)
                last.then_inc(s["max_ready"], 1)

            def scores(u, par, x):
                hf, kt, lo = steps[x]
                pe.wait_ge(s["exp_done"], u * NS + x + 1)
                if x == 0:
                    pe.wait_ge(nm_in[0], (u + 1) * 16 * NM)
                if x == H1:
                    pe.wait_ge(nm_in[1], (u + 1) * 16 * NM)
                q0 = hf * HALF
                diag = causal and kt * P >= q0
                for c in range(2):
                    a, z = max(lo, c * G), (c + 1) * G
                    if a >= z:
                        continue
                    here = diag and a == lo
                    last = nc.tensor.matmul(SP_[x % 2][:, a:z], KS[par][0:NR + NM, kt * P:(kt + 1) * P],
                                            QS[par][0:NR + NM, q0 + a:q0 + z], start=True, stop=not here)
                    if here:
                        last = nc.tensor.matmul(SP_[x % 2][:, lo:lo + P], big["identB"][:, :], big["maskK"][:, :],
                                                start=False, stop=True)
                last.then_inc(s["scores_ready"], 1)

            def values(u, par, x):
                hf, kt, lo = steps[x]
                pe.wait_ge(s["exp_done"], u * NS + x + 1 + 2)
                if x == 0:
                    pe.wait_ge(s["vh_ready"], u + 1)
                if x == 0 or x == H1:
                    pe.wait_ge(s["o_copied"], 2 * u + (x == H1))
                last_kt = {j: (min(KT, (hf * HALF + (j + 1) * 256) // P) - 1 if causal else KT - 1) for j in range(4)}
                for j in range(4):
                    a, z = max(lo, 256 * j), 256 * (j + 1)
                    if a >= z:
                        continue
                    last = nc.tensor.matmul(OP[32 * j:32 * j + 32, a - 256 * j:256], Vh[par][:, kt, :],
                                            PR[x % NP][:, a:z], start=kt == 0, stop=kt == last_kt[j])
                last.then_inc(s["pv_done"], 1)

            def turn_output(k, maxima_before):
                pe.wait_ge(s["o_copied"], k + 1)
                pe.wait_ge(s["ao_link"], 2 * k)
                pe.wait_ge(s["nmT_made"], maxima_before)
                for c in range(2):
                    last = nc.tensor.transpose(TB[:, c * P:(c + 1) * P], Osb[:, c * P:(c + 1) * P], big["identF"][:, :])
                last.then_inc(s["o_turned"], 1)

            def turn_max(k, pos, outputs_before):
                pe.wait_ge(s["nm_made"], k + 1)
                pe.wait_ge(s["nmT_made"], k)
                pe.wait_ge(s["ao_link"], 2 * outputs_before)
                nc.tensor.transpose(TB[0:16, 2 * P:3 * P], nmp[pos][:, :, :].rearrange("p a q -> p (a q)"),
                                    big["identF"][:, :]).then_inc(s["nm_turned"], 1)

            for x in range(shift, NS):
                for _, j, _ in max_part(-1, x, True):
                    maxima(0, 0, j)
            turn_max(0, 0, 0)
            pe.wait_ge(s["ones_in"], 32)

            def emit(u, par, prev, nxt):
                for x in range(NS):
                    scores(u, par, x)
                    for w, j, own in max_part(u, x, nxt):
                        maxima(w, par if own else 1 - par, j)
                    if x > 0:
                        values(u, par, x - 1)
                    elif prev:
                        values(u - 1, 1 - par, NS - 1)
                    if x == O_PREV and prev:
                        turn_output(2 * u - 1, 2 * u + 1 + (M_SECOND < O_PREV))
                    if x == M_SECOND:
                        turn_max(2 * u + 1, 1, 2 * u - (0 if O_PREV < M_SECOND or not prev else 1))
                    if x == O_THIS:
                        turn_output(2 * u, 2 * u + 2 + (M_FIRST < O_THIS and nxt))
                    if x == M_FIRST and nxt:
                        turn_max(2 * u + 2, 0, 2 * u + (O_THIS < M_FIRST))

            unit_loop(pe, emit)
            values(U - 1, 1, NS - 1)
            turn_output(2 * U - 1, 2 * U)

        @block.scalar
        def _(act):
            act.sem_inc(s["exp_done"], 2)

            def copy_output(k):
                act.wait_ge(s["o_turned"], k)
                nc.scalar.copy(Osb[:, :], OP[:, 0:D]).then_inc(s["o_copied"], 1)

            def emit(u, par, prev, nxt):
                for x in range(NS):
                    hf, kt, lo = steps[x]
                    act.wait_ge(s["scores_ready"], u * NS + x + 1)
                    act.wait_ge(s["pv_done"], u * NS + x + 1)
                    nc.scalar.activation(PR[x % NP][:, lo:], SP_[x % 2][:, lo:], ACT.Exp).then_inc(s["exp_done"], 1)
                    if x == 1 and prev:
                        act.wait_ge(s["pv_done"], u * NS + NP)
                        copy_output(2 * u - 1)
                    if x == H1 + 1:
                        act.wait_ge(s["pv_done"], u * NS + H1 + NP)
                        copy_output(2 * u)

            unit_loop(act, emit)
            act.wait_ge(s["pv_done"], U * NS + NP)
            copy_output(2 * U - 1)

        @block.vector
        def _(dve):
            dve.sem_inc(s["max_read"], 2)
            if causal:
                for i in range(2):
                    nc.vector.memset(mx[i][:, :, :], LOWEST).then_inc(s["mx_preset"], 1)
                dve.wait_ge(s["mx_preset"], 2)

            def reduce_chunk(u, par, j):
                hf, qt, c, w = chunks[j]
                dve.wait_ge(s["max_ready"], u * NC + j + 1)
                nc.vector.tensor_reduce(mx[par][:, qt, c:c + 1], MP[j % 2][:, 0:w], AX.X, ALU.max)\
                    .then_inc(s["max_read"], 1)

            def make_max(u, par, pos, k):
                hf = order[pos]
                done = u * NC + (per_half[order[0]] if pos == 0 else NC)
                dve.wait_ge(s["max_read"], done + 2)
                dve.wait_ge(s["nm_made"], k)
                link = chain(dve, s["nm_link"], 3 * k)
                link(nc.vector.tensor_reduce(nm[:, :], mx[par][:, 8 * hf:8 * hf + 8, :], AX.X, ALU.max, negate=True))
                link(nc.vector.tensor_copy(nm0[:, :], nm[:, :]))
                link(nc.vector.tensor_copy(nmp[pos][:, 0, :], nm0[:, :]))
                nc.vector.tensor_tensor(nmp[pos][:, 1, :], nm[:, :], nm0[:, :], ALU.subtract).then_inc(s["nm_made"], 1)

            def take_max(k, pos, first):
                dve.wait_ge(s["nm_turned"], k + 1)
                if not first:
                    dve.wait_ge(nm_in[pos], (k // 2) * 16 * NM)
                nc.vector.tensor_copy(nmT[pos][:, :], TB[0:16, 2 * P:3 * P]).then_inc(s["nmT_made"], 1)

            def take_output(u, pos, k):
                hf = order[pos]
                dve.wait_ge(s["o_turned"], k + 1)
                tv = TB[:, 0:D].rearrange("p (c j r) -> p c j r", c=2, j=4)
                dve.wait_ge(s["ao_link"], 2 * k)
                link = chain(dve, s["ao_link"], 2 * k)
                link(nc.vector.reciprocal(rec[:, :, :], tv[:, :, :, HD]))
                b, h = u // H, u % H
                dst = V[:, :].rearrange("p (b k c) -> p b k c", b=B, k=KT)[
                    :, bass.ds(b, 1), 8 * hf:8 * hf + 8, bass.ds(h * HD, HD)].rearrange("p b (j c) d -> p c (b j) d", j=4)
                nc.vector.tensor_tensor(dst, tv[:, :, :, 0:HD], rec[:, :, :].unsqueeze(3).to_broadcast([P, 2, 4, HD]),
                                        ALU.mult).then_inc(s["ao_link"], 1)

            for x in range(shift, NS):
                for _, j, _ in max_part(-1, x, True):
                    reduce_chunk(0, 0, j)
            make_max(0, 0, 0, 0)
            take_max(0, 0, True)

            def emit(u, par, prev, nxt):
                for x in range(NS):
                    for w, j, own in max_part(u, x, nxt):
                        reduce_chunk(w, par if own else 1 - par, j)
                    if x == shift - 1:
                        make_max(u, par, 1, 2 * u + 1)
                    if x == M_SECOND:
                        take_max(2 * u + 1, 1, False)
                    if x == shift + z1 and nxt:
                        make_max(u + 1, 1 - par, 0, 2 * u + 2)
                    if x == M_FIRST and nxt:
                        take_max(2 * u + 2, 0, False)
                    if x == O_PREV and prev:
                        take_output(u - 1, 1, 2 * u - 1)
                    if x == O_THIS:
                        take_output(u, 0, 2 * u)

            unit_loop(dve, emit)
            take_output(U - 1, 1, 2 * U - 1)


def combine(nc, tag, big, AO, sb, pb, sem):
    causal = tag == "A"
    w0 = 3 * D if causal else 7 * D
    X = big["X"]
    with ExitStack() as st:
        aT = [sb(f"aT{tag}{i}", [P, KD, G], F32, st) for i in range(2)]
        stage = [sb(f"stage{tag}{i}", [P, GT, D], F32, st) for i in range(2)]
        TP = [pb(f"cT{tag}{i}", [P, G], st) for i in range(4)]
        PO = [pb(f"cO{tag}{i}", [P, G], st) for i in range(4)]
        staged, turned, aT_ready, out_ready, out_read = (sem(f"{n}{tag}") for n in (
            "c_staged", "c_turned", "c_aT_ready", "c_out_ready", "c_out_read"))
        block = st.enter_context(nc.Block())
        def groups(eng):
            with eng.Fori(0, NG // 2) as i:
                for par in range(2):
                    yield i, par, 2 * i + par

        @block.gpsimd
        def _(pool):
            for i, par, g in groups(pool):
                pool.wait_ge(turned, 2 * KD * i)
                nc.gpsimd.tensor_copy(stage[par][:, :, :].rearrange("p t d -> p (t d)"),
                                      AO[:, bass.ds(g * GT * D, GT * D)]).then_inc(staged, 1)

        @block.tensor
        def _(pe):
            for i, par, g in groups(pe):
                pe.wait_ge(staged, g + 1)
                pe.wait_ge(aT_ready, 2 * KD * i)
                for kk in range(KD):
                    for t in range(GT):
                        last = nc.tensor.transpose(TP[2 * par + kk][:, t * P:(t + 1) * P],
                                                   stage[par][:, t, kk * P:(kk + 1) * P], big["identF"][:, :])
                    last.then_inc(turned, 1)
                pe.wait_ge(aT_ready, KD * (g + 1))
                pe.wait_ge(out_read, 4 * i)
                for pair in range(2):
                    for t in (2 * pair, 2 * pair + 1):
                        for kk in range(KD):
                            last = nc.tensor.matmul(PO[2 * par + pair][:, (t % 2) * D:(t % 2 + 1) * D],
                                                    aT[par][:, kk, t * P:(t + 1) * P], big["WT"][:, kk, w0:w0 + D],
                                                    start=kk == 0, stop=kk == KD - 1)
                    last.then_inc(out_ready, 1)

        @block.scalar
        def _(act):
            for i, par, g in groups(act):
                act.wait_ge(out_ready, 4 * i)
                for kk in range(KD):
                    act.wait_ge(turned, KD * g + kk + 1)
                    nc.scalar.copy(aT[par][:, kk, :], TP[2 * par + kk][:, :]).then_inc(aT_ready, 1)

        @block.vector
        def _(dve):
            for i, par, g in groups(dve):
                for pair in range(2):
                    dve.wait_ge(out_ready, 2 * g + pair + 1)
                    xs = X[:, bass.ds((g * GT + 2 * pair) * D, 2 * D)]
                    nc.vector.tensor_tensor(xs, PO[2 * par + pair][:, :], xs, ALU.add).then_inc(out_read, 1)


def experts(nc, tag, big, sb, pb, sem, ffn_loaded):
    X = big["X"]
    with ExitStack() as st:
        stats = sb(f"fstats{tag}", [P, NT, 6], F32, st)
        XN = sb(f"fXN{tag}", [P, GT, D], F32, st)
        xT = sb(f"fxT{tag}", [P, KD, G], F32, st)
        hT = [sb(f"fhT{tag}{i}", [P, HT, G], F32, st) for i in range(2)]
        lg = sb(f"flg{tag}", [P, GT, NE], F32, st)
        m1 = sb(f"fm1{tag}", [P, GT], F32, st)
        pr = sb(f"fpr{tag}", [P, GT, NE], F32, st)
        beats = sb(f"fbeats{tag}", [P, GT, NE, NE], F32, st)
        rank = sb(f"frank{tag}", [P, GT, NE], F32, st)
        wt = sb(f"fwt{tag}", [P, GT, EX], F32, st)
        wT = sb(f"fwT{tag}", [EX, G], F32, st)
        TP = [pb(f"fTP{tag}{i}", [P, G], st) for i in range(2)]
        HP = [pb(f"fHP{tag}{i}", [P, G], st) for i in range(2)]
        YP = [pb(f"fYP{tag}{i}", [P, G], st) for i in range(2)]
        LP = pb(f"fLP{tag}", [P, G], st)
        s = {n: sem(f"f_{n}{tag}") for n in (
            "ln_link", "root_done", "rstd_done", "xn_ready", "turned", "xT_ready", "lg_ready", "r_link", "ls_ready",
            "e_done", "wt_ready", "wT_turned", "wT_ready", "h_ready", "h_done", "y_ready", "y_read", "preset")}
        NL = 20
        order = [SH] + list(range(NE))
        block = st.enter_context(nc.Block())

        @block.vector
        def _(dve):
            link = chain(dve, s["ln_link"])
            norm_stats(nc, dve, link, big, stats)
            dve.sem_inc(s["y_read"], 2)
            nc.vector.memset(beats[:, :, :, :], 0.0).then_inc(s["preset"], 1)
            nc.vector.memset(wt[:, :, SH:], 1.0).then_inc(s["preset"], 1)
            dve.wait_ge(s["preset"], 2)
            dve.wait_ge(s["root_done"], 1)
            nc.vector.reciprocal(big["rstd"][:, :], big["std"][:, :]).then_inc(s["rstd_done"], 1)
            dve.wait_ge(s["rstd_done"], 1)
            with dve.Fori(0, NG) as g:
                dve.wait_ge(s["turned"], KD * g)
                for t in range(GT):
                    nc.vector.tensor_scalar(XN[:, t, :], X[:, bass.ds((g * GT + t) * D, D)],
                                            big["mv"][:, bass.ds(g * GT + t, 1), 0], big["rstd"][:, bass.ds(g * GT + t, 1)],
                                            ALU.subtract, ALU.mult).then_inc(s["xn_ready"], 1)
                dve.wait_ge(s["lg_ready"], g + 1)
                link = chain(dve, s["r_link"], NL * g)
                link(nc.vector.tensor_tensor(lg[:, :, :], LP[:, 0:GT * NE].rearrange("p (t e) -> p t e", e=NE),
                                             big["rb"][:, :].unsqueeze(1).to_broadcast([P, GT, NE]), ALU.add))
                link(nc.vector.tensor_reduce(m1[:, :], lg[:, :, :], AX.X, ALU.max))
                nc.vector.tensor_tensor(lg[:, :, :], lg[:, :, :], m1[:, :].unsqueeze(2).to_broadcast([P, GT, NE]),
                                        ALU.subtract).then_inc(s["ls_ready"], 1)
                dve.wait_ge(s["e_done"], g + 1)
                link(nc.vector.tensor_reduce(m1[:, :], pr[:, :, :], AX.X, ALU.add))
                link(nc.vector.reciprocal(m1[:, :], m1[:, :]))
                link(nc.vector.tensor_tensor(pr[:, :, :], pr[:, :, :], m1[:, :].unsqueeze(2).to_broadcast([P, GT, NE]),
                                             ALU.mult))
                for j in range(NE):
                    if j + 1 < NE:
                        link(nc.vector.tensor_tensor(beats[:, :, j, j + 1:], pr[:, :, j:j + 1].to_broadcast([P, GT, NE - 1 - j]),
                                                     pr[:, :, j + 1:], ALU.is_ge))
                    if j > 0:
                        link(nc.vector.tensor_tensor(beats[:, :, j, 0:j], pr[:, :, j:j + 1].to_broadcast([P, GT, j]),
                                                     pr[:, :, 0:j], ALU.is_gt))
                link(nc.vector.tensor_reduce(rank[:, :, :], beats[:, :, :, :].rearrange("p t j e -> p t e j"), AX.X, ALU.add))
                assert link.count[0] == NL, link.count
                nc.vector.scalar_tensor_tensor(wt[:, :, 0:NE], rank[:, :, :], 2.0, pr[:, :, :], ALU.is_lt, ALU.mult)\
                    .then_inc(s["wt_ready"], 1)
                dve.wait_ge(s["wT_turned"], g + 1)
                nc.vector.tensor_copy(wT[:, :], TP[0][0:EX, :]).then_inc(s["wT_ready"], 1)
                for n, e in enumerate(order):
                    for t in range(GT):
                        k = n * GT + t
                        dve.wait_ge(s["y_ready"], g * EX * GT + k + 1)
                        if n:
                            dve.wait_ge(s["y_read"], g * EX * GT + k - GT + 1 + 2)
                        else:
                            dve.wait_ge(s["wt_ready"], g + 1)
                        xs = X[:, bass.ds((g * GT + t) * D, D)]
                        if e == SH:
                            nc.vector.tensor_tensor(xs, YP[k % 2][:, 0:D], xs, ALU.add).then_inc(s["y_read"], 1)
                        else:
                            nc.vector.scalar_tensor_tensor(xs, YP[k % 2][:, 0:D], wt[:, t, e:e + 1], xs, ALU.mult,
                                                           ALU.add).then_inc(s["y_read"], 1)

        @block.scalar
        def _(act):
            act.wait_ge(s["ln_link"], 2)
            nc.scalar.activation(big["std"][:, :], big["mv"][:, :, 1], ACT.Sqrt, bias=big["eps"][:, :])\
                .then_inc(s["root_done"], 1)
            act.sem_inc(s["h_done"], 2)
            with act.Fori(0, NG) as g:
                act.wait_ge(s["y_ready"], g * EX * GT)
                for kk in range(KD):
                    act.wait_ge(s["turned"], KD * g + kk + 1)
                    nc.scalar.copy(xT[:, kk, :], TP[kk][:, :]).then_inc(s["xT_ready"], 1)
                act.wait_ge(s["ls_ready"], g + 1)
                nc.scalar.activation(pr[:, :, :], lg[:, :, :], ACT.Exp).then_inc(s["e_done"], 1)
                for n, e in enumerate(order):
                    for m in range(HT):
                        k = n * HT + m
                        act.wait_ge(s["h_ready"], g * EX * HT + k + 1)
                        if m == 0 and n >= 2:
                            act.wait_ge(s["y_ready"], (g * EX + n - 1) * GT)
                        nc.scalar.activation(hT[n % 2][:, m, :], HP[k % 2][:, :], ACT.Gelu,
                                             bias=big["b1"][:, e, m:m + 1]).then_inc(s["h_done"], 1)

        @block.tensor
        def _(pe):
            pe.wait_ge(ffn_loaded, 16 * 2 * EX)

            def up(g, n):
                e = order[n]
                for m in range(HT):
                    k = n * HT + m
                    pe.wait_ge(s["h_done"], g * EX * HT + k + 1)
                    for kk in range(KD):
                        last = nc.tensor.matmul(HP[k % 2][:, :], big["w1"][:, e, kk, m * P:(m + 1) * P], xT[:, kk, :],
                                                start=kk == 0, stop=kk == KD - 1)
                    last.then_inc(s["h_ready"], 1)

            def down(g, n):
                e = order[n]
                pe.wait_ge(s["h_done"], g * EX * HT + (n + 1) * HT + 2)
                for t in range(GT):
                    k = n * GT + t
                    pe.wait_ge(s["y_read"], g * EX * GT + k + 1)
                    if n == 0:
                        nc.tensor.matmul(YP[k % 2][:, 0:D], wT[:, t * P:(t + 1) * P], big["b2"][:, :],
                                         start=True, stop=False)
                    for m in range(HT):
                        last = nc.tensor.matmul(YP[k % 2][:, 0:D], hT[n % 2][:, m, t * P:(t + 1) * P],
                                                big["w2"][:, e, m, :], start=n > 0 and m == 0, stop=m == HT - 1)
                    last.then_inc(s["y_ready"], 1)

            with pe.Fori(0, NG) as g:
                pe.wait_ge(s["wT_ready"], g)
                for kk in range(KD):
                    for t in range(GT):
                        if kk == 0:
                            pe.wait_ge(s["xn_ready"], GT * g + t + 1)
                        last = nc.tensor.transpose(TP[kk][:, t * P:(t + 1) * P], XN[:, t, kk * P:(kk + 1) * P],
                                                   big["identF"][:, :])
                    last.then_inc(s["turned"], 1)
                pe.wait_ge(s["xT_ready"], KD * (g + 1))
                for t in range(GT):
                    for kk in range(KD):
                        last = nc.tensor.matmul(LP[:, t * NE:(t + 1) * NE], xT[:, kk, t * P:(t + 1) * P],
                                                big["rw"][:, kk, :], start=kk == 0, stop=kk == KD - 1)
                last.then_inc(s["lg_ready"], 1)
                up(g, 0)
                pe.wait_ge(s["wt_ready"], g + 1)
                for t in range(GT):
                    last = nc.tensor.transpose(TP[0][0:EX, t * P:(t + 1) * P], wt[:, t, :], big["identF"][:, :])
                last.then_inc(s["wT_turned"], 1)
                pe.wait_ge(s["wT_ready"], g + 1)
                for n in range(EX):
                    if n + 1 < EX:
                        up(g, n + 1)
                    down(g, n)



def finish(nc, out, big, sem):
    written = sem("written")
    with nc.Block() as block:
        @block.sync
        def _(sp):
            view = out.rearrange("b (t p) d -> p (b t) d", p=P)
            X3 = big["X"][:, :].rearrange("p (t d) -> p t d", d=D)
            for g in range(NG):
                sp.dma_start(view[:, g * GT:(g + 1) * GT, :], X3[:, g * GT:(g + 1) * GT, :]).then_inc(written, 16)
            sp.wait_ge(written, 16 * NG)


NAMES = """L0_attn_a_hidden_states L0_attn_a_c_attn_kernel L0_attn_a_c_attn_bias L0_attn_a_c_proj_kernel
L0_attn_a_c_proj_bias L0_attn_b_Wq L0_attn_b_bq L0_attn_b_Wk L0_attn_b_bk L0_attn_b_Wv L0_attn_b_bv L0_attn_b_Wo
L0_attn_b_bo L0_attn_b_Wqs L0_attn_b_bqs L0_attn_b_Wks L0_attn_b_bks L0_attn_b_Wvs L0_attn_b_bvs L0_attn_b_temp
L0_ffn_router_w L0_ffn_router_b L0_ffn_sw1 L0_ffn_sb1 L0_ffn_sw2 L0_ffn_sb2 L0_ffn_rw1 L0_ffn_rb1 L0_ffn_rw2
L0_ffn_rb2""".split()


def kernel(**inputs):
    import numpy as np
    import concourse.bacc as bacc
    from concourse.bass_utils import run_bass_kernel_spmd

    nc = bacc.Bacc("TRN2", target_bir_lowering=False, num_devices=1)
    arrays, io = {}, {}
    for name in NAMES:
        a = np.ascontiguousarray(inputs[name])
        if a.ndim == 0:
            a = a.reshape(1)
        arrays[name] = a
        io[name] = nc.dram_tensor(name, a.shape, mybir.dt.from_np(a.dtype), kind="ExternalInput").ap()
    out = nc.dram_tensor("out", (B, S, D), F32, kind="ExternalOutput").ap()
    build(nc, io, out)
    r = run_bass_kernel_spmd(nc, [arrays], core_ids=[0])
    return r.results[0]["out"]
```

```python
from contextlib import ExitStack

import concourse.bass as bass
from concourse import mybir

F32 = mybir.dt.float32
BF16 = mybir.dt.bfloat16
ALU = mybir.AluOpType
ACT = mybir.ActivationFunctionType
AX = mybir.AxisListType

P = 128
B, S, D = 2, 2048, 256
T = B * S
NT = T // P
H, HD = 16, 16
U = B * H
KT = S // P
KD = D // P
G = 512
NG = T // G
GT = G // P
NE, HID = 8, 512
EX = NE + 1
SH = NE
HT = HID // P
TOP = 2
ST = TOP * NT + NE
SLOTS = ST * P
C3 = 3
XR = H * C3
EPS = 1e-5
NEG = -1e30
LOWEST = -3e38

Q_RUNS = [(0, 1, 3), (1, 1, 2), (2, 1, 1)]
K_RUNS = [(0, 3, 1), (0, 2, 1), (0, 1, 1)]


def build(nc, io, out):
    ctx = ExitStack()
    with ctx:
        def sb(name, shape, dt=F32, at=ctx):
            return at.enter_context(nc.sbuf_tensor(name, shape, dt))

        def pb(name, shape, at, dt=F32):
            return at.enter_context(nc.psum_tensor(name, shape, dt))

        phase_sems = []

        def sem(name, keep=False):
            handle = nc.alloc_semaphore(name)
            if not keep:
                phase_sems.append(handle)
            return handle

        def clear_sems():
            nc.clear_and_free_semaphores(phase_sems)
            nc.all_engine_barrier()
            phase_sems.clear()

        scratch = {}
        for side in "qk":
            scratch[side] = nc.dram_tensor(f"{side}_pieces", [B, 3, D, S], BF16, kind="Internal").ap()
            scratch[side + "x"] = nc.dram_tensor(f"{side}x_pieces", [B, 3, XR, S], BF16, kind="Internal").ap()

        turned_w = nc.dram_tensor("turned_w", [2, P, KD, 4 * D], F32, kind="Internal").ap()
        slots_in = nc.dram_tensor("slots_in", [SLOTS, D], F32, kind="Internal").ap()
        slots_out = nc.dram_tensor("slots_out", [SLOTS, D], F32, kind="Internal").ap()
        scratch.update(w=turned_w, slots_in=slots_in, slots_out=slots_out)

        big = dict(
            X=sb("X", [P, NT * D]),
            w1=sb("w1", [P, EX, KD, HID]),
            w2=sb("w2", [P, EX, HT, D]),
            b1=sb("b1", [P, EX, HT]),
            b2=sb("b2", [EX, D]),
            rw=sb("rw", [P, KD, NE]),
            rb=sb("rb", [P, NE]),
            bcolA=sb("bcolA", [P, 6]),
            bcolB=sb("bcolB", [P, 6]),
            scolA=sb("scolA", [P, 1]),
            scolB=sb("scolB", [P, 1]),
            vbA=sb("vbA", [P, D]), vbB=sb("vbB", [P, D]),
            obA=sb("obA", [P, D]), obB=sb("obB", [P, D]),
            XW=sb("XW", [P, KD, 5, XR]),
            xb=sb("xb", [P, 3]),
            identF=sb("identF", [P, P]),
            identB=sb("identB", [P, P], BF16),
            maskK=sb("maskK", [P, P], BF16),
            maskQ=sb("maskQ", [P, P], BF16),
            before=sb("before", [P, P], BF16),
            all1=sb("all1", [P, P], BF16),
            stats=sb("stats", [P, NT, 6]),
            mv=sb("mv", [P, NT, 2]), std=sb("std", [P, NT]), rstd=sb("rstd", [P, NT]),
            eps=sb("eps", [P, 1]),
        )
        ffn_loaded = sem("ffn_loaded", keep=True)
        slots_zeroed = sem("slots_zeroed", keep=True)
        setup(nc, io, big, scratch, sb, pb, sem, ffn_loaded, slots_zeroed)
        attention(nc, "A", True, big, scratch, sb, pb, sem)
        experts(nc, "A", big, scratch, sb, pb, sem, ffn_loaded, slots_zeroed)
        clear_sems()
        attention(nc, "B", False, big, scratch, sb, pb, sem)
        experts(nc, "B", big, scratch, sb, pb, sem, ffn_loaded, slots_zeroed)
        finish(nc, out, big, sem)


def chain(eng, sem, base=0):
    n = [0]

    def link(ins):
        n[0] += 1
        ins.then_inc(sem, 1)
        eng.wait_ge(sem, base + n[0])
    link.count = n
    return link


def setup(nc, io, big, scratch, sb, pb, sem, ffn_loaded, slots_zeroed):
    with ExitStack() as st:
        natural = sb("natural", [P, 16, D], F32, st)
        WT = sb("WT", [P, KD, 8 * D], F32, st)
        zeros = sb("zero_rows", [P, D], F32, st)
        wcol = sb("wcol", [P, 3, C3], F32, st)
        blockdiag = sb("blockdiag", [P, 5, 2, H, C3], F32, st)
        xb_in = sb("xb_in", [P, 3], F32, st)
        banks = [pb(f"setup_ps{i}", [P, 512], st) for i in range(8)]
        X = big["X"]
        x_loaded, w_loaded, small_loaded = sem("x_loaded"), sem("w_loaded"), sem("small_loaded")
        ident_made, masks_made, bd_link = sem("ident_made"), sem("masks_made"), sem("bd_link")
        turned, turned_out, comp_done, comp_out = sem("turned"), sem("turned_out"), sem("comp_done"), sem("comp_out")
        zeroed, kept, measured = sem("zeroed"), sem("kept"), sem("measured")
        block = st.enter_context(nc.Block())
        sets = [(0, 0), (1, 1), (1, 2), (2, 2), (2, 1)]
        small = []

        x_view = io["L0_attn_a_hidden_states"].rearrange("b (t p) d -> p (b t) d", p=P)
        X3 = X[:, :].rearrange("p (t d) -> p t d", d=D)

        @block.sync
        def _(sp):
            names = [("L0_attn_a_c_attn_kernel", 0, 6), ("L0_attn_a_c_proj_kernel", 6, 2), ("L0_attn_b_Wq", 8, 2),
                     ("L0_attn_b_Wk", 10, 2), ("L0_attn_b_Wv", 12, 2), ("L0_attn_b_Wo", 14, 2)]
            for name, at, n in names:
                sp.dma_start(natural[:, at:at + n, :], io[name].rearrange("(m p) d -> p m d", p=P)).then_inc(w_loaded, 16)
            for g in range(NG):
                sp.dma_start(X3[:, g * GT:(g + 1) * GT, :], x_view[:, g * GT:(g + 1) * GT, :]).then_inc(x_loaded, 16)
            for e in range(EX):
                src = io["L0_ffn_sw1"] if e == SH else io["L0_ffn_rw1"][e]
                sp.dma_start(big["w1"][:, e, :, :], src.rearrange("(k p) h -> p k h", p=P)).then_inc(ffn_loaded, 16)
                src = io["L0_ffn_sw2"] if e == SH else io["L0_ffn_rw2"][e]
                sp.dma_start(big["w2"][:, e, :, :], src.rearrange("(k p) d -> p k d", p=P)).then_inc(ffn_loaded, 16)
            sp.wait_ge(turned_out, 8)
            for layer in range(2):
                sp.dma_start(scratch["w"][layer], WT[:, :, layer * 4 * D:(layer + 1) * 4 * D]).then_inc(kept, 16)
            sp.wait_ge(zeroed, 9)
            for j in range(8):
                n = ST // 8
                sp.dma_start(scratch["slots_in"][j * n * P:(j + 1) * n * P, :].rearrange("(a p) d -> p a d", p=P),
                             zeros[:, :].unsqueeze(1).to_broadcast([P, n, D])).then_inc(slots_zeroed, 16)
            sp.wait_ge(kept, 32)
            sp.wait_ge(slots_zeroed, 16 * 8)
            sp.wait_ge(x_loaded, 16 * NG)

        @block.scalar
        def _(act):
            def load(dst, src):
                act.dma_start(dst, src, allow_slow_non_contiguous=True).then_inc(small_loaded, 16)
                small.append(1)
            for i, n in enumerate(("L0_attn_b_Wqs", "L0_attn_b_Wks", "L0_attn_b_Wvs")):
                for r in range(P // HD):
                    load(wcol[r * HD:(r + 1) * HD, i, :], io[n].rearrange("c d -> d c"))
            load(big["bcolA"][:, :], io["L0_attn_a_c_attn_bias"].rearrange("(m p) -> p m", p=P))
            for i, n in enumerate(("L0_attn_b_bq", "L0_attn_b_bk", "L0_attn_b_bv")):
                load(big["bcolB"][:, 2 * i:2 * i + 2], io[n].rearrange("(m p) -> p m", p=P))
            load(big["scolB"][:, :], io["L0_attn_b_temp"].partition_broadcast(P))
            load(big["vbA"][:, :], io["L0_attn_a_c_attn_bias"][2 * D:3 * D].partition_broadcast(P))
            load(big["obA"][:, :], io["L0_attn_a_c_proj_bias"].partition_broadcast(P))
            load(big["vbB"][:, :], io["L0_attn_b_bv"].partition_broadcast(P))
            load(big["obB"][:, :], io["L0_attn_b_bo"].partition_broadcast(P))
            load(big["rb"][:, :], io["L0_ffn_router_b"].partition_broadcast(P))
            load(big["rw"][:, :, :], io["L0_ffn_router_w"].rearrange("(k p) e -> p k e", p=P))
            load(big["b1"][:, 0:NE, :], io["L0_ffn_rb1"].rearrange("e (m p) -> p e m", p=P))
            load(big["b1"][:, SH, :], io["L0_ffn_sb1"].rearrange("(m p) -> p m", p=P))
            load(big["b2"][0:NE, :], io["L0_ffn_rb2"])
            load(big["b2"][SH:SH + 1, :], io["L0_ffn_sb2"].rearrange("(a d) -> a d", a=1))
            for (src, rot), (row, col) in zip(sets, [(0, 0), (0, 1), (64, 1), (0, 2), (64, 2)]):
                b = io[("L0_attn_b_bqs", "L0_attn_b_bks", "L0_attn_b_bvs")[src]]
                for c in range(C3):
                    f = (c + rot) % C3
                    load(xb_in[row + c:row + c + 3 * (H - 1) + 1:3, col:col + 1],
                         b[f:f + 1].partition_broadcast(H))

        @block.gpsimd
        def _(pool):
            pool.memset(big["identF"][:, :], 0.0).then_inc(zeroed, 1)
            pool.memset(big["identB"][:, :], 0.0).then_inc(zeroed, 1)
            pool.memset(big["maskK"][:, :], 0.0).then_inc(zeroed, 1)
            pool.memset(big["maskQ"][:, :], 0.0).then_inc(zeroed, 1)
            pool.memset(big["scolA"][:, :], HD ** -0.5).then_inc(zeroed, 1)
            pool.memset(big["eps"][:, :], EPS).then_inc(zeroed, 1)
            pool.memset(zeros[:, :], 0.0).then_inc(zeroed, 1)
            pool.memset(big["before"][:, :], 0.0).then_inc(zeroed, 1)
            pool.memset(big["all1"][:, :], 1.0).then_inc(zeroed, 1)
            pool.wait_ge(zeroed, 9)
            pool.affine_select(out=big["before"][:, :], in_=big["before"][:, :], compare_op=ALU.is_ge, fill=1.0, base=0,
                               pattern=[[-1, P]], channel_multiplier=1).then_inc(masks_made, 1)
            for m in ("identF", "identB"):
                pool.affine_select(out=big[m][:, :], in_=big[m][:, :], compare_op=ALU.not_equal, fill=1.0, base=0,
                                   pattern=[[-1, P]], channel_multiplier=1).then_inc(ident_made, 1)
            pool.affine_select(out=big["maskK"][:, :], in_=big["maskK"][:, :], compare_op=ALU.is_ge, fill=NEG, base=0,
                               pattern=[[1, P]], channel_multiplier=-1).then_inc(masks_made, 1)
            pool.affine_select(out=big["maskQ"][:, :], in_=big["maskQ"][:, :], compare_op=ALU.is_ge, fill=NEG, base=0,
                               pattern=[[-1, P]], channel_multiplier=1).then_inc(masks_made, 1)
            pool.wait_ge(small_loaded, 16 * len(small))
            for s, (src, rot) in enumerate(sets):
                for c in range(C3):
                    f = (c + rot) % C3
                    pool.tensor_copy(blockdiag[:, s, :, :, c],
                                     wcol[:, src, f:f + 1].unsqueeze(2).to_broadcast([P, 2, H])).then_inc(bd_link, 1)
            n = 15
            pool.wait_ge(bd_link, n)
            pool.affine_select(out=blockdiag[:, :, :, :, :], in_=blockdiag[:, :, :, :, :], compare_op=ALU.is_ge,
                               fill=0.0, base=0, pattern=[[0, 5], [P, 2], [-HD, H], [0, C3]],
                               channel_multiplier=1).then_inc(bd_link, 1)
            pool.wait_ge(bd_link, n + 1)
            pool.affine_select(out=blockdiag[:, :, :, :, :], in_=blockdiag[:, :, :, :, :], compare_op=ALU.is_ge,
                               fill=0.0, base=HD - 1, pattern=[[0, 5], [-P, 2], [HD, H], [0, C3]],
                               channel_multiplier=-1).then_inc(bd_link, 1)

        @block.tensor
        def _(pe):
            pe.wait_ge(ident_made, 1)
            pe.wait_ge(w_loaded, 16 * 6)
            for n in range(8):
                kk, m0 = n // 4, 4 * (n % 4)
                if n >= 4:
                    pe.wait_ge(turned_out, n - 3)
                for j in range(4):
                    last = nc.tensor.transpose(banks[n % 4][:, j * P:(j + 1) * P],
                                               natural[:, m0 + j, kk * P:(kk + 1) * P], big["identF"][:, :])
                last.then_inc(turned, 1)
            pe.wait_ge(bd_link, 17)
            for kk in range(KD):
                for s, (src, _rot) in enumerate(sets):
                    at = (kk * 5 + s) * XR
                    for half in range(2):
                        last = nc.tensor.matmul(banks[4][:, at:at + XR],
                                                natural[:, 8 + 2 * src + half, kk * P:(kk + 1) * P],
                                                blockdiag[:, s, half, :, :].rearrange("p h c -> p (h c)"),
                                                start=half == 0, stop=half == 1)
            last.then_inc(comp_done, 1)
            for (s, (src, _rot)), (row, col) in zip(enumerate(sets), [(0, 0), (0, 1), (64, 1), (0, 2), (64, 2)]):
                for half in range(2):
                    last = nc.tensor.matmul(banks[5][row:row + XR, col:col + 1],
                                            blockdiag[:, s, half, :, :].rearrange("p h c -> p (h c)"),
                                            big["bcolB"][:, 2 * src + half:2 * src + half + 1],
                                            start=half == 0, stop=half == 1)
            last.then_inc(comp_done, 1)

        @block.vector
        def _(dve):
            for n in range(8):
                dve.wait_ge(turned, n + 1)
                kk, m0 = n // 4, 4 * (n % 4)
                nc.vector.tensor_copy(WT[:, kk, m0 * P:(m0 + 4) * P], banks[n % 4][:, :]).then_inc(turned_out, 1)
            dve.wait_ge(x_loaded, 16 * NG)
            token_stats(nc, dve, big, range(NT), measured, 0)
            dve.wait_ge(comp_done, 1)
            nc.vector.tensor_copy(big["XW"][:, :, :, :].rearrange("p k s r -> p (k s r)"),
                                  banks[4][:, 0:10 * XR]).then_inc(comp_out, 1)
            dve.wait_ge(comp_done, 2)
            dve.wait_ge(small_loaded, 16 * len(small))
            for row, cols in ((0, slice(0, 3)), (64, slice(1, 3))):
                nc.vector.tensor_tensor(big["xb"][row:row + XR, cols], banks[5][row:row + XR, cols],
                                        xb_in[row:row + XR, cols], ALU.add).then_inc(comp_out, 1)


def token_stats(nc, dve, big, tiles, measured, before):
    for n, t in enumerate(tiles):
        nc.vector.bn_stats(big["stats"][:, t, :], big["X"][:, t * D:(t + 1) * D]).then_inc(measured, 1)
    dve.wait_ge(measured, before + len(tiles))
    for t in tiles:
        nc.vector.bn_aggr(big["mv"][:, t, :], big["stats"][:, t, :])


def attention(nc, tag, causal, big, scratch, sb, pb, sem):
    with ExitStack() as st:
        big["WT"] = sb(f"WT{tag}", [P, KD, 4 * D], F32, st)
        V = sb(f"V{tag}", [P, NT * D], F32, st)
        project(nc, tag, causal, big, scratch, V, sb, pb, sem)
        units(nc, tag, causal, big, scratch, V, sb, pb, sem)
        combine(nc, tag, big, V, sb, pb, sem)


def project(nc, tag, causal, big, scratch, V, sb, pb, sem):
    extra = not causal
    NI = 6 if extra else 4
    NPC = 4
    NPQ = 5 if extra else 4
    w0 = 0
    bcol = big["bcolA"] if causal else big["bcolB"]
    scol = big["scolA"] if causal else big["scolB"]
    vb = big["vbA"] if causal else big["vbB"]
    X = big["X"]
    with ExitStack() as st:
        XN = [sb(f"XN{tag}{i}", [P, GT, D], F32, st) for i in range(2)]
        xT = [sb(f"xT{tag}{i}", [P, KD, G], F32, st) for i in range(2)]
        Y = [sb(f"Y{tag}{i}", [P, G], F32, st) for i in range(2)]
        R = [sb(f"R{tag}{i}", [P, G], F32, st) for i in range(2)]
        PC = [sb(f"PC{tag}{i}", [P, 3, G], BF16, st) for i in range(NPC)]
        if extra:
            V1V2 = sb(f"V1V2{tag}", [P, G], F32, st)
            prodA = sb(f"prodA{tag}", [XR, G], F32, st)
            prodB = sb(f"prodB{tag}", [XR, G], F32, st)
        qbias = sb(f"qbias{tag}", [P, 3], F32, st)
        TP = [pb(f"TP{tag}{i}", [P, G], st) for i in range(2)]
        PQ = [pb(f"PQ{tag}{i}", [P, G], st) for i in range(2)]
        PV = [pb(f"PV{tag}{i}", [P, G], st) for i in range(2)]
        PE_ = [pb(f"PE{tag}{i}", [P, G], st) for i in range(2)] if extra else None
        s = {n: sem(f"{n}{tag}") for n in (
            "root_done", "rstd_done", "xn_ready", "turned", "xT_ready", "qk_ready", "qk_read", "y_ready",
            "r_ready", "p1_ready", "p2_ready", "v_ready", "v_read", "ex_ready", "vv_ready", "prod_link", "cross_ready")}
        stored = [sem(f"stored{tag}{i}") for i in range(NPC)]

        w_in = sem(f"w_in{tag}")

        def pieces_free(eng, i, k):
            eng.wait_ge(stored[k % NPC], 16 * (i * (2 * NI // NPC) + k // NPC + 1))

        block = st.enter_context(nc.Block())

        def groups(eng):
            with eng.Fori(0, NG // 2 - 1) as i:
                for par in range(2):
                    yield i, par, 2 * i + par, True
            for par in range(2):
                yield NG // 2 - 1, par, NG - 2 + par, par == 0

        @block.vector
        def _(dve):
            dve.wait_ge(s["root_done"], 1)
            nc.vector.reciprocal(big["rstd"][:, :], big["std"][:, :]).then_inc(s["rstd_done"], 1)
            for m in range(2):
                nc.vector.tensor_tensor(qbias[:, m:m + 1], bcol[:, m:m + 1], scol[:, :], ALU.mult).then_inc(s["rstd_done"], 1)
            nc.vector.tensor_tensor(qbias[0:XR, 2:3], big["xb"][0:XR, 0:1], scol[0:XR, :], ALU.mult)\
                .then_inc(s["rstd_done"], 1)
            dve.wait_ge(s["rstd_done"], 4)
            dve.sem_inc(s["p2_ready"], 1)
            dve.sem_inc(s["r_ready"], 2)
            dve.sem_inc(s["v_read"], 2)
            if extra:
                dve.sem_inc(s["cross_ready"], 1)

            def normalise(par, g):
                dve.wait_ge(s["turned"], KD * (g + 1))
                for t in range(GT):
                    nc.vector.tensor_scalar(XN[par][:, t, :], X[:, bass.ds((g * GT + t) * D, D)],
                                            big["mv"][:, bass.ds(g * GT + t, 1), 0], big["rstd"][:, bass.ds(g * GT + t, 1)],
                                            ALU.subtract, ALU.mult).then_inc(s["xn_ready"], 1)

            normalise(0, 0)
            for i, par, g, more in groups(dve):
                if more:
                    normalise(1 - par, g + 1)

                def remainder(n, first):
                    rows = P if n < 4 else XR
                    k = par * NI + n
                    if n < NPQ:
                        dve.wait_ge(s["qk_read"], 2 * i * NPQ + par * NPQ + n + 1 + 2)
                    else:
                        dve.wait_ge(s["y_ready"], g + 1)
                    dve.wait_ge(s["p1_ready"], 2 * i * NI + k + 1)
                    dve.wait_ge(s["p2_ready"], 2 * i * NI + (par * NI if first or n == 1 else k - 1) + 1)
                    nc.vector.tensor_tensor(R[k % 2][0:rows, :], Y[k % 2][0:rows, :], PC[k % NPC][0:rows, 0, :],
                                            ALU.subtract).then_inc(s["r_ready"], 1)

                def last_piece(n):
                    rows = P if n < 4 else XR
                    k = par * NI + n
                    dve.wait_ge(s["p1_ready"], 2 * i * NI + k + 1 + 2)
                    dve.wait_ge(s["r_ready"], 2 * i * NI + k + 1 + 2)
                    nc.vector.tensor_tensor(PC[k % NPC][0:rows, 2, :], R[k % 2][0:rows, :], PC[k % NPC][0:rows, 1, :],
                                            ALU.subtract).then_inc(s["p2_ready"], 1)

                for n in range(NI):
                    if n == 5:
                        dve.wait_ge(s["ex_ready"], 2 * (g + 1))
                        dve.wait_ge(s["vv_ready"], 2 * (g + 1))
                        for dst, row in ((prodA, 0), (prodB, 64)):
                            nc.vector.scalar_tensor_tensor(
                                dst[:, :], PE_[0][row:row + XR, :], big["xb"][row:row + XR, 1:2],
                                V1V2[row:row + XR, :], ALU.add, ALU.mult).then_inc(s["prod_link"], 1)
                        dve.wait_ge(s["prod_link"], 2 * (g + 1))
                        nc.vector.tensor_tensor(Y[(par * NI + n) % 2][0:XR, :], prodA[:, :], prodB[:, :],
                                                ALU.subtract).then_inc(s["cross_ready"], 1)
                    remainder(n, n == 0)
                    if n >= 1:
                        last_piece(n - 1)
                last_piece(NI - 1)
                for pair in range(2):
                    dve.wait_ge(s["v_ready"], 2 * g + pair + 1 + 4)
                    nc.vector.tensor_tensor(
                        V[:, bass.ds((g * GT + 2 * pair) * D, 2 * D)].rearrange("p (t d) -> p t d", d=D),
                        PV[pair][:, :].rearrange("p (t d) -> p t d", d=D),
                        vb[:, :].unsqueeze(1).to_broadcast([P, 2, D]), ALU.add).then_inc(s["v_read"], 1)

        @block.scalar
        def _(act):
            nc.scalar.activation(big["std"][:, :], big["mv"][:, :, 1], ACT.Sqrt, bias=big["eps"][:, :])\
                .then_inc(s["root_done"], 1)
            act.sem_inc(s["xT_ready"], KD)
            act.sem_inc(s["qk_read"], 2)
            act.sem_inc(s["p1_ready"], 2)
            act.wait_ge(s["rstd_done"], 4)

            def copy_turned(par, g):
                act.wait_ge(s["v_ready"], 2 * (g + 1))
                for kk in range(KD):
                    act.wait_ge(s["turned"], KD * g + kk + 1 + 2 * KD)
                    nc.scalar.copy(xT[par][:, kk, :], TP[kk][:, :]).then_inc(s["xT_ready"], 1)

            copy_turned(0, 0)
            for i, par, g, more in groups(act):

                def middle(n):
                    rows = P if n < 4 else XR
                    k = par * NI + n
                    act.wait_ge(s["r_ready"], 2 * i * NI + k + 1 + 2)
                    nc.scalar.copy(PC[k % NPC][0:rows, 1, :], R[k % 2][0:rows, :]).then_inc(s["p1_ready"], 1)

                for n in range(NI):
                    k = par * NI + n
                    y, rows = Y[k % 2], (P if n < 4 else XR)
                    pieces_free(act, i, k)
                    if extra and n == 5:
                        act.wait_ge(s["ex_ready"], 2 * (g + 1))
                        act.wait_ge(s["cross_ready"], g + 1)
                        for row in (0, 64):
                            nc.scalar.activation(V1V2[row:row + XR, :], PE_[1][row:row + XR, :], ACT.Identity,
                                                 bias=big["xb"][row:row + XR, 2:3]).then_inc(s["vv_ready"], 1)
                        middle(n - 1)
                        act.wait_ge(s["cross_ready"], g + 2)
                        nc.scalar.copy(PC[k % NPC][0:rows, 0, :], y[0:rows, :]).then_inc(s["y_ready"], 1)
                        continue
                    q = par * NPQ + n
                    act.wait_ge(s["qk_ready"], 2 * i * NPQ + q + 1)
                    act.wait_ge(s["r_ready"], 2 * i * NI + k + 1)
                    for dst in (y[0:rows, :], PC[k % NPC][0:rows, 0, :]):
                        if n < 2:
                            last = nc.scalar.activation(dst, PQ[q % 2][:, :], ACT.Identity, bias=qbias[:, n:n + 1],
                                                        scale=scol[:, :])
                        elif n < 4:
                            last = nc.scalar.activation(dst, PQ[q % 2][:, :], ACT.Identity, bias=bcol[:, n:n + 1])
                        else:
                            last = nc.scalar.activation(dst, PQ[q % 2][0:XR, :], ACT.Identity,
                                                        bias=qbias[0:XR, 2:3], scale=scol[0:XR, :])
                    last.then_inc(s["qk_read"], 1)
                    if n >= 1:
                        middle(n - 1)
                if more:
                    copy_turned(1 - par, g + 1)
                middle(NI - 1)

        @block.tensor
        def _(pe):
            pe.sem_inc(s["turned"], 2 * KD)
            pe.sem_inc(s["v_ready"], 4)
            pe.wait_ge(w_in, 16)

            def turn(par, g):
                pe.wait_ge(s["xT_ready"], KD * (g + 1))
                for kk in range(KD):
                    for t in range(GT):
                        if kk == 0:
                            pe.wait_ge(s["xn_ready"], GT * g + t + 1)
                        last = nc.tensor.transpose(TP[kk][:, t * P:(t + 1) * P],
                                                   XN[par][:, t, kk * P:(kk + 1) * P], big["identF"][:, :])
                    last.then_inc(s["turned"], 1)

            turn(0, 0)
            for i, par, g, more in groups(pe):
                pe.wait_ge(s["xT_ready"], KD * (g + 2))
                for n in range(NPQ):
                    q = par * NPQ + n
                    pe.wait_ge(s["qk_read"], 2 * i * NPQ + q + 1)
                    for kk in range(KD):
                        if n < 4:
                            last = nc.tensor.matmul(PQ[q % 2][:, :], big["WT"][:, kk, w0 + n * P:w0 + (n + 1) * P],
                                                    xT[par][:, kk, :], start=kk == 0, stop=kk == KD - 1)
                        else:
                            last = nc.tensor.matmul(PQ[q % 2][0:XR, :], big["XW"][:, kk, 0, :], xT[par][:, kk, :],
                                                    start=kk == 0, stop=kk == KD - 1)
                    last.then_inc(s["qk_ready"], 1)
                if extra:
                    pe.wait_ge(s["cross_ready"], g + 1)
                    for b, sets in ((0, (1, 2)), (1, (3, 4))):
                        for kk in range(KD):
                            for row, j in zip((0, 64), sets):
                                last = nc.tensor.matmul(PE_[b][row:row + XR, :], big["XW"][:, kk, j, :],
                                                        xT[par][:, kk, :], start=kk == 0, stop=kk == KD - 1)
                        last.then_inc(s["ex_ready"], 1)
                if more:
                    turn(1 - par, g + 1)
                for pair in range(2):
                    pe.wait_ge(s["v_read"], 2 * g + pair + 1)
                    for t in (2 * pair, 2 * pair + 1):
                        for kk in range(KD):
                            last = nc.tensor.matmul(PV[pair][:, (t % 2) * D:(t % 2 + 1) * D],
                                                    xT[par][:, kk, t * P:(t + 1) * P],
                                                    big["WT"][:, kk, w0 + 2 * D:w0 + 3 * D],
                                                    start=kk == 0, stop=kk == KD - 1)
                    last.then_inc(s["v_ready"], 1)

        @block.sync
        def _(sp):
            sp.dma_start(big["WT"][:, :, :], scratch["w"][0 if causal else 1]).then_inc(w_in, 16)
            for n in range(NPC):
                sp.sem_inc(stored[n], 16)
            for i, par, g, more in groups(sp):
                b, t0 = g // (NG // B), (g % (NG // B)) * G
                for n in range(NI):
                    k = par * NI + n
                    sp.wait_ge(s["p2_ready"], 2 * i * NI + k + 1 + 1)
                    if n < 4:
                        dst = scratch["q" if n < 2 else "k"][bass.ds(b, 1), :, (n % 2) * P:(n % 2 + 1) * P, bass.ds(t0, G)]
                        rows = P
                    else:
                        dst = scratch["qx" if n == 4 else "kx"][bass.ds(b, 1), :, :, bass.ds(t0, G)]
                        rows = XR
                    sp.dma_start(dst.rearrange("b k r t -> r (b k) t"), PC[k % NPC][0:rows, :, :]).then_inc(stored[k % NPC], 16)
            for n in range(NPC):
                sp.wait_ge(stored[n], 16 * NI * NG // NPC + 16)


def plan_units(causal):
    HALF = S // 2
    order = [1, 0]
    steps = []
    for hf in order:
        for kt in range(KT):
            lo = max(0, kt * P - hf * HALF) if causal else 0
            if lo < HALF:
                steps.append((hf, kt, lo))
    chunks = []
    for hf in order:
        for qt in range(8 * hf, 8 * hf + 8):
            keys = (qt + 1) * P if causal else S
            for c in range((keys + G - 1) // G):
                chunks.append((hf, qt, c, min(G, keys - c * G)))
    shift = 4 if causal else 6
    ahead = 1.1 if causal else 1.0
    n = len(steps)
    weight = [(HALF - lo) // P + 2 for _, _, lo in steps]
    cyc = [(shift + j) % n for j in range(n)]
    total = sum(weight)
    total_c = sum(w + P for *_, w in chunks)
    at = [[] for _ in range(n)]
    acc = 0
    j = 0
    donew = 0
    for pos, stp in enumerate(cyc):
        acc += weight[stp]
        while j < len(chunks) and (donew + chunks[j][3] / 2) / total_c <= ahead * acc / total or (pos == n - 1 and j < len(chunks)):
            at[pos].append(j)
            donew += chunks[j][3] + P
            j += 1
    return order, steps, chunks, shift, cyc, at


def units(nc, tag, causal, big, scratch, V, sb, pb, sem):
    extra = not causal
    NM = 2
    NR = NM + 6 * HD + (6 * C3 if extra else 0)
    HALF = S // 2
    order, steps, chunks, shift, cyc, at = plan_units(causal)
    NS, NC, NP = len(steps), len(chunks), 4
    assert NS % NP == 0 and NC % 2 == 0
    H1 = sum(1 for x in steps if x[0] == order[0])
    per_half = {hf: sum(1 for c in chunks if c[0] == hf) for hf in order}
    z1 = next(p for p in range(NS) if at[p] and at[p][-1] >= per_half[order[0]] - 1)
    O_PREV, O_THIS = 2, H1 + 2
    M_SECOND = shift + 1
    M_FIRST = shift + z1 + 1
    assert M_FIRST < NS and len({O_PREV, O_THIS, M_SECOND, M_FIRST}) == 4 and M_SECOND < H1
    with ExitStack() as st:
        QS = [sb(f"QS{tag}{i}", [P, S], BF16, st) for i in range(2)]
        KS = [sb(f"KS{tag}{i}", [P, S], BF16, st) for i in range(2)]
        Vh = [sb(f"Vh{tag}{i}", [P, KT, 32], F32, st) for i in range(2)]
        PR = [sb(f"PR{tag}{i}", [P, HALF], F32, st) for i in range(NP)]
        Osb = sb(f"Osb{tag}", [P, D], F32, st)
        mx = [sb(f"mx{tag}{i}", [P, KT, 4], F32, st) for i in range(2)]
        nm = sb(f"nm{tag}", [P, 8], F32, st)
        nmp = [sb(f"nmp{tag}{i}", [P, 8, NM], BF16, st) for i in range(2)]
        rec = sb(f"rec{tag}", [P, 2, 4], F32, st)
        ones = sb(f"ones{tag}", [NM, S], BF16, st)
        zeros = sb(f"zeros{tag}", [NM, S], BF16, st)
        SP_ = [pb(f"S{tag}{i}", [P, HALF], st) for i in range(2)]
        MP = [pb(f"M{tag}{i}", [P, G], st) for i in range(2)]
        OP = pb(f"O{tag}", [P, G], st)
        TB = pb(f"T{tag}", [P, G], st)
        s = {n: sem(f"{n}{tag}") for n in (
            "ones_made", "ones_in", "vh_preset", "mx_preset", "vh_ready", "scores_ready", "exp_done", "max_ready", "max_read", "pv_done",
            "o_copied", "o_turned", "nm_link", "nm_made", "nm_turned", "nm_rows", "ao_link", "bias_added")}
        loaded = [sem(f"qk_loaded{tag}{i}") for i in range(2)]
        nload = 7 + (6 if extra else 0)
        block = st.enter_context(nc.Block())

        def unit_loop(eng, emit):
            emit(0, 0, False, True)
            with eng.Fori(0, (U - 2) // 2) as i:
                emit(2 * i + 1, 1, True, True)
                emit(2 * i + 2, 0, True, True)
            emit(U - 1, 1, True, False)

        def max_part(u, st_, nxt):
            pos = (st_ - shift) % NS
            if st_ < shift:
                return [(u, j, True) for j in at[pos]]
            return [(u + 1, j, False) for j in at[pos]] if nxt else []

        @block.gpsimd
        def _(pool):
            for i in range(2):
                pool.memset(Vh[i][:, :, HD:], 0.0).then_inc(s["vh_preset"], 1)
            pool.memset(zeros[:, :], 0.0).then_inc(s["ones_made"], 1)
            pool.memset(ones[:, :], 1.0).then_inc(s["ones_made"], 1)
            pool.wait_ge(s["vh_preset"], 2)
            for i in range(2):
                pool.memset(Vh[i][:, :, HD:HD + 1], 1.0).then_inc(s["vh_preset"], 1)
            pool.wait_ge(s["vh_preset"], 4)

            def copy_values(u, par, _prev, _nxt):
                if not (isinstance(u, int) and u < 2):
                    pool.wait_ge(s["pv_done"], (u - 1) * NS + NP)
                b, h = u // H, u % H
                src = V[:, :].rearrange("p (b k c) -> p b k c", b=B, k=KT)
                nc.gpsimd.tensor_copy(Vh[par][:, :, 0:HD], src[:, bass.ds(b, 1), :, bass.ds(h * HD, HD)]
                                      .rearrange("p b k c -> p (b k) c")).then_inc(s["vh_ready"], 1)

            unit_loop(pool, copy_values)
            ob = big["obA"] if causal else big["obB"]
            with pool.Fori(0, NT) as t:
                nc.gpsimd.tensor_tensor(big["X"][:, bass.ds(t * D, D)], big["X"][:, bass.ds(t * D, D)], ob[:, :],
                                        ALU.add).then_inc(s["bias_added"], 1)

        def load_unit(sp, u, par):
            b, h = u // H, u % H
            sp.dma_start(QS[par][0:NM, :], zeros[:, :]).then_inc(loaded[par], 16)
            for side, buf, runs in (("q", QS, Q_RUNS), ("k", KS, K_RUNS)):
                for scr, width, row in [(scratch[side], HD, NM)] + ([(scratch[side + "x"], C3, NM + 6 * HD)] if extra else []):
                    for first, pieces, copies in runs:
                        n = pieces * copies * width
                        src = scr[bass.ds(b, 1), first:first + pieces, bass.ds(h * width, width), :]\
                            .rearrange("b k r t -> (b k) r t")
                        if copies > 1:
                            src = src.to_broadcast([copies, width, S])
                        sp.dma_start(buf[par][row:row + n, :], src).then_inc(loaded[par], 16)
                        row += n

        @block.sync
        def _(sp):
            sp.wait_ge(s["ones_made"], 2)
            for i in range(2):
                sp.dma_start(KS[i][0:NM, :], ones[:, :]).then_inc(s["ones_in"], 16)
            load_unit(sp, 0, 0)

            def emit(u, par, _prev, nxt):
                if nxt:
                    sp.wait_ge(s["scores_ready"], u * NS)
                    load_unit(sp, u + 1, 1 - par)

            unit_loop(sp, emit)

        @block.tensor
        def _(pe):
            pe.sem_inc(s["pv_done"], NP)

            def maxima(u, par, j):
                hf, qt, c, w = chunks[j]
                if j == 0:
                    pe.wait_ge(loaded[par], (u // 2 + 1) * 16 * nload)
                pe.wait_ge(s["max_read"], u * NC + j + 1)
                diag = causal and c == qt // 4
                last = nc.tensor.matmul(MP[j % 2][:, 0:w], QS[par][0:NR, qt * P:(qt + 1) * P],
                                        KS[par][0:NR, c * G:c * G + w], start=True, stop=not diag)
                if diag:
                    last = nc.tensor.matmul(MP[j % 2][:, w - P:w], big["identB"][:, :], big["maskQ"][:, :],
                                            start=False, stop=True)
                last.then_inc(s["max_ready"], 1)

            def scores(u, par, x):
                hf, kt, lo = steps[x]
                pe.wait_ge(s["exp_done"], u * NS + x + 1)
                if x == 0 or x == H1:
                    pe.wait_ge(s["nm_rows"], 2 * u + 1 + (x == H1))
                q0 = hf * HALF
                diag = causal and kt * P >= q0
                for c in range(2):
                    a, z = max(lo, c * G), (c + 1) * G
                    if a >= z:
                        continue
                    here = diag and a == lo
                    last = nc.tensor.matmul(SP_[x % 2][:, a:z], KS[par][0:NR, kt * P:(kt + 1) * P],
                                            QS[par][0:NR, q0 + a:q0 + z], start=True, stop=not here)
                    if here:
                        last = nc.tensor.matmul(SP_[x % 2][:, lo:lo + P], big["identB"][:, :], big["maskK"][:, :],
                                                start=False, stop=True)
                last.then_inc(s["scores_ready"], 1)

            def values(u, par, x):
                hf, kt, lo = steps[x]
                pe.wait_ge(s["exp_done"], u * NS + x + 1 + 2)
                if x == 0:
                    pe.wait_ge(s["vh_ready"], u + 1)
                if x == 0 or x == H1:
                    pe.wait_ge(s["o_copied"], 2 * u + (x == H1))
                last_kt = {j: (min(KT, (hf * HALF + (j + 1) * 256) // P) - 1 if causal else KT - 1) for j in range(4)}
                for j in range(4):
                    a, z = max(lo, 256 * j), 256 * (j + 1)
                    if a >= z:
                        continue
                    last = nc.tensor.matmul(OP[32 * j:32 * j + 32, a - 256 * j:256], Vh[par][:, kt, :],
                                            PR[x % NP][:, a:z], start=kt == 0, stop=kt == last_kt[j])
                last.then_inc(s["pv_done"], 1)

            def turn_output(k, maxima_before):
                pe.wait_ge(s["o_copied"], k + 1)
                pe.wait_ge(s["ao_link"], 2 * k)
                pe.wait_ge(s["nm_rows"], maxima_before)
                for c in range(2):
                    last = nc.tensor.transpose(TB[:, c * P:(c + 1) * P], Osb[:, c * P:(c + 1) * P], big["identF"][:, :])
                last.then_inc(s["o_turned"], 1)

            def turn_max(k, pos, outputs_before):
                pe.wait_ge(s["nm_made"], k + 1)
                pe.wait_ge(s["nm_rows"], k)
                pe.wait_ge(s["ao_link"], 2 * outputs_before)
                for q in range(8):
                    last = nc.tensor.transpose(TB[:, :].bitcast(BF16)[0:NM, q * P:(q + 1) * P], nmp[pos][:, q, :],
                                               big["identB"][:, :])
                last.then_inc(s["nm_turned"], 1)

            pe.wait_ge(s["ones_in"], 32)
            for x in range(shift, NS):
                for _, j, _ in max_part(-1, x, True):
                    maxima(0, 0, j)
            turn_max(0, 0, 0)

            def emit(u, par, prev, nxt):
                for x in range(NS):
                    scores(u, par, x)
                    mp = max_part(u, x, nxt)
                    for w, j, own in mp[:(len(mp) + 1) // 2]:
                        maxima(w, par if own else 1 - par, j)
                    if x > 0:
                        values(u, par, x - 1)
                    elif prev:
                        values(u - 1, 1 - par, NS - 1)
                    for w, j, own in mp[(len(mp) + 1) // 2:]:
                        maxima(w, par if own else 1 - par, j)
                    if x == O_PREV and prev:
                        turn_output(2 * u - 1, 2 * u + 1 + (M_SECOND < O_PREV))
                    if x == M_SECOND:
                        turn_max(2 * u + 1, 1, 2 * u - (0 if O_PREV < M_SECOND or not prev else 1))
                    if x == O_THIS:
                        turn_output(2 * u, 2 * u + 2 + (M_FIRST < O_THIS and nxt))
                    if x == M_FIRST and nxt:
                        turn_max(2 * u + 2, 0, 2 * u + (O_THIS < M_FIRST))

            unit_loop(pe, emit)
            values(U - 1, 1, NS - 1)
            turn_output(2 * U - 1, 2 * U)

        @block.scalar
        def _(act):
            act.sem_inc(s["exp_done"], 2)

            def put_max(k, pos, par):
                hf = order[pos]
                act.wait_ge(s["nm_turned"], k + 1)
                nc.scalar.copy(QS[par][0:NM, hf * HALF:(hf + 1) * HALF], TB[:, :].bitcast(BF16)[0:NM, 0:HALF])\
                    .then_inc(s["nm_rows"], 1)

            def copy_output(k):
                act.wait_ge(s["o_turned"], k)
                nc.scalar.copy(Osb[:, :], OP[:, 0:D]).then_inc(s["o_copied"], 1)

            def emit(u, par, prev, nxt):
                for x in range(NS):
                    hf, kt, lo = steps[x]
                    act.wait_ge(s["scores_ready"], u * NS + x + 1)
                    act.wait_ge(s["pv_done"], u * NS + x + 1)
                    nc.scalar.activation(PR[x % NP][:, lo:], SP_[x % 2][:, lo:], ACT.Exp).then_inc(s["exp_done"], 1)
                    if x == 0 and prev:
                        act.wait_ge(s["pv_done"], u * NS + NP)
                        copy_output(2 * u - 1)
                    if x == H1:
                        act.wait_ge(s["pv_done"], u * NS + H1 + NP)
                        copy_output(2 * u)
                    if x == M_SECOND:
                        put_max(2 * u + 1, 1, par)
                    if x == M_FIRST and nxt:
                        put_max(2 * u + 2, 0, 1 - par)

            put_max(0, 0, 0)
            unit_loop(act, emit)
            act.wait_ge(s["pv_done"], U * NS + NP)
            copy_output(2 * U - 1)

        @block.vector
        def _(dve):
            dve.sem_inc(s["max_read"], 2)
            if causal:
                for i in range(2):
                    nc.vector.memset(mx[i][:, :, :], LOWEST).then_inc(s["mx_preset"], 1)
                dve.wait_ge(s["mx_preset"], 2)

            def reduce_chunk(u, par, j):
                hf, qt, c, w = chunks[j]
                dve.wait_ge(s["max_ready"], u * NC + j + 1)
                nc.vector.tensor_reduce(mx[par][:, qt, c:c + 1], MP[j % 2][:, 0:w], AX.X, ALU.max)\
                    .then_inc(s["max_read"], 1)

            def make_max(u, par, pos, k):
                hf = order[pos]
                done = u * NC + (per_half[order[0]] if pos == 0 else NC)
                dve.wait_ge(s["max_read"], done + 2)
                dve.wait_ge(s["nm_made"], k)
                if not (isinstance(k, int) and k < 2):
                    dve.wait_ge(s["nm_turned"], k - 1)
                link = chain(dve, s["nm_link"], 2 * k)
                link(nc.vector.tensor_reduce(nm[:, :], mx[par][:, 8 * hf:8 * hf + 8, :], AX.X, ALU.max, negate=True))
                link(nc.vector.tensor_copy(nmp[pos][:, :, 0], nm[:, :]))
                nc.vector.tensor_tensor(nmp[pos][:, :, 1], nm[:, :], nmp[pos][:, :, 0], ALU.subtract)\
                    .then_inc(s["nm_made"], 1)

            def take_output(u, pos, k):
                hf = order[pos]
                dve.wait_ge(s["o_turned"], k + 1)
                tv = TB[:, 0:D].rearrange("p (c j r) -> p c j r", c=2, j=4)
                dve.wait_ge(s["ao_link"], 2 * k)
                link = chain(dve, s["ao_link"], 2 * k)
                link(nc.vector.reciprocal(rec[:, :, :], tv[:, :, :, HD]))
                b, h = u // H, u % H
                dst = V[:, :].rearrange("p (b k c) -> p b k c", b=B, k=KT)[
                    :, bass.ds(b, 1), 8 * hf:8 * hf + 8, bass.ds(h * HD, HD)].rearrange("p b (j c) d -> p c (b j) d", j=4)
                nc.vector.tensor_tensor(dst, tv[:, :, :, 0:HD], rec[:, :, :].unsqueeze(3).to_broadcast([P, 2, 4, HD]),
                                        ALU.mult).then_inc(s["ao_link"], 1)

            for x in range(shift, NS):
                for _, j, _ in max_part(-1, x, True):
                    reduce_chunk(0, 0, j)
            make_max(0, 0, 0, 0)

            def emit(u, par, prev, nxt):
                for x in range(NS):
                    for w, j, own in max_part(u, x, nxt):
                        reduce_chunk(w, par if own else 1 - par, j)
                    if x == shift - 1:
                        make_max(u, par, 1, 2 * u + 1)
                    if x == shift + z1 and nxt:
                        make_max(u + 1, 1 - par, 0, 2 * u + 2)
                    if x == O_PREV and prev:
                        take_output(u - 1, 1, 2 * u - 1)
                    if x == O_THIS:
                        take_output(u, 0, 2 * u)

            unit_loop(dve, emit)
            take_output(U - 1, 1, 2 * U - 1)


def combine(nc, tag, big, AO, sb, pb, sem):
    causal = tag == "A"
    w0 = 3 * D
    X = big["X"]
    with ExitStack() as st:
        aT = [sb(f"aT{tag}{i}", [P, KD, G], F32, st) for i in range(2)]
        stage = [sb(f"stage{tag}{i}", [P, GT, D], F32, st) for i in range(2)]
        TP = [pb(f"cT{tag}{i}", [P, G], st) for i in range(4)]
        PO = [pb(f"cO{tag}{i}", [P, G], st) for i in range(4)]
        staged, turned, aT_ready, out_ready, out_read, measured = (sem(f"{n}{tag}") for n in (
            "c_staged", "c_turned", "c_aT_ready", "c_out_ready", "c_out_read", "c_measured"))
        block = st.enter_context(nc.Block())

        def groups(eng):
            with eng.Fori(0, NG // 2) as i:
                for par in range(2):
                    yield par, 2 * i + par

        @block.gpsimd
        def _(pool):
            for par, g in groups(pool):
                pool.wait_ge(turned, KD * (g + 1))
                nc.gpsimd.tensor_copy(stage[par][:, :, :].rearrange("p t d -> p (t d)"),
                                      AO[:, bass.ds(g * GT * D, GT * D)]).then_inc(staged, 1)

        @block.tensor
        def _(pe):
            pe.sem_inc(turned, 2 * KD)
            pe.sem_inc(out_ready, 4)

            def turn(par, g):
                pe.wait_ge(staged, g + 1)
                pe.wait_ge(aT_ready, KD * (g + 1))
                for kk in range(KD):
                    for t in range(GT):
                        last = nc.tensor.transpose(TP[2 * par + kk][:, t * P:(t + 1) * P],
                                                   stage[par][:, t, kk * P:(kk + 1) * P], big["identF"][:, :])
                    last.then_inc(turned, 1)

            def project_out(par, g):
                pe.wait_ge(aT_ready, KD * (g + 1) + 2 * KD)
                for pair in range(2):
                    pe.wait_ge(out_read, 2 * g + pair + 1)
                    for t in (2 * pair, 2 * pair + 1):
                        for kk in range(KD):
                            last = nc.tensor.matmul(PO[2 * par + pair][:, (t % 2) * D:(t % 2 + 1) * D],
                                                    aT[par][:, kk, t * P:(t + 1) * P], big["WT"][:, kk, w0:w0 + D],
                                                    start=kk == 0, stop=kk == KD - 1)
                    last.then_inc(out_ready, 1)

            turn(0, 0)
            with pe.Fori(0, NG // 2 - 1) as i:
                for par in range(2):
                    turn(1 - par, 2 * i + par + 1)
                    project_out(par, 2 * i + par)
            turn(1, NG - 1)
            project_out(0, NG - 2)
            project_out(1, NG - 1)

        @block.scalar
        def _(act):
            act.sem_inc(aT_ready, 2 * KD)
            for par, g in groups(act):
                act.wait_ge(out_ready, 2 * (g + 1))
                for kk in range(KD):
                    act.wait_ge(turned, KD * g + kk + 1 + 2 * KD)
                    nc.scalar.copy(aT[par][:, kk, :], TP[2 * par + kk][:, :]).then_inc(aT_ready, 1)

        @block.vector
        def _(dve):
            dve.sem_inc(out_read, 4)
            for par, g in groups(dve):
                for pair in range(2):
                    dve.wait_ge(out_ready, 2 * g + pair + 1 + 4)
                    xs = X[:, bass.ds((g * GT + 2 * pair) * D, 2 * D)]
                    nc.vector.tensor_tensor(xs, PO[2 * par + pair][:, :], xs, ALU.add).then_inc(out_read, 1)
                dve.wait_ge(out_read, 2 * (g + 1) + 4)
                for t in range(GT):
                    last = nc.vector.bn_stats(big["stats"][:, bass.ds(g * GT + t, 1), :].rearrange("p a b -> p (a b)"),
                                              X[:, bass.ds((g * GT + t) * D, D)])
                last.then_inc(measured, 1)
            dve.wait_ge(measured, NG)
            for t in range(NT):
                nc.vector.bn_aggr(big["mv"][:, t, :], big["stats"][:, t, :])


def experts(nc, tag, big, scratch, sb, pb, sem, ffn_loaded, slots_zeroed):
    with ExitStack() as st:
        r = dict(
            xT=sb(f"xT_all{tag}", [P, KD, T], F32, st),
            XN=sb(f"XN_all{tag}", [P, NT, D], F32, st),
            wt=sb(f"wt{tag}", [P, NT, EX], F32, st),
            slot=[sb(f"slot{tag}{k}", [P, NT], mybir.dt.uint32, st) for k in range(TOP)],
            w=[sb(f"w{tag}{k}", [P, NT], F32, st) for k in range(TOP)],
            eid=sb(f"eid{tag}", [1, ST], mybir.dt.int32, st),
        )
        route(nc, tag, big, r, sb, pb, sem)
        apply_experts(nc, tag, big, scratch, r, sb, pb, sem, ffn_loaded, slots_zeroed)


def route(nc, tag, big, r, sb, pb, sem):
    X, XN, xT, wt = big["X"], r["XN"], r["xT"], r["wt"]
    with ExitStack() as st:
        lg = sb(f"flg{tag}", [P, NT, NE], F32, st)
        pr = sb(f"fpr{tag}", [P, NT, NE], F32, st)
        m1 = sb(f"fm1{tag}", [P, NT], F32, st)
        beats = sb(f"fbeats{tag}", [P, 2, NT, NE], F32, st)
        rank = sb(f"frank{tag}", [P, NT, NE], F32, st)
        chosen = sb(f"fchosen{tag}", [P, NT, NE], BF16, st)
        run = [sb(f"frun{tag}{i}", [P, NT, NE], F32, st) for i in range(2)]
        base = [sb(f"fbase{tag}{i}", [P, NE], F32, st) for i in range(2)]
        tiles_of = sb(f"ftiles{tag}", [P, NE], F32, st)
        edge = sb(f"fedge{tag}", [P, NT], F32, st)
        tile_no = sb(f"ftile_no{tag}", [1, ST], F32, st)
        over = sb(f"fover{tag}", [P, NE, NT], F32, st)
        reach = sb(f"freach{tag}", [1, ST, NE - 1], F32, st)
        TP = [pb(f"rTP{tag}{i}", [P, G], st) for i in range(4)]
        LP = pb(f"rLP{tag}", [P, G], st)
        PP = [pb(f"rPP{tag}{i}", [P, G], st) for i in range(2)]
        s = {n: sem(f"r_{n}{tag}") for n in (
            "root_done", "rstd_done", "xn_ready", "turned", "xT_ready", "lg_ready", "link", "ls_ready",
            "e_done", "chosen_ready", "prefix_ready", "numbers", "preset")}
        block = st.enter_context(nc.Block())

        @block.gpsimd
        def _(pool):
            pool.iota(edge[:, :], pattern=[[P, NT]], base=0, channel_multiplier=0,
                      allow_small_or_imprecise_dtypes=True).then_inc(s["numbers"], 1)
            pool.iota(tile_no[:, :], pattern=[[1, ST]], base=0, channel_multiplier=0,
                      allow_small_or_imprecise_dtypes=True).then_inc(s["numbers"], 1)

        @block.vector
        def _(dve):
            nc.vector.memset(wt[:, :, SH:], 1.0).then_inc(s["preset"], 1)
            dve.wait_ge(s["root_done"], 1)
            nc.vector.reciprocal(big["rstd"][:, :], big["std"][:, :]).then_inc(s["rstd_done"], 1)
            dve.wait_ge(s["rstd_done"], 1)
            with dve.Fori(0, NT) as t:
                nc.vector.tensor_scalar(XN[:, bass.ds(t, 1), :].rearrange("p t d -> p (t d)"), X[:, bass.ds(t * D, D)],
                                        big["mv"][:, bass.ds(t, 1), 0], big["rstd"][:, bass.ds(t, 1)],
                                        ALU.subtract, ALU.mult).then_inc(s["xn_ready"], 1)
            dve.wait_ge(s["lg_ready"], 1)
            dve.wait_ge(s["numbers"], 2)
            link = chain(dve, s["link"])

            def per_token(v):
                return v.unsqueeze(2).to_broadcast([P, NT, NE])

            link(nc.vector.tensor_tensor(lg[:, :, :], LP[:, 0:NT * NE].rearrange("p (t e) -> p t e", e=NE),
                                         big["rb"][:, :].unsqueeze(1).to_broadcast([P, NT, NE]), ALU.add))
            link(nc.vector.tensor_reduce(m1[:, :], lg[:, :, :], AX.X, ALU.max))
            nc.vector.tensor_tensor(lg[:, :, :], lg[:, :, :], per_token(m1[:, :]), ALU.subtract).then_inc(s["ls_ready"], 1)
            dve.wait_ge(s["e_done"], 1)
            link(nc.vector.tensor_reduce(m1[:, :], pr[:, :, :], AX.X, ALU.add))
            link(nc.vector.reciprocal(m1[:, :], m1[:, :]))
            link(nc.vector.tensor_tensor(pr[:, :, :], pr[:, :, :], per_token(m1[:, :]), ALU.mult))
            link(nc.vector.memset(rank[:, :, :], 0.0))
            for j in range(NE):
                bt = beats[:, j % 2, :, :]
                if j + 1 < NE:
                    last = nc.vector.tensor_tensor(bt[:, :, j + 1:], pr[:, :, j:j + 1].to_broadcast([P, NT, NE - 1 - j]),
                                                   pr[:, :, j + 1:], ALU.is_ge)
                if j > 0:
                    last = nc.vector.tensor_tensor(bt[:, :, 0:j], pr[:, :, j:j + 1].to_broadcast([P, NT, j]),
                                                   pr[:, :, 0:j], ALU.is_gt)
                link(last)
                if j + 1 < NE:
                    last = nc.vector.tensor_tensor(rank[:, :, j + 1:], rank[:, :, j + 1:], bt[:, :, j + 1:], ALU.add)
                if j > 0:
                    last = nc.vector.tensor_tensor(rank[:, :, 0:j], rank[:, :, 0:j], bt[:, :, 0:j], ALU.add)
                link(last)
            nc.vector.tensor_scalar(chosen[:, :, :], rank[:, :, :], float(TOP), None, ALU.is_lt).then_inc(s["chosen_ready"], 1)
            nc.vector.scalar_tensor_tensor(wt[:, :, 0:NE], rank[:, :, :], float(TOP), pr[:, :, :], ALU.is_lt, ALU.mult)\
                .then_inc(s["preset"], 1)
            dve.wait_ge(s["prefix_ready"], 2)
            link(nc.vector.tensor_copy(run[0][:, :, :], PP[1][:, 0:NT * NE].rearrange("p (t e) -> p t e", e=NE)))
            a, k = 0, 1
            while k < NT:
                nc.vector.tensor_copy(run[1 - a][:, 0:k, :], run[a][:, 0:k, :])
                link(nc.vector.tensor_tensor(run[1 - a][:, k:, :], run[a][:, k:, :], run[a][:, 0:NT - k, :], ALU.add))
                a, k = 1 - a, 2 * k
            link(nc.vector.tensor_tensor(over[:, :, :], run[a][:, NT - 1, :].unsqueeze(2).to_broadcast([P, NE, NT]),
                                         edge[:, :].unsqueeze(1).to_broadcast([P, NE, NT]), ALU.is_gt))
            link(nc.vector.tensor_reduce(tiles_of[:, :], over[:, :, :], AX.X, ALU.add))
            link(nc.vector.memset(base[0][:, 0:1], 0.0))
            link(nc.vector.tensor_copy(base[0][:, 1:], tiles_of[:, 0:NE - 1]))
            b, k = 0, 1
            while k < NE:
                nc.vector.tensor_copy(base[1 - b][:, 0:k], base[b][:, 0:k])
                link(nc.vector.tensor_tensor(base[1 - b][:, k:], base[b][:, k:], base[b][:, 0:NE - k], ALU.add))
                b, k = 1 - b, 2 * k
            link(nc.vector.tensor_tensor(run[a][:, :, :], run[a][:, :, :],
                                         PP[1][:, 0:NT * NE].rearrange("p (t e) -> p t e", e=NE), ALU.subtract))
            link(nc.vector.tensor_tensor(run[a][:, :, :], run[a][:, :, :],
                                         PP[0][:, 0:NT * NE].rearrange("p (t e) -> p t e", e=NE), ALU.add))
            link(nc.vector.tensor_scalar(base[1 - b][:, :], base[b][:, :], float(P), None, ALU.mult))
            link(nc.vector.tensor_tensor(run[a][:, :, :], run[a][:, :, :],
                                         base[1 - b][:, :].unsqueeze(1).to_broadcast([P, NT, NE]), ALU.add))
            for k in range(TOP):
                for src, dst in ((run[a], r["slot"][k]), (pr, r["w"][k])):
                    link(nc.vector.scalar_tensor_tensor(run[1 - a][:, :, :], rank[:, :, :], float(k), src[:, :, :],
                                                        ALU.is_equal, ALU.mult))
                    link(nc.vector.tensor_reduce(m1[:, :], run[1 - a][:, :, :], AX.X, ALU.add))
                    link(nc.vector.tensor_copy(dst[:, :], m1[:, :]))
            link(nc.vector.tensor_tensor(reach[:, :, :], tile_no[:, :].unsqueeze(2).to_broadcast([1, ST, NE - 1]),
                                         base[b][0:1, 1:].unsqueeze(1).to_broadcast([1, ST, NE - 1]), ALU.is_ge))
            link(nc.vector.tensor_reduce(tile_no[:, :], reach[:, :, :], AX.X, ALU.add))
            link(nc.vector.tensor_copy(r["eid"][:, :], tile_no[:, :]))

        @block.scalar
        def _(act):
            nc.scalar.activation(big["std"][:, :], big["mv"][:, :, 1], ACT.Sqrt, bias=big["eps"][:, :])\
                .then_inc(s["root_done"], 1)
            act.sem_inc(s["xT_ready"], 2 * KD)
            for g in range(NG):
                for kk in range(KD):
                    act.wait_ge(s["turned"], KD * g + kk + 1)
                    nc.scalar.copy(xT[:, kk, g * G:(g + 1) * G], TP[(g % 2) * KD + kk][:, :]).then_inc(s["xT_ready"], 1)
            act.wait_ge(s["ls_ready"], 1)
            nc.scalar.activation(pr[:, :, :], lg[:, :, :], ACT.Exp).then_inc(s["e_done"], 1)

        @block.tensor
        def _(pe):
            for g in range(NG + 1):
                if g < NG:
                    for kk in range(KD):
                        pe.wait_ge(s["xT_ready"], KD * g + kk + 1)
                        for t in range(GT):
                            if kk == 0:
                                pe.wait_ge(s["xn_ready"], GT * g + t + 1)
                            last = nc.tensor.transpose(TP[(g % 2) * KD + kk][:, t * P:(t + 1) * P],
                                                       XN[:, g * GT + t, kk * P:(kk + 1) * P], big["identF"][:, :])
                        last.then_inc(s["turned"], 1)
                if g:
                    pe.wait_ge(s["xT_ready"], KD * g + 2 * KD)
                    for t in range((g - 1) * GT, g * GT):
                        for kk in range(KD):
                            last = nc.tensor.matmul(LP[:, t * NE:(t + 1) * NE], xT[:, kk, t * P:(t + 1) * P],
                                                    big["rw"][:, kk, :], start=kk == 0, stop=kk == KD - 1)
            last.then_inc(s["lg_ready"], 1)
            pe.wait_ge(s["chosen_ready"], 1)
            flat = chosen[:, :, :].rearrange("p t e -> p (t e)")
            for j, m in enumerate(("before", "all1")):
                nc.tensor.matmul(PP[j][:, 0:NT * NE], big[m][:, :], flat, start=True, stop=True)\
                    .then_inc(s["prefix_ready"], 1)


def apply_experts(nc, tag, big, scratch, r, sb, pb, sem, ffn_loaded, slots_zeroed):
    X, XN, xT, wt = big["X"], r["XN"], r["xT"], r["wt"]
    again = tag == "A"
    HALVES = (range(0, NG // 2), range(NG // 2, NG))
    TURN = 4
    YG = 4
    with ExitStack() as st:
        flat = XN[:, :, :].rearrange("p t d -> p (t d)")
        at = [0]

        def carve(shape):
            n = 1
            for x in shape:
                n *= x
            v = flat[:, at[0]:at[0] + n]
            at[0] += n
            return v.rearrange("p (a b) -> p a b", b=shape[1]) if len(shape) == 2 else v

        xg = [carve([D]) for _ in range(4)]
        xgT = [carve([KD, P]) for _ in range(2)]
        hs = [carve([HID]) for _ in range(2)]
        hT = [carve([HT, P]) for _ in range(2)]
        ys = [carve([D]) for _ in range(2)]
        yg = [[carve([D]) for _ in range(TOP)] for _ in range(YG)]
        hTs = [sb(f"hTs{tag}{i}", [P, HT, G], F32, st) for i in range(2)]
        wT = sb(f"fwT{tag}", [EX, G], F32, st)
        TX = [pb(f"eTX{tag}{i}", [P, G], st) for i in range(2)]
        UP = [pb(f"eUP{tag}{i}", [P, G], st) for i in range(2)]
        HP = pb(f"eHP{tag}", [P, G], st)
        YP = [pb(f"eYP{tag}{i}", [P, G], st) for i in range(2)]
        WP = pb(f"eWP{tag}", [P, G], st)
        s = {n: sem(f"e_{n}{tag}") for n in (
            "scattered", "sh_ready", "sh_gelu", "wT_turned", "wT_ready", "sh_y", "sh_added", "x_turned", "xgT_ready",
            "up_done", "hs_ready", "h_turned", "hT_ready", "y_done", "ys_ready", "combined", "mix", "measured")}
        xg_in = [sem(f"e_xg_in{tag}{i}") for i in range(4)]
        stored = [sem(f"e_stored{tag}{i}") for i in range(2)]
        gathered = [sem(f"e_gathered{tag}{i}") for i in range(YG)]
        block = st.enter_context(nc.Block())

        def tile_loop(eng, emit, tail):
            with eng.Fori(0, ST // TURN - tail) as j:
                for k in range(TURN):
                    emit(TURN * j + k, k)
            for i in range(ST - TURN * tail, ST):
                emit(i, i % TURN)

        @block.gpsimd
        def _(pool):
            pool.wait_ge(slots_zeroed, 16 * 8)
            for t in range(NT):
                for k in range(TOP):
                    nc.gpsimd.indirect_dma_start(
                        scratch["slots_in"][:, :], bass.IndirectOffsetOnAxis(ap=r["slot"][k][:, t:t + 1], axis=0),
                        XN[:, t, :], None).then_inc(s["scattered"], 16)
            for par in range(2):
                pool.wait_ge(stored[par], 16 * (ST // 2 + 1))
            for t in range(NT):
                if t >= YG:
                    pool.wait_ge(s["combined"], t - YG + 1)
                for k in range(TOP):
                    nc.gpsimd.indirect_dma_start(
                        yg[t % YG][k], None, scratch["slots_out"][:, :],
                        bass.IndirectOffsetOnAxis(ap=r["slot"][k][:, t:t + 1], axis=0)).then_inc(gathered[t % YG], 16)

        @block.sync
        def _(sp):
            for par in range(2):
                sp.sem_inc(stored[par], 16)
            sp.wait_ge(s["scattered"], 16 * TOP * NT)

            def load(i, k):
                sp.wait_ge(s["x_turned"], i + 1)
                sp.dma_start(xg[k % 4], scratch["slots_in"][bass.ds(i * P, P), :]).then_inc(xg_in[k % 4], 16)

            def emit(i, k, more=True):
                if not (isinstance(i, int) and i + 4 >= ST):
                    load(i + 4, k)
                sp.wait_ge(s["ys_ready"], i + 1 + 2)
                sp.dma_start(scratch["slots_out"][bass.ds(i * P, P), :], ys[k % 2]).then_inc(stored[k % 2], 16)

            for i in range(4):
                load(i, i)
            tile_loop(sp, emit, 1)
            for par in range(2):
                sp.wait_ge(stored[par], 16 * (ST // 2 + 1))

        @block.tensor
        def _(pe):
            pe.sem_inc(s["x_turned"], 4)
            pe.sem_inc(s["up_done"], 2)
            pe.sem_inc(s["h_turned"], 2)
            pe.sem_inc(s["y_done"], 2)
            pe.wait_ge(ffn_loaded, 16 * 2 * EX)

            def shared_up(g):
                for m in range(HT):
                    k = g * HT + m
                    if k >= 2:
                        pe.wait_ge(s["sh_gelu"], k - 1)
                    for kk in range(KD):
                        last = nc.tensor.matmul(UP[k % 2][:, :], big["w1"][:, SH, kk, m * P:(m + 1) * P],
                                                xT[:, kk, g * G:(g + 1) * G], start=kk == 0, stop=kk == KD - 1)
                    last.then_inc(s["sh_ready"], 1)

            def shared_down(g):
                if g:
                    pe.wait_ge(s["wT_ready"], g)
                for t in range(GT):
                    last = nc.tensor.transpose(WP[0:EX, t * P:(t + 1) * P], wt[:, g * GT + t, :], big["identF"][:, :])
                last.then_inc(s["wT_turned"], 1)
                pe.wait_ge(s["wT_ready"], g + 1)
                pe.wait_ge(s["sh_gelu"], (g + 1) * HT)
                for t in range(GT):
                    k = g * GT + t
                    if k >= 2:
                        pe.wait_ge(s["sh_added"], k - 1)
                    nc.tensor.matmul(YP[k % 2][:, 0:D], wT[:, t * P:(t + 1) * P], big["b2"][:, :], start=True, stop=False)
                    for m in range(HT):
                        last = nc.tensor.matmul(YP[k % 2][:, 0:D], hTs[g % 2][:, m, t * P:(t + 1) * P],
                                                big["w2"][:, SH, m, :], start=False, stop=m == HT - 1)
                    last.then_inc(s["sh_y"], 1)

            def shared(groups):
                shared_up(groups[0])
                for g in groups:
                    if g + 1 in groups:
                        shared_up(g + 1)
                    shared_down(g)

            def turn_x(i, k):
                pe.wait_ge(xg_in[k % 4], 16 * (i // 4 + 1))
                pe.wait_ge(s["xgT_ready"], i + 1)
                for kk in range(KD):
                    last = nc.tensor.transpose(TX[k % 2][:, kk * P:(kk + 1) * P], xg[k % 4][:, kk * P:(kk + 1) * P],
                                               big["identF"][:, :])
                last.then_inc(s["x_turned"], 1)

            def up(i, k):
                e = pe.value_load(r["eid"][0:1, bass.ds(i, 1)], min_val=0, max_val=NE - 1)
                pe.wait_ge(s["xgT_ready"], i + 1 + 2)
                pe.wait_ge(s["hs_ready"], i + 1)
                w = big["w1"][:, bass.ds(e, 1), :, :].rearrange("p e k h -> p (e k) h")
                for kk in range(KD):
                    last = nc.tensor.matmul(UP[k % 2][:, :], xgT[k % 2][:, kk, :], w[:, kk, :], start=kk == 0,
                                            stop=kk == KD - 1)
                last.then_inc(s["up_done"], 1)

            def turn_h(i, k):
                pe.wait_ge(s["hs_ready"], i + 1 + 2)
                pe.wait_ge(s["hT_ready"], i + 1)
                for m in range(HT):
                    last = nc.tensor.transpose(HP[:, m * P:(m + 1) * P], hs[k % 2][:, m * P:(m + 1) * P],
                                               big["identF"][:, :])
                last.then_inc(s["h_turned"], 1)

            def down(i, k):
                e = pe.value_load(r["eid"][0:1, bass.ds(i, 1)], min_val=0, max_val=NE - 1)
                pe.wait_ge(s["hT_ready"], i + 1 + 1)
                pe.wait_ge(s["ys_ready"], i + 1)
                w = big["w2"][:, bass.ds(e, 1), :, :].rearrange("p e k d -> p (e k) d")
                for m in range(HT):
                    last = nc.tensor.matmul(YP[k % 2][:, 0:D], hT[k % 2][:, m, :], w[:, m, :], start=m == 0,
                                            stop=m == HT - 1)
                last.then_inc(s["y_done"], 1)

            shared(HALVES[0])
            pe.wait_ge(s["sh_added"], len(HALVES[0]) * GT)
            turn_x(0, 0)
            turn_x(1, 1)
            up(0, 0)
            turn_h(0, 0)

            def emit(i, k):
                static = isinstance(i, int)
                if not static or i + 2 < ST:
                    turn_x(i + 2, k + 2)
                if not static or i + 1 < ST:
                    up(i + 1, k + 1)
                down(i, k)
                if not static or i + 1 < ST:
                    turn_h(i + 1, k + 1)

            tile_loop(pe, emit, 1)
            pe.wait_ge(s["ys_ready"], ST + 2)
            shared(HALVES[1])

        @block.scalar
        def _(act):
            act.sem_inc(s["xgT_ready"], 2)
            act.sem_inc(s["hT_ready"], 1)

            def shared(groups):
                for g in groups:
                    for m in range(HT):
                        act.wait_ge(s["sh_ready"], g * HT + m + 1)
                        if m == 0 and g >= 2:
                            act.wait_ge(s["sh_y"], (g - 1) * GT)
                        nc.scalar.activation(hTs[g % 2][:, m, :], UP[(g * HT + m) % 2][:, :], ACT.Gelu,
                                             bias=big["b1"][:, SH, m:m + 1]).then_inc(s["sh_gelu"], 1)

            def copy_x(i, k):
                act.wait_ge(s["x_turned"], i + 1 + 4)
                act.wait_ge(s["up_done"], i + 1)
                nc.scalar.copy(xgT[k % 2].rearrange("p a b -> p (a b)"), TX[k % 2][:, 0:D]).then_inc(s["xgT_ready"], 1)

            def gelus(i, k):
                e = act.value_load(r["eid"][0:1, bass.ds(i, 1)], min_val=0, max_val=NE - 1)
                act.wait_ge(s["h_turned"], i + 1 + 2)
                act.wait_ge(s["y_done"], i + 1)
                for m in range(HT):
                    last = nc.scalar.activation(hT[k % 2][:, m, :], HP[:, m * P:(m + 1) * P], ACT.Gelu,
                                                bias=big["b1"][:, bass.ds(e, 1), m:m + 1].rearrange("p a b -> p (a b)"))
                last.then_inc(s["hT_ready"], 1)

            shared(HALVES[0])
            copy_x(0, 0)
            copy_x(1, 1)

            def emit(i, k):
                gelus(i, k)
                if not isinstance(i, int) or i + 2 < ST:
                    copy_x(i + 2, k + 2)

            tile_loop(act, emit, 1)
            shared(HALVES[1])

        @block.vector
        def _(dve):
            dve.sem_inc(s["hs_ready"], 2)
            dve.sem_inc(s["ys_ready"], 2)

            def shared(g):
                dve.wait_ge(s["wT_turned"], g + 1)
                if g:
                    dve.wait_ge(s["sh_y"], g * GT)
                nc.vector.tensor_copy(wT[:, :], WP[0:EX, :]).then_inc(s["wT_ready"], 1)
                for t in range(GT):
                    k = g * GT + t
                    dve.wait_ge(s["sh_y"], k + 1)
                    xs = X[:, k * D:(k + 1) * D]
                    nc.vector.tensor_tensor(xs, YP[k % 2][:, 0:D], xs, ALU.add).then_inc(s["sh_added"], 1)

            def combine_tile(t):
                dve.wait_ge(gathered[t % YG], 16 * TOP * (t // YG + 1))
                xs = X[:, t * D:(t + 1) * D]
                nc.vector.scalar_tensor_tensor(xs, yg[t % YG][0], r["w"][0][:, t:t + 1], xs, ALU.mult, ALU.add)\
                    .then_inc(s["mix"], 1)
                dve.wait_ge(s["mix"], t + 1)
                nc.vector.scalar_tensor_tensor(xs, yg[t % YG][1], r["w"][1][:, t:t + 1], xs, ALU.mult, ALU.add)\
                    .then_inc(s["combined"], 1)

            def copy_h(i, k):
                dve.wait_ge(s["up_done"], i + 1 + 2)
                dve.wait_ge(s["h_turned"], i + 1)
                nc.vector.tensor_copy(hs[k % 2], UP[k % 2][:, :]).then_inc(s["hs_ready"], 1)

            def copy_y(i, k):
                dve.wait_ge(s["y_done"], i + 1 + 2)
                dve.wait_ge(stored[k % 2], 16 * (i // 2 + 1))
                nc.vector.tensor_copy(ys[k % 2], YP[k % 2][:, 0:D]).then_inc(s["ys_ready"], 1)

            for g in HALVES[0]:
                shared(g)
            copy_h(0, 0)

            def emit(i, k):
                if not isinstance(i, int) or i + 1 < ST:
                    copy_h(i + 1, k + 1)
                copy_y(i, k)

            tile_loop(dve, emit, 1)
            done = 0
            for q, g in enumerate(HALVES[1]):
                shared(g)
                for t in range(done, 5 * q):
                    dve.wait_ge(s["sh_added"], g * GT + GT)
                    combine_tile(t)
                done = max(done, 5 * q)
            dve.wait_ge(s["sh_added"], NT)
            for t in range(done, NT):
                combine_tile(t)
                if again and t % GT == GT - 1:
                    dve.wait_ge(s["combined"], t + 1)
                    first = 0 if t < done + GT else t - GT + 1
                    token_stats(nc, dve, big, range(first, t + 1), s["measured"], first)


def finish(nc, out, big, sem):
    written = sem("written")
    with nc.Block() as block:
        @block.sync
        def _(sp):
            view = out.rearrange("b (t p) d -> p (b t) d", p=P)
            X3 = big["X"][:, :].rearrange("p (t d) -> p t d", d=D)
            for g in range(NG):
                sp.dma_start(view[:, g * GT:(g + 1) * GT, :], X3[:, g * GT:(g + 1) * GT, :]).then_inc(written, 16)
            sp.wait_ge(written, 16 * NG)


NAMES = """L0_attn_a_hidden_states L0_attn_a_c_attn_kernel L0_attn_a_c_attn_bias L0_attn_a_c_proj_kernel
L0_attn_a_c_proj_bias L0_attn_b_Wq L0_attn_b_bq L0_attn_b_Wk L0_attn_b_bk L0_attn_b_Wv L0_attn_b_bv L0_attn_b_Wo
L0_attn_b_bo L0_attn_b_Wqs L0_attn_b_bqs L0_attn_b_Wks L0_attn_b_bks L0_attn_b_Wvs L0_attn_b_bvs L0_attn_b_temp
L0_ffn_router_w L0_ffn_router_b L0_ffn_sw1 L0_ffn_sb1 L0_ffn_sw2 L0_ffn_sb2 L0_ffn_rw1 L0_ffn_rb1 L0_ffn_rw2
L0_ffn_rb2""".split()


def kernel(**inputs):
    import numpy as np
    import concourse.bacc as bacc
    from concourse.bass_utils import run_bass_kernel_spmd

    nc = bacc.Bacc("TRN2", target_bir_lowering=False, num_devices=1)
    arrays, io = {}, {}
    for name in NAMES:
        a = np.ascontiguousarray(inputs[name])
        if a.ndim == 0:
            a = a.reshape(1)
        arrays[name] = a
        io[name] = nc.dram_tensor(name, a.shape, mybir.dt.from_np(a.dtype), kind="ExternalInput").ap()
    out = nc.dram_tensor("out", (B, S, D), F32, kind="ExternalOutput").ap()
    build(nc, io, out)
    r = run_bass_kernel_spmd(nc, [arrays], core_ids=[0])
    return r.results[0]["out"]
```

```python
from contextlib import ExitStack

import concourse.bass as bass
from concourse import mybir

F32 = mybir.dt.float32
BF16 = mybir.dt.bfloat16
ALU = mybir.AluOpType
ACT = mybir.ActivationFunctionType
AX = mybir.AxisListType

P = 128
B, S, D = 2, 2048, 256
T = B * S
NT = T // P
H, HD = 16, 16
U = B * H
KT = S // P
KD = D // P
G = 512
NG = T // G
GT = G // P
NE, HID = 8, 512
EX = NE + 1
SH = NE
HT = HID // P
TOP = 2
ST = TOP * NT + NE
TURNS = (U - 2) // 2
ZT = -(-ST // TURNS)
SLOTS = ZT * TURNS * P
C3 = 3
XR = H * C3
EPS = 1e-5
NEG = -1e30
LOWEST = -3e38

Q_RUNS = [(0, 1, 3), (1, 1, 2), (2, 1, 1)]
K_RUNS = [(0, 3, 1), (0, 2, 1), (0, 1, 1)]


def build(nc, io, out):
    ctx = ExitStack()
    with ctx:
        def sb(name, shape, dt=F32, at=ctx):
            return at.enter_context(nc.sbuf_tensor(name, shape, dt))

        def pb(name, shape, at, dt=F32):
            return at.enter_context(nc.psum_tensor(name, shape, dt))

        phase_sems = []

        def sem(name, keep=False):
            handle = nc.alloc_semaphore(name)
            if not keep:
                phase_sems.append(handle)
            return handle

        def clear_sems():
            nc.clear_and_free_semaphores(phase_sems)
            nc.all_engine_barrier()
            phase_sems.clear()

        scratch = {}
        for side in "qk":
            scratch[side] = nc.dram_tensor(f"{side}_pieces", [B, 3, D, S], BF16, kind="Internal").ap()
            scratch[side + "x"] = nc.dram_tensor(f"{side}x_pieces", [B, 3, XR, S], BF16, kind="Internal").ap()

        turned_w = nc.dram_tensor("turned_w", [2, P, KD, 4 * D], F32, kind="Internal").ap()
        slots_in = nc.dram_tensor("slots_in", [SLOTS, D], F32, kind="Internal").ap()
        slots_out = nc.dram_tensor("slots_out", [ST * P, D], F32, kind="Internal").ap()
        scratch.update(w=turned_w, slots_in=slots_in, slots_out=slots_out)

        big = dict(
            X=sb("X", [P, NT * D]),
            w1=sb("w1", [P, EX, KD, HID]),
            w2=sb("w2", [P, EX, HT, D]),
            b1=sb("b1", [P, EX, HT]),
            b2=sb("b2", [EX, D]),
            rw=sb("rw", [P, KD, 32]),
            rb=sb("rb", [P, NE]),
            bcolA=sb("bcolA", [P, 6]),
            bcolB=sb("bcolB", [P, 6]),
            scolA=sb("scolA", [P, 1]),
            scolB=sb("scolB", [P, 1]),
            vbA=sb("vbA", [P, D]), vbB=sb("vbB", [P, D]),
            obA=sb("obA", [P, D]), obB=sb("obB", [P, D]),
            XW=sb("XW", [P, KD, 5, XR]),
            xb=sb("xb", [P, 3]),
            identF=sb("identF", [P, P]),
            identB=sb("identB", [P, P], BF16),
            maskK=sb("maskK", [P, P], BF16),
            maskQ=sb("maskQ", [P, P], BF16),
            before=sb("before", [P, P], BF16),
            all1=sb("all1", [P, P], BF16),
            stats=sb("stats", [P, NT, 6]),
            mv=sb("mv", [P, NT, 2]), std=sb("std", [P, NT]), rstd=sb("rstd", [P, NT]),
            zeros=sb("zeros", [P, D]),
            eps=sb("eps", [P, 1]),
        )
        ffn_loaded = sem("ffn_loaded", keep=True)
        slots_zeroed = sem("slots_zeroed", keep=True)
        setup(nc, io, big, scratch, sb, pb, sem)

        w1_blocks = big["w1"][:, 0:NE, :, :].rearrange("p e k h -> p (e k) h")
        w2_blocks = big["w2"][:, 0:NE, :, :].rearrange("p e k d -> p (e k) d")
        w1_given = io["L0_ffn_rw1"].rearrange("e (k p) h -> p (e k) h", p=P)
        w2_given = io["L0_ffn_rw2"].rearrange("e (k p) d -> p (e k) d", p=P)
        assert NE * KD == TURNS + 1 and NE * HT == 2 * (TURNS + 1)

        def load_blocks(sp, n):
            sp.dma_start(w1_blocks[:, bass.ds(n, 1), :], w1_given[:, bass.ds(n, 1), :]).then_inc(ffn_loaded, 16)
            sp.dma_start(w2_blocks[:, bass.ds(2 * n, 2), :], w2_given[:, bass.ds(2 * n, 2), :]).then_inc(ffn_loaded, 16)

        def side_loads(sp, turn):
            if turn is None:
                sp.dma_start(big["w1"][:, SH, :, :], io["L0_ffn_sw1"].rearrange("(k p) h -> p k h", p=P))\
                    .then_inc(ffn_loaded, 16)
                sp.dma_start(big["w2"][:, SH, :, :], io["L0_ffn_sw2"].rearrange("(k p) d -> p k d", p=P))\
                    .then_inc(ffn_loaded, 16)
                load_blocks(sp, 0)
            else:
                load_blocks(sp, turn + 1)
                sp.dma_start(slots_in[bass.ds(turn * (ZT * P), ZT * P), :].rearrange("(a p) d -> p a d", p=P),
                             big["zeros"][:, :].unsqueeze(1).to_broadcast([P, ZT, D])).then_inc(slots_zeroed, 16)

        attention(nc, "A", True, big, scratch, sb, pb, sem, side_loads)
        experts(nc, "A", big, scratch, None, sb, pb, sem, ffn_loaded, slots_zeroed)
        clear_sems()
        attention(nc, "B", False, big, scratch, sb, pb, sem, None)
        experts(nc, "B", big, scratch, out, sb, pb, sem, ffn_loaded, slots_zeroed)


def chain(eng, sem, base=0):
    n = [0]

    def link(ins):
        n[0] += 1
        ins.then_inc(sem, 1)
        eng.wait_ge(sem, base + n[0])
    link.count = n
    return link


def setup(nc, io, big, scratch, sb, pb, sem):
    with ExitStack() as st:
        natural = sb("natural", [P, 16, D], F32, st)
        WT = sb("WT", [P, KD, 8 * D], F32, st)
        wcol = sb("wcol", [P, 3, C3], F32, st)
        blockdiag = sb("blockdiag", [P, 5, 2, H, C3], F32, st)
        xb_in = sb("xb_in", [P, 3], F32, st)
        banks = [pb(f"setup_ps{i}", [P, 512], st) for i in range(8)]
        X = big["X"]
        x_loaded, w_loaded, small_loaded, cols_loaded = (sem(n) for n in (
            "x_loaded", "w_loaded", "small_loaded", "cols_loaded"))
        ident_made, masks_made, bd_link = sem("ident_made"), sem("masks_made"), sem("bd_link")
        turned, turned_out, comp_done, comp_out = sem("turned"), sem("turned_out"), sem("comp_done"), sem("comp_out")
        zeroed, router_zeroed, kept, measured = (sem(n) for n in ("zeroed", "router_zeroed", "kept", "measured"))
        block = st.enter_context(nc.Block())
        sets = [(0, 0), (1, 1), (1, 2), (2, 2), (2, 1)]
        small = []

        x_view = io["L0_attn_a_hidden_states"].rearrange("b (t p) d -> p (b t) d", p=P)
        X3 = X[:, :].rearrange("p (t d) -> p t d", d=D)

        @block.scalar
        def _(act):
            def load(dst, src):
                act.dma_start(dst, src, allow_slow_non_contiguous=True).then_inc(small_loaded, 16)
                small.append(1)
            load(big["bcolA"][:, :], io["L0_attn_a_c_attn_bias"].rearrange("(m p) -> p m", p=P))
            for i, n in enumerate(("L0_attn_b_bq", "L0_attn_b_bk", "L0_attn_b_bv")):
                load(big["bcolB"][:, 2 * i:2 * i + 2], io[n].rearrange("(m p) -> p m", p=P))
            load(big["scolB"][:, :], io["L0_attn_b_temp"].partition_broadcast(P))
            load(big["vbA"][:, :], io["L0_attn_a_c_attn_bias"][2 * D:3 * D].partition_broadcast(P))
            load(big["obA"][:, :], io["L0_attn_a_c_proj_bias"].partition_broadcast(P))
            load(big["vbB"][:, :], io["L0_attn_b_bv"].partition_broadcast(P))
            load(big["obB"][:, :], io["L0_attn_b_bo"].partition_broadcast(P))
            load(big["rb"][:, :], io["L0_ffn_router_b"].partition_broadcast(P))
            act.wait_ge(router_zeroed, 1)
            load(big["rw"][:, :, 0:NE], io["L0_ffn_router_w"].rearrange("(k p) e -> p k e", p=P))
            load(big["b1"][:, 0:NE, :], io["L0_ffn_rb1"].rearrange("e (m p) -> p e m", p=P))
            load(big["b1"][:, SH, :], io["L0_ffn_sb1"].rearrange("(m p) -> p m", p=P))
            load(big["b2"][0:NE, :], io["L0_ffn_rb2"])
            load(big["b2"][SH:SH + 1, :], io["L0_ffn_sb2"].rearrange("(a d) -> a d", a=1))
            for (src, rot), (row, col) in zip(sets, [(0, 0), (0, 1), (64, 1), (0, 2), (64, 2)]):
                b = io[("L0_attn_b_bqs", "L0_attn_b_bks", "L0_attn_b_bvs")[src]]
                for c in range(C3):
                    f = (c + rot) % C3
                    load(xb_in[row + c:row + c + 3 * (H - 1) + 1:3, col:col + 1],
                         b[f:f + 1].partition_broadcast(H))

        @block.sync
        def _(sp):
            names = [("L0_attn_a_c_attn_kernel", 0, 6), ("L0_attn_a_c_proj_kernel", 6, 2), ("L0_attn_b_Wq", 8, 2),
                     ("L0_attn_b_Wk", 10, 2), ("L0_attn_b_Wv", 12, 2), ("L0_attn_b_Wo", 14, 2)]
            for name, at, n in names:
                sp.dma_start(natural[:, at:at + n, :], io[name].rearrange("(m p) d -> p m d", p=P)).then_inc(w_loaded, 16)
            for i, n in enumerate(("L0_attn_b_Wqs", "L0_attn_b_Wks", "L0_attn_b_Wvs")):
                for c in range(C3):
                    sp.dma_start(wcol[:, i, c:c + 1], io[n][c:c + 1, :].to_broadcast([P // HD, HD]),
                                 allow_slow_non_contiguous=True).then_inc(cols_loaded, 16)
            for g in range(NG):
                sp.dma_start(X3[:, g * GT:(g + 1) * GT, :], x_view[:, g * GT:(g + 1) * GT, :]).then_inc(x_loaded, 16)
            sp.wait_ge(turned_out, 8)
            for layer in range(2):
                sp.dma_start(scratch["w"][layer], WT[:, :, layer * 4 * D:(layer + 1) * 4 * D]).then_inc(kept, 16)
            sp.wait_ge(kept, 32)
            sp.wait_ge(x_loaded, 16 * NG)

        @block.gpsimd
        def _(pool):
            pool.memset(big["rw"][:, :, :], 0.0).then_inc(router_zeroed, 1)
            pool.memset(big["identF"][:, :], 0.0).then_inc(zeroed, 1)
            pool.memset(big["identB"][:, :], 0.0).then_inc(zeroed, 1)
            pool.memset(big["maskK"][:, :], 0.0).then_inc(zeroed, 1)
            pool.memset(big["maskQ"][:, :], 0.0).then_inc(zeroed, 1)
            pool.memset(big["scolA"][:, :], HD ** -0.5).then_inc(zeroed, 1)
            pool.memset(big["eps"][:, :], EPS).then_inc(zeroed, 1)
            pool.memset(big["zeros"][:, :], 0.0).then_inc(zeroed, 1)
            pool.memset(big["before"][:, :], 0.0).then_inc(zeroed, 1)
            pool.memset(big["all1"][:, :], 1.0).then_inc(zeroed, 1)
            pool.wait_ge(zeroed, 9)
            pool.affine_select(out=big["before"][:, :], in_=big["before"][:, :], compare_op=ALU.is_ge, fill=1.0, base=0,
                               pattern=[[-1, P]], channel_multiplier=1).then_inc(masks_made, 1)
            for m in ("identF", "identB"):
                pool.affine_select(out=big[m][:, :], in_=big[m][:, :], compare_op=ALU.not_equal, fill=1.0, base=0,
                                   pattern=[[-1, P]], channel_multiplier=1).then_inc(ident_made, 1)
            pool.affine_select(out=big["maskK"][:, :], in_=big["maskK"][:, :], compare_op=ALU.is_ge, fill=NEG, base=0,
                               pattern=[[1, P]], channel_multiplier=-1).then_inc(masks_made, 1)
            pool.affine_select(out=big["maskQ"][:, :], in_=big["maskQ"][:, :], compare_op=ALU.is_ge, fill=NEG, base=0,
                               pattern=[[-1, P]], channel_multiplier=1).then_inc(masks_made, 1)
            pool.wait_ge(cols_loaded, 16 * 3 * C3)
            for s, (src, rot) in enumerate(sets):
                for c in range(C3):
                    f = (c + rot) % C3
                    pool.tensor_copy(blockdiag[:, s, :, :, c],
                                     wcol[:, src, f:f + 1].unsqueeze(2).to_broadcast([P, 2, H])).then_inc(bd_link, 1)
            n = 15
            pool.wait_ge(bd_link, n)
            pool.affine_select(out=blockdiag[:, :, :, :, :], in_=blockdiag[:, :, :, :, :], compare_op=ALU.is_ge,
                               fill=0.0, base=0, pattern=[[0, 5], [P, 2], [-HD, H], [0, C3]],
                               channel_multiplier=1).then_inc(bd_link, 1)
            pool.wait_ge(bd_link, n + 1)
            pool.affine_select(out=blockdiag[:, :, :, :, :], in_=blockdiag[:, :, :, :, :], compare_op=ALU.is_ge,
                               fill=0.0, base=HD - 1, pattern=[[0, 5], [-P, 2], [HD, H], [0, C3]],
                               channel_multiplier=-1).then_inc(bd_link, 1)

        @block.tensor
        def _(pe):
            pe.wait_ge(ident_made, 1)
            pe.wait_ge(w_loaded, 16 * 6)
            for n in range(8):
                kk, m0 = n // 4, 4 * (n % 4)
                if n >= 4:
                    pe.wait_ge(turned_out, n - 3)
                for j in range(4):
                    last = nc.tensor.transpose(banks[n % 4][:, j * P:(j + 1) * P],
                                               natural[:, m0 + j, kk * P:(kk + 1) * P], big["identF"][:, :])
                last.then_inc(turned, 1)
            pe.wait_ge(bd_link, 17)
            for kk in range(KD):
                for s, (src, _rot) in enumerate(sets):
                    at = (kk * 5 + s) * XR
                    for half in range(2):
                        last = nc.tensor.matmul(banks[4][:, at:at + XR],
                                                natural[:, 8 + 2 * src + half, kk * P:(kk + 1) * P],
                                                blockdiag[:, s, half, :, :].rearrange("p h c -> p (h c)"),
                                                start=half == 0, stop=half == 1)
            last.then_inc(comp_done, 1)
            pe.wait_ge(small_loaded, 16 * len(small))
            for (s, (src, _rot)), (row, col) in zip(enumerate(sets), [(0, 0), (0, 1), (64, 1), (0, 2), (64, 2)]):
                for half in range(2):
                    last = nc.tensor.matmul(banks[5][row:row + XR, col:col + 1],
                                            blockdiag[:, s, half, :, :].rearrange("p h c -> p (h c)"),
                                            big["bcolB"][:, 2 * src + half:2 * src + half + 1],
                                            start=half == 0, stop=half == 1)
            last.then_inc(comp_done, 1)

        @block.vector
        def _(dve):
            for n in range(8):
                dve.wait_ge(turned, n + 1)
                kk, m0 = n // 4, 4 * (n % 4)
                nc.vector.tensor_copy(WT[:, kk, m0 * P:(m0 + 4) * P], banks[n % 4][:, :]).then_inc(turned_out, 1)
            dve.wait_ge(x_loaded, 16 * NG)
            token_stats(nc, dve, big, measured)
            dve.wait_ge(comp_done, 1)
            nc.vector.tensor_copy(big["XW"][:, :, :, :].rearrange("p k s r -> p (k s r)"),
                                  banks[4][:, 0:10 * XR]).then_inc(comp_out, 1)
            dve.wait_ge(comp_done, 2)
            dve.wait_ge(small_loaded, 16 * len(small))
            for row, cols in ((0, slice(0, 3)), (64, slice(1, 3))):
                nc.vector.tensor_tensor(big["xb"][row:row + XR, cols], banks[5][row:row + XR, cols],
                                        xb_in[row:row + XR, cols], ALU.add).then_inc(comp_out, 1)


def token_stats(nc, dve, big, measured):
    for t in range(NT):
        nc.vector.bn_stats(big["stats"][:, t, :], big["X"][:, t * D:(t + 1) * D]).then_inc(measured, 1)
    dve.wait_ge(measured, NT)
    for t in range(NT):
        nc.vector.bn_aggr(big["mv"][:, t, :], big["stats"][:, t, :])


def attention(nc, tag, causal, big, scratch, sb, pb, sem, side_loads):
    with ExitStack() as st:
        big["WT"] = sb(f"WT{tag}", [P, KD, 4 * D], F32, st)
        V = sb(f"V{tag}", [P, NT * D], F32, st)
        project(nc, tag, causal, big, scratch, V, sb, pb, sem)
        units(nc, tag, causal, big, scratch, V, sb, pb, sem, side_loads)
        combine(nc, tag, big, V, sb, pb, sem)


def project(nc, tag, causal, big, scratch, V, sb, pb, sem):
    extra = not causal
    NI = 6 if extra else 4
    NPC = 4
    NPQ = 5 if extra else 4
    bcol = big["bcolA"] if causal else big["bcolB"]
    scol = big["scolA"] if causal else big["scolB"]
    vb = big["vbA"] if causal else big["vbB"]
    X = big["X"]
    with ExitStack() as st:
        XN = [sb(f"XN{tag}{i}", [P, GT, D], F32, st) for i in range(2)]
        xT = [sb(f"xT{tag}{i}", [P, KD, G], F32, st) for i in range(2)]
        Y = [sb(f"Y{tag}{i}", [P, G], F32, st) for i in range(2)]
        R = [sb(f"R{tag}{i}", [P, G], F32, st) for i in range(2)]
        PC = [sb(f"PC{tag}{i}", [P, 3, G], BF16, st) for i in range(NPC)]
        if extra:
            V1V2 = sb(f"V1V2{tag}", [P, G], F32, st)
            prodA = sb(f"prodA{tag}", [XR, G], F32, st)
            prodB = sb(f"prodB{tag}", [XR, G], F32, st)
        qbias = sb(f"qbias{tag}", [P, 3], F32, st)
        TP = [pb(f"TP{tag}{i}", [P, G], st) for i in range(2)]
        PQ = [pb(f"PQ{tag}{i}", [P, G], st) for i in range(2)]
        PV = [pb(f"PV{tag}{i}", [P, G], st) for i in range(2)]
        PE_ = [pb(f"PE{tag}{i}", [P, G], st) for i in range(2)] if extra else None
        s = {n: sem(f"{n}{tag}") for n in (
            "root_done", "rstd_done", "xn_ready", "turned", "xT_ready", "qk_ready", "qk_read", "y_ready",
            "r_ready", "p1_ready", "p2_ready", "v_ready", "v_read", "ex_ready", "vv_ready", "prod_link", "cross_ready")}
        stored = [sem(f"stored{tag}{i}") for i in range(NPC)]

        w_in = sem(f"w_in{tag}")

        def pieces_free(eng, i, k):
            eng.wait_ge(stored[k % NPC], 16 * (i * (2 * NI // NPC) + k // NPC + 1))

        block = st.enter_context(nc.Block())

        def groups(eng):
            with eng.Fori(0, NG // 2 - 1) as i:
                for par in range(2):
                    yield i, par, 2 * i + par, True
            for par in range(2):
                yield NG // 2 - 1, par, NG - 2 + par, par == 0

        @block.vector
        def _(dve):
            dve.wait_ge(s["root_done"], 1)
            nc.vector.reciprocal(big["rstd"][:, :], big["std"][:, :]).then_inc(s["rstd_done"], 1)
            for m in range(2):
                nc.vector.tensor_tensor(qbias[:, m:m + 1], bcol[:, m:m + 1], scol[:, :], ALU.mult).then_inc(s["rstd_done"], 1)
            nc.vector.tensor_tensor(qbias[0:XR, 2:3], big["xb"][0:XR, 0:1], scol[0:XR, :], ALU.mult)\
                .then_inc(s["rstd_done"], 1)
            dve.wait_ge(s["rstd_done"], 4)
            dve.sem_inc(s["p2_ready"], 1)
            dve.sem_inc(s["r_ready"], 2)
            dve.sem_inc(s["v_read"], 2)
            if extra:
                dve.sem_inc(s["cross_ready"], 1)

            def normalise(par, g):
                dve.wait_ge(s["turned"], KD * (g + 1))
                for t in range(GT):
                    nc.vector.tensor_scalar(XN[par][:, t, :], X[:, bass.ds((g * GT + t) * D, D)],
                                            big["mv"][:, bass.ds(g * GT + t, 1), 0], big["rstd"][:, bass.ds(g * GT + t, 1)],
                                            ALU.subtract, ALU.mult).then_inc(s["xn_ready"], 1)

            normalise(0, 0)
            for i, par, g, more in groups(dve):
                if more:
                    normalise(1 - par, g + 1)

                def remainder(n, first):
                    rows = P if n < 4 else XR
                    k = par * NI + n
                    if n < NPQ:
                        dve.wait_ge(s["qk_read"], 2 * i * NPQ + par * NPQ + n + 1 + 2)
                    else:
                        dve.wait_ge(s["y_ready"], g + 1)
                    dve.wait_ge(s["p1_ready"], 2 * i * NI + k + 1)
                    dve.wait_ge(s["p2_ready"], 2 * i * NI + (par * NI if first or n == 1 else k - 1) + 1)
                    nc.vector.tensor_tensor(R[k % 2][0:rows, :], Y[k % 2][0:rows, :], PC[k % NPC][0:rows, 0, :],
                                            ALU.subtract).then_inc(s["r_ready"], 1)

                def last_piece(n):
                    rows = P if n < 4 else XR
                    k = par * NI + n
                    dve.wait_ge(s["p1_ready"], 2 * i * NI + k + 1 + 2)
                    dve.wait_ge(s["r_ready"], 2 * i * NI + k + 1 + 2)
                    nc.vector.tensor_tensor(PC[k % NPC][0:rows, 2, :], R[k % 2][0:rows, :], PC[k % NPC][0:rows, 1, :],
                                            ALU.subtract).then_inc(s["p2_ready"], 1)

                for n in range(NI):
                    if n == 5:
                        dve.wait_ge(s["ex_ready"], 2 * (g + 1))
                        dve.wait_ge(s["vv_ready"], 2 * (g + 1))
                        for dst, row in ((prodA, 0), (prodB, 64)):
                            nc.vector.scalar_tensor_tensor(
                                dst[:, :], PE_[0][row:row + XR, :], big["xb"][row:row + XR, 1:2],
                                V1V2[row:row + XR, :], ALU.add, ALU.mult).then_inc(s["prod_link"], 1)
                        dve.wait_ge(s["prod_link"], 2 * (g + 1))
                        nc.vector.tensor_tensor(Y[(par * NI + n) % 2][0:XR, :], prodA[:, :], prodB[:, :],
                                                ALU.subtract).then_inc(s["cross_ready"], 1)
                    remainder(n, n == 0)
                    if n >= 1:
                        last_piece(n - 1)
                last_piece(NI - 1)
                for pair in range(2):
                    dve.wait_ge(s["v_ready"], 2 * g + pair + 1 + 4)
                    nc.vector.tensor_tensor(
                        V[:, bass.ds((g * GT + 2 * pair) * D, 2 * D)].rearrange("p (t d) -> p t d", d=D),
                        PV[pair][:, :].rearrange("p (t d) -> p t d", d=D),
                        vb[:, :].unsqueeze(1).to_broadcast([P, 2, D]), ALU.add).then_inc(s["v_read"], 1)

        @block.scalar
        def _(act):
            nc.scalar.activation(big["std"][:, :], big["mv"][:, :, 1], ACT.Sqrt, bias=big["eps"][:, :])\
                .then_inc(s["root_done"], 1)
            act.sem_inc(s["xT_ready"], KD)
            act.sem_inc(s["qk_read"], 2)
            act.sem_inc(s["p1_ready"], 2)
            act.wait_ge(s["rstd_done"], 4)

            def copy_turned(par, g):
                act.wait_ge(s["v_ready"], 2 * (g + 1))
                for kk in range(KD):
                    act.wait_ge(s["turned"], KD * g + kk + 1 + 2 * KD)
                    nc.scalar.copy(xT[par][:, kk, :], TP[kk][:, :]).then_inc(s["xT_ready"], 1)

            copy_turned(0, 0)
            for i, par, g, more in groups(act):

                def middle(n):
                    rows = P if n < 4 else XR
                    k = par * NI + n
                    act.wait_ge(s["r_ready"], 2 * i * NI + k + 1 + 2)
                    nc.scalar.copy(PC[k % NPC][0:rows, 1, :], R[k % 2][0:rows, :]).then_inc(s["p1_ready"], 1)

                for n in range(NI):
                    k = par * NI + n
                    y, rows = Y[k % 2], (P if n < 4 else XR)
                    pieces_free(act, i, k)
                    if extra and n == 5:
                        act.wait_ge(s["ex_ready"], 2 * (g + 1))
                        act.wait_ge(s["cross_ready"], g + 1)
                        for row in (0, 64):
                            nc.scalar.activation(V1V2[row:row + XR, :], PE_[1][row:row + XR, :], ACT.Identity,
                                                 bias=big["xb"][row:row + XR, 2:3]).then_inc(s["vv_ready"], 1)
                        middle(n - 1)
                        act.wait_ge(s["cross_ready"], g + 2)
                        nc.scalar.copy(PC[k % NPC][0:rows, 0, :], y[0:rows, :]).then_inc(s["y_ready"], 1)
                        continue
                    q = par * NPQ + n
                    act.wait_ge(s["qk_ready"], 2 * i * NPQ + q + 1)
                    act.wait_ge(s["r_ready"], 2 * i * NI + k + 1)
                    for dst in (y[0:rows, :], PC[k % NPC][0:rows, 0, :]):
                        if n < 2:
                            last = nc.scalar.activation(dst, PQ[q % 2][:, :], ACT.Identity, bias=qbias[:, n:n + 1],
                                                        scale=scol[:, :])
                        elif n < 4:
                            last = nc.scalar.activation(dst, PQ[q % 2][:, :], ACT.Identity, bias=bcol[:, n:n + 1])
                        else:
                            last = nc.scalar.activation(dst, PQ[q % 2][0:XR, :], ACT.Identity,
                                                        bias=qbias[0:XR, 2:3], scale=scol[0:XR, :])
                    last.then_inc(s["qk_read"], 1)
                    if n >= 1:
                        middle(n - 1)
                if more:
                    copy_turned(1 - par, g + 1)
                middle(NI - 1)

        @block.tensor
        def _(pe):
            pe.sem_inc(s["turned"], 2 * KD)
            pe.sem_inc(s["v_ready"], 4)
            pe.wait_ge(w_in, 16)

            def turn(par, g):
                pe.wait_ge(s["xT_ready"], KD * (g + 1))
                for kk in range(KD):
                    for t in range(GT):
                        if kk == 0:
                            pe.wait_ge(s["xn_ready"], GT * g + t + 1)
                        last = nc.tensor.transpose(TP[kk][:, t * P:(t + 1) * P],
                                                   XN[par][:, t, kk * P:(kk + 1) * P], big["identF"][:, :])
                    last.then_inc(s["turned"], 1)

            turn(0, 0)
            for i, par, g, more in groups(pe):
                pe.wait_ge(s["xT_ready"], KD * (g + 2))
                for n in range(NPQ):
                    q = par * NPQ + n
                    pe.wait_ge(s["qk_read"], 2 * i * NPQ + q + 1)
                    for kk in range(KD):
                        if n < 4:
                            last = nc.tensor.matmul(PQ[q % 2][:, :], big["WT"][:, kk, n * P:(n + 1) * P],
                                                    xT[par][:, kk, :], start=kk == 0, stop=kk == KD - 1)
                        else:
                            last = nc.tensor.matmul(PQ[q % 2][0:XR, :], big["XW"][:, kk, 0, :], xT[par][:, kk, :],
                                                    start=kk == 0, stop=kk == KD - 1)
                    last.then_inc(s["qk_ready"], 1)
                if extra:
                    pe.wait_ge(s["cross_ready"], g + 1)
                    for b, sets in ((0, (1, 2)), (1, (3, 4))):
                        for kk in range(KD):
                            for row, j in zip((0, 64), sets):
                                last = nc.tensor.matmul(PE_[b][row:row + XR, :], big["XW"][:, kk, j, :],
                                                        xT[par][:, kk, :], start=kk == 0, stop=kk == KD - 1)
                        last.then_inc(s["ex_ready"], 1)
                if more:
                    turn(1 - par, g + 1)
                for pair in range(2):
                    pe.wait_ge(s["v_read"], 2 * g + pair + 1)
                    for t in (2 * pair, 2 * pair + 1):
                        for kk in range(KD):
                            last = nc.tensor.matmul(PV[pair][:, (t % 2) * D:(t % 2 + 1) * D],
                                                    xT[par][:, kk, t * P:(t + 1) * P],
                                                    big["WT"][:, kk, 2 * D:3 * D],
                                                    start=kk == 0, stop=kk == KD - 1)
                    last.then_inc(s["v_ready"], 1)

        @block.sync
        def _(sp):
            sp.dma_start(big["WT"][:, :, :], scratch["w"][0 if causal else 1]).then_inc(w_in, 16)
            for n in range(NPC):
                sp.sem_inc(stored[n], 16)
            for i, par, g, more in groups(sp):
                b, t0 = g // (NG // B), (g % (NG // B)) * G
                for n in range(NI):
                    k = par * NI + n
                    sp.wait_ge(s["p2_ready"], 2 * i * NI + k + 1 + 1)
                    if n < 4:
                        dst = scratch["q" if n < 2 else "k"][bass.ds(b, 1), :, (n % 2) * P:(n % 2 + 1) * P, bass.ds(t0, G)]
                        rows = P
                    else:
                        dst = scratch["qx" if n == 4 else "kx"][bass.ds(b, 1), :, :, bass.ds(t0, G)]
                        rows = XR
                    sp.dma_start(dst.rearrange("b k r t -> r (b k) t"), PC[k % NPC][0:rows, :, :]).then_inc(stored[k % NPC], 16)
            for n in range(NPC):
                sp.wait_ge(stored[n], 16 * NI * NG // NPC + 16)


def plan_units(causal):
    HALF = S // 2
    order = [1, 0]
    steps = []
    for hf in order:
        kts = [kt for kt in range(KT) if not causal or kt * P < (hf + 1) * HALF]
        lo = {kt: max(0, kt * P - hf * HALF) if causal else 0 for kt in kts}
        while kts:
            kt = kts.pop(0)
            parts = [(kt, lo[kt], lo[kt])]
            if kts and HALF - lo[kts[-1]] == lo[kt]:
                parts.append((kts[-1], lo[kts[-1]], 0))
                kts.pop()
            steps.append((hf, parts))
    chunks = []
    for hf in order:
        for qt in range(8 * hf, 8 * hf + 8):
            keys = (qt + 1) * P if causal else S
            for c in range((keys + G - 1) // G):
                chunks.append((hf, qt, c, min(G, keys - c * G)))
    shift = 4 if causal else 7
    ahead = 1.1 if causal else 1.0
    n = len(steps)
    weight = [sum(HALF - lo for _, lo, _ in parts) // P + 2 for _, parts in steps]
    cyc = [(shift + j) % n for j in range(n)]
    total = sum(weight)
    total_c = sum(w + P for *_, w in chunks)
    at = [[] for _ in range(n)]
    acc = 0
    j = 0
    donew = 0
    for pos, stp in enumerate(cyc):
        acc += weight[stp]
        while j < len(chunks) and (donew + chunks[j][3] / 2) / total_c <= ahead * acc / total or (pos == n - 1 and j < len(chunks)):
            at[pos].append(j)
            donew += chunks[j][3] + P
            j += 1
    return order, steps, chunks, shift, cyc, at


def units(nc, tag, causal, big, scratch, V, sb, pb, sem, side_loads):
    extra = not causal
    NM = 2
    NR = NM + 6 * HD + (6 * C3 if extra else 0)
    HALF = S // 2
    order, steps, chunks, shift, cyc, at = plan_units(causal)
    NS, NC = len(steps), len(chunks)
    NP = 4 if NS % 4 == 0 else 3
    assert NS % NP == 0 and NS % 2 == 0 and NC % 2 == 0
    H1 = sum(1 for x in steps if x[0] == order[0])
    per_half = {hf: sum(1 for c in chunks if c[0] == hf) for hf in order}
    z1 = next(p for p in range(NS) if at[p] and at[p][-1] >= per_half[order[0]] - 1)
    last_kt = {(hf, j): [kt for h, parts in steps for kt, lo, _ in parts if h == hf and lo < 256 * (j + 1)][-1]
               for hf in order for j in range(4)}
    O_PREV, O_THIS = 2, H1 + 2
    M_SECOND = shift + 1
    M_FIRST = shift + z1 + 1
    M_FIRST += M_FIRST == O_THIS
    assert M_FIRST < NS and len({O_PREV, O_THIS, M_SECOND, M_FIRST}) == 4 and M_SECOND < H1
    with ExitStack() as st:
        QS = [sb(f"QS{tag}{i}", [P, S], BF16, st) for i in range(2)]
        KS = [sb(f"KS{tag}{i}", [P, S], BF16, st) for i in range(2)]
        Vh = [sb(f"Vh{tag}{i}", [P, KT, 32], F32, st) for i in range(2)]
        PR = [sb(f"PR{tag}{i}", [P, HALF], F32, st) for i in range(NP)]
        Osb = sb(f"Osb{tag}", [P, D], F32, st)
        mx = [sb(f"mx{tag}{i}", [P, KT, 4], F32, st) for i in range(2)]
        nm = sb(f"nm{tag}", [P, 8], F32, st)
        nmp = [sb(f"nmp{tag}{i}", [P, 8, NM], BF16, st) for i in range(2)]
        rec = sb(f"rec{tag}", [P, 2, 4], F32, st)
        ones = sb(f"ones{tag}", [NM, S], BF16, st)
        zeros = sb(f"zeros{tag}", [NM, S], BF16, st)
        SP_ = [pb(f"S{tag}{i}", [P, HALF], st) for i in range(2)]
        MP = [pb(f"M{tag}{i}", [P, G], st) for i in range(2)]
        OP = pb(f"O{tag}", [P, G], st)
        TB = pb(f"T{tag}", [P, G], st)
        s = {n: sem(f"{n}{tag}") for n in (
            "ones_made", "ones_in", "vh_preset", "mx_preset", "vh_ready", "scores_ready", "exp_done", "max_ready", "max_read", "pv_done",
            "o_copied", "o_turned", "nm_link", "nm_made", "nm_turned", "nm_rows", "ao_link", "bias_added")}
        loaded = [sem(f"qk_loaded{tag}{i}") for i in range(2)]
        nload = 7 + (6 if extra else 0)
        block = st.enter_context(nc.Block())

        def unit_loop(eng, emit):
            emit(0, 0, False, True)
            with eng.Fori(0, (U - 2) // 2) as i:
                emit(2 * i + 1, 1, True, True)
                emit(2 * i + 2, 0, True, True)
            emit(U - 1, 1, True, False)

        def max_part(u, st_, nxt):
            pos = (st_ - shift) % NS
            if st_ < shift:
                return [(u, j, True) for j in at[pos]]
            return [(u + 1, j, False) for j in at[pos]] if nxt else []

        @block.gpsimd
        def _(pool):
            for i in range(2):
                pool.memset(Vh[i][:, :, HD:], 0.0).then_inc(s["vh_preset"], 1)
            pool.memset(zeros[:, :], 0.0).then_inc(s["ones_made"], 1)
            pool.memset(ones[:, :], 1.0).then_inc(s["ones_made"], 1)
            pool.wait_ge(s["vh_preset"], 2)
            for i in range(2):
                pool.memset(Vh[i][:, :, HD:HD + 1], 1.0).then_inc(s["vh_preset"], 1)
            pool.wait_ge(s["vh_preset"], 4)

            def copy_values(u, par, _prev, _nxt):
                if not (isinstance(u, int) and u < 2):
                    pool.wait_ge(s["pv_done"], (u - 1) * NS + NP)
                b, h = u // H, u % H
                src = V[:, :].rearrange("p (b k c) -> p b k c", b=B, k=KT)
                nc.gpsimd.tensor_copy(Vh[par][:, :, 0:HD], src[:, bass.ds(b, 1), :, bass.ds(h * HD, HD)]
                                      .rearrange("p b k c -> p (b k) c")).then_inc(s["vh_ready"], 1)

            unit_loop(pool, copy_values)
            ob = big["obA"] if causal else big["obB"]
            with pool.Fori(0, NT) as t:
                nc.gpsimd.tensor_tensor(big["X"][:, bass.ds(t * D, D)], big["X"][:, bass.ds(t * D, D)], ob[:, :],
                                        ALU.add).then_inc(s["bias_added"], 1)

        def load_unit(sp, u, par):
            b, h = u // H, u % H
            sp.dma_start(QS[par][0:NM, :], zeros[:, :]).then_inc(loaded[par], 16)
            for side, buf, runs in (("q", QS, Q_RUNS), ("k", KS, K_RUNS)):
                for scr, width, row in [(scratch[side], HD, NM)] + ([(scratch[side + "x"], C3, NM + 6 * HD)] if extra else []):
                    for first, pieces, copies in runs:
                        n = pieces * copies * width
                        src = scr[bass.ds(b, 1), first:first + pieces, bass.ds(h * width, width), :]\
                            .rearrange("b k r t -> (b k) r t")
                        if copies > 1:
                            src = src.to_broadcast([copies, width, S])
                        sp.dma_start(buf[par][row:row + n, :], src).then_inc(loaded[par], 16)
                        row += n

        @block.sync
        def _(sp):
            sp.wait_ge(s["ones_made"], 2)
            for i in range(2):
                sp.dma_start(KS[i][0:NM, :], ones[:, :]).then_inc(s["ones_in"], 16)
            load_unit(sp, 0, 0)

            def emit(u, par, prev, nxt):
                if nxt:
                    sp.wait_ge(s["scores_ready"], u * NS)
                    load_unit(sp, u + 1, 1 - par)
                if side_loads and (par == 1 and prev and nxt):
                    side_loads(sp, u // 2)
                if side_loads and not prev:
                    side_loads(sp, None)

            unit_loop(sp, emit)

        @block.tensor
        def _(pe):
            pe.sem_inc(s["pv_done"], NP)

            def maxima(u, par, j):
                hf, qt, c, w = chunks[j]
                if j == 0:
                    pe.wait_ge(loaded[par], (u // 2 + 1) * 16 * nload)
                pe.wait_ge(s["max_read"], u * NC + j + 1)
                diag = causal and c == qt // 4
                last = nc.tensor.matmul(MP[j % 2][:, 0:w], QS[par][0:NR, qt * P:(qt + 1) * P],
                                        KS[par][0:NR, c * G:c * G + w], start=True, stop=not diag)
                if diag:
                    last = nc.tensor.matmul(MP[j % 2][:, w - P:w], big["identB"][:, :], big["maskQ"][:, :],
                                            start=False, stop=True)
                last.then_inc(s["max_ready"], 1)

            def scores(u, par, x):
                hf, parts = steps[x]
                pe.wait_ge(s["exp_done"], u * NS + x + 1)
                if x == 0 or x == H1:
                    pe.wait_ge(s["nm_rows"], 2 * u + 1 + (x == H1))
                q0 = hf * HALF
                for kt, lo, at_ in parts:
                    diag = causal and kt * P >= q0
                    for c in range(2):
                        a, z = max(at_, c * G), min(at_ + HALF - lo, (c + 1) * G)
                        if a >= z:
                            continue
                        here = diag and a == at_
                        q = q0 + lo + a - at_
                        last = nc.tensor.matmul(SP_[x % 2][:, a:z], KS[par][0:NR, kt * P:(kt + 1) * P],
                                                QS[par][0:NR, q:q + z - a], start=True, stop=not here)
                        if here:
                            last = nc.tensor.matmul(SP_[x % 2][:, a:a + P], big["identB"][:, :], big["maskK"][:, :],
                                                    start=False, stop=True)
                last.then_inc(s["scores_ready"], 1)

            def values(u, par, x, quarters=range(4)):
                hf, parts = steps[x]
                if 0 in quarters:
                    pe.wait_ge(s["exp_done"], u * NS + x + 1 + 2)
                if x == 0 and 0 in quarters:
                    pe.wait_ge(s["vh_ready"], u + 1)
                if (x == 0 or x == H1) and 0 in quarters:
                    pe.wait_ge(s["o_copied"], 2 * u + (x == H1))
                for kt, lo, at_ in parts:
                    for j in quarters:
                        a, z = max(lo, 256 * j), 256 * (j + 1)
                        if a >= z:
                            continue
                        last = nc.tensor.matmul(OP[32 * j:32 * j + 32, a - 256 * j:256], Vh[par][:, kt, :],
                                                PR[x % NP][:, at_ + a - lo:at_ + z - lo], start=kt == 0,
                                                stop=kt == last_kt[hf, j])
                if 3 in quarters:
                    last.then_inc(s["pv_done"], 1)

            def turn_output(k, maxima_before):
                pe.wait_ge(s["o_copied"], k + 1)
                pe.wait_ge(s["ao_link"], 2 * k)
                pe.wait_ge(s["nm_rows"], maxima_before)
                for c in range(2):
                    last = nc.tensor.transpose(TB[:, c * P:(c + 1) * P], Osb[:, c * P:(c + 1) * P], big["identF"][:, :])
                last.then_inc(s["o_turned"], 1)

            def turn_max(k, pos, outputs_before):
                pe.wait_ge(s["nm_made"], k + 1)
                pe.wait_ge(s["nm_rows"], k)
                pe.wait_ge(s["ao_link"], 2 * outputs_before)
                for q in range(8):
                    last = nc.tensor.transpose(TB[:, :].bitcast(BF16)[0:NM, q * P:(q + 1) * P], nmp[pos][:, q, :],
                                               big["identB"][:, :])
                last.then_inc(s["nm_turned"], 1)

            pe.wait_ge(s["ones_in"], 32)
            for x in range(shift, NS):
                for _, j, _ in max_part(-1, x, True):
                    maxima(0, 0, j)
            turn_max(0, 0, 0)

            def emit(u, par, prev, nxt):
                for x in range(NS):
                    scores(u, par, x)
                    mp = [(w, par if own else 1 - par, j) for w, j, own in max_part(u, x, nxt)]
                    before = (u, par, x - 1) if x > 0 else (u - 1, 1 - par, NS - 1) if prev else None
                    if before and len(mp) >= 3:
                        cuts = [mp[:1], mp[1:-1], mp[-1:]]
                    else:
                        cuts = [mp[:(len(mp) + 1) // 2], [], mp[(len(mp) + 1) // 2:]]
                    for part, quarters in zip(cuts, (None, (0, 1), (2, 3))):
                        if quarters and before:
                            values(*before, quarters)
                        for m in part:
                            maxima(*m)
                    if x == O_PREV and prev:
                        turn_output(2 * u - 1, 2 * u + 1 + (M_SECOND < O_PREV))
                    if x == M_SECOND:
                        turn_max(2 * u + 1, 1, 2 * u - (0 if O_PREV < M_SECOND or not prev else 1))
                    if x == O_THIS:
                        turn_output(2 * u, 2 * u + 2 + (M_FIRST < O_THIS and nxt))
                    if x == M_FIRST and nxt:
                        turn_max(2 * u + 2, 0, 2 * u + (O_THIS < M_FIRST))

            unit_loop(pe, emit)
            values(U - 1, 1, NS - 1)
            turn_output(2 * U - 1, 2 * U)

        @block.scalar
        def _(act):
            act.sem_inc(s["exp_done"], 2)

            def put_max(k, pos, par):
                hf = order[pos]
                act.wait_ge(s["nm_turned"], k + 1)
                nc.scalar.copy(QS[par][0:NM, hf * HALF:(hf + 1) * HALF], TB[:, :].bitcast(BF16)[0:NM, 0:HALF])\
                    .then_inc(s["nm_rows"], 1)

            def copy_output(k):
                act.wait_ge(s["o_turned"], k)
                nc.scalar.copy(Osb[:, :], OP[:, 0:D]).then_inc(s["o_copied"], 1)

            def emit(u, par, prev, nxt):
                for x in range(NS):
                    lo = min(at_ for _, _, at_ in steps[x][1])
                    act.wait_ge(s["scores_ready"], u * NS + x + 1)
                    act.wait_ge(s["pv_done"], u * NS + x + 1)
                    nc.scalar.activation(PR[x % NP][:, lo:], SP_[x % 2][:, lo:], ACT.Exp).then_inc(s["exp_done"], 1)
                    if x == 0 and prev:
                        act.wait_ge(s["pv_done"], u * NS + NP)
                        copy_output(2 * u - 1)
                    if x == H1:
                        act.wait_ge(s["pv_done"], u * NS + H1 + NP)
                        copy_output(2 * u)
                    if x == M_SECOND:
                        put_max(2 * u + 1, 1, par)
                    if x == M_FIRST and nxt:
                        put_max(2 * u + 2, 0, 1 - par)

            put_max(0, 0, 0)
            unit_loop(act, emit)
            act.wait_ge(s["pv_done"], U * NS + NP)
            copy_output(2 * U - 1)

        @block.vector
        def _(dve):
            dve.sem_inc(s["max_read"], 2)
            if causal:
                for i in range(2):
                    nc.vector.memset(mx[i][:, :, :], LOWEST).then_inc(s["mx_preset"], 1)
                dve.wait_ge(s["mx_preset"], 2)

            def reduce_chunk(u, par, j):
                hf, qt, c, w = chunks[j]
                dve.wait_ge(s["max_ready"], u * NC + j + 1)
                nc.vector.tensor_reduce(mx[par][:, qt, c:c + 1], MP[j % 2][:, 0:w], AX.X, ALU.max)\
                    .then_inc(s["max_read"], 1)

            def make_max(u, par, pos, k):
                hf = order[pos]
                done = u * NC + (per_half[order[0]] if pos == 0 else NC)
                dve.wait_ge(s["max_read"], done + 2)
                dve.wait_ge(s["nm_made"], k)
                if not (isinstance(k, int) and k < 2):
                    dve.wait_ge(s["nm_turned"], k - 1)
                link = chain(dve, s["nm_link"], 2 * k)
                link(nc.vector.tensor_reduce(nm[:, :], mx[par][:, 8 * hf:8 * hf + 8, :], AX.X, ALU.max, negate=True))
                link(nc.vector.tensor_copy(nmp[pos][:, :, 0], nm[:, :]))
                nc.vector.tensor_tensor(nmp[pos][:, :, 1], nm[:, :], nmp[pos][:, :, 0], ALU.subtract)\
                    .then_inc(s["nm_made"], 1)

            def take_output(u, pos, k):
                hf = order[pos]
                dve.wait_ge(s["o_turned"], k + 1)
                tv = TB[:, 0:D].rearrange("p (c j r) -> p c j r", c=2, j=4)
                dve.wait_ge(s["ao_link"], 2 * k)
                link = chain(dve, s["ao_link"], 2 * k)
                link(nc.vector.reciprocal(rec[:, :, :], tv[:, :, :, HD]))
                b, h = u // H, u % H
                dst = V[:, :].rearrange("p (b k c) -> p b k c", b=B, k=KT)[
                    :, bass.ds(b, 1), 8 * hf:8 * hf + 8, bass.ds(h * HD, HD)].rearrange("p b (j c) d -> p c (b j) d", j=4)
                nc.vector.tensor_tensor(dst, tv[:, :, :, 0:HD], rec[:, :, :].unsqueeze(3).to_broadcast([P, 2, 4, HD]),
                                        ALU.mult).then_inc(s["ao_link"], 1)

            for x in range(shift, NS):
                for _, j, _ in max_part(-1, x, True):
                    reduce_chunk(0, 0, j)
            make_max(0, 0, 0, 0)

            def emit(u, par, prev, nxt):
                for x in range(NS):
                    for w, j, own in max_part(u, x, nxt):
                        reduce_chunk(w, par if own else 1 - par, j)
                    if x == shift - 1:
                        make_max(u, par, 1, 2 * u + 1)
                    if x == shift + z1 and nxt:
                        make_max(u + 1, 1 - par, 0, 2 * u + 2)
                    if x == O_PREV and prev:
                        take_output(u - 1, 1, 2 * u - 1)
                    if x == O_THIS:
                        take_output(u, 0, 2 * u)

            unit_loop(dve, emit)
            take_output(U - 1, 1, 2 * U - 1)


def combine(nc, tag, big, AO, sb, pb, sem):
    X = big["X"]
    with ExitStack() as st:
        aT = [sb(f"aT{tag}{i}", [P, KD, G], F32, st) for i in range(2)]
        stage = [sb(f"stage{tag}{i}", [P, GT, D], F32, st) for i in range(2)]
        TP = [pb(f"cT{tag}{i}", [P, G], st) for i in range(4)]
        PO = [pb(f"cO{tag}{i}", [P, G], st) for i in range(4)]
        staged, turned, aT_ready, out_ready, out_read, measured = (sem(f"{n}{tag}") for n in (
            "c_staged", "c_turned", "c_aT_ready", "c_out_ready", "c_out_read", "c_measured"))
        block = st.enter_context(nc.Block())

        def groups(eng):
            with eng.Fori(0, NG // 2) as i:
                for par in range(2):
                    yield par, 2 * i + par

        @block.gpsimd
        def _(pool):
            for par, g in groups(pool):
                pool.wait_ge(turned, KD * (g + 1))
                nc.gpsimd.tensor_copy(stage[par][:, :, :].rearrange("p t d -> p (t d)"),
                                      AO[:, bass.ds(g * GT * D, GT * D)]).then_inc(staged, 1)

        @block.tensor
        def _(pe):
            pe.sem_inc(turned, 2 * KD)
            pe.sem_inc(out_ready, 4)

            def turn(par, g):
                pe.wait_ge(staged, g + 1)
                pe.wait_ge(aT_ready, KD * (g + 1))
                for kk in range(KD):
                    for t in range(GT):
                        last = nc.tensor.transpose(TP[2 * par + kk][:, t * P:(t + 1) * P],
                                                   stage[par][:, t, kk * P:(kk + 1) * P], big["identF"][:, :])
                    last.then_inc(turned, 1)

            def project_out(par, g):
                pe.wait_ge(aT_ready, KD * (g + 1) + 2 * KD)
                for pair in range(2):
                    pe.wait_ge(out_read, 2 * g + pair + 1)
                    for t in (2 * pair, 2 * pair + 1):
                        for kk in range(KD):
                            last = nc.tensor.matmul(PO[2 * par + pair][:, (t % 2) * D:(t % 2 + 1) * D],
                                                    aT[par][:, kk, t * P:(t + 1) * P], big["WT"][:, kk, 3 * D:4 * D],
                                                    start=kk == 0, stop=kk == KD - 1)
                    last.then_inc(out_ready, 1)

            turn(0, 0)
            with pe.Fori(0, NG // 2 - 1) as i:
                for par in range(2):
                    turn(1 - par, 2 * i + par + 1)
                    project_out(par, 2 * i + par)
            turn(1, NG - 1)
            project_out(0, NG - 2)
            project_out(1, NG - 1)

        @block.scalar
        def _(act):
            act.sem_inc(aT_ready, 2 * KD)
            for par, g in groups(act):
                act.wait_ge(out_ready, 2 * (g + 1))
                for kk in range(KD):
                    act.wait_ge(turned, KD * g + kk + 1 + 2 * KD)
                    nc.scalar.copy(aT[par][:, kk, :], TP[2 * par + kk][:, :]).then_inc(aT_ready, 1)

        @block.vector
        def _(dve):
            dve.sem_inc(out_read, 4)
            for par, g in groups(dve):
                for pair in range(2):
                    dve.wait_ge(out_ready, 2 * g + pair + 1 + 4)
                    xs = X[:, bass.ds((g * GT + 2 * pair) * D, 2 * D)]
                    nc.vector.tensor_tensor(xs, PO[2 * par + pair][:, :], xs, ALU.add).then_inc(out_read, 1)
                dve.wait_ge(out_read, 2 * (g + 1) + 4)
                for t in range(GT):
                    last = nc.vector.bn_stats(big["stats"][:, bass.ds(g * GT + t, 1), :].rearrange("p a b -> p (a b)"),
                                              X[:, bass.ds((g * GT + t) * D, D)])
                last.then_inc(measured, 1)
            dve.wait_ge(measured, NG)
            for t in range(NT):
                nc.vector.bn_aggr(big["mv"][:, t, :], big["stats"][:, t, :])


def experts(nc, tag, big, scratch, out, sb, pb, sem, ffn_loaded, slots_zeroed):
    with ExitStack() as st:
        r = dict(
            xT=sb(f"xT_all{tag}", [P, KD, T], F32, st),
            XN=sb(f"XN_all{tag}", [P, NT, D], F32, st),
            wt=sb(f"wt{tag}", [P, NT, EX], F32, st),
            slot=[sb(f"slot{tag}{k}", [P, NT], mybir.dt.uint32, st) for k in range(TOP)],
            w=[sb(f"w{tag}{k}", [P, NT], F32, st) for k in range(TOP)],
            eid=sb(f"eid{tag}", [1, ST], mybir.dt.int32, st),
            pr=sb(f"fpr{tag}", [P, NT, NE], F32, st),
            rank=sb(f"frank{tag}", [P, NT, NE], F32, st),
            base=sb(f"fbase{tag}", [P, NE], F32, st),
            tile_no=sb(f"ftile_no{tag}", [1, ST], F32, st),
        )
        route(nc, tag, big, r, sb, pb, sem)
        apply_experts(nc, tag, big, scratch, out, r, sb, pb, sem, ffn_loaded, slots_zeroed)


def route(nc, tag, big, r, sb, pb, sem):
    X, XN, xT, wt = big["X"], r["XN"], r["xT"], r["wt"]
    with ExitStack() as st:
        lg = sb(f"flg{tag}", [P, NT, NE], F32, st)
        pr, rank, tile_no = r["pr"], r["rank"], r["tile_no"]
        m1 = sb(f"fm1{tag}", [P, NT], F32, st)
        slot_f = sb(f"fslot{tag}", [P, TOP, NT], F32, st)
        beats = sb(f"fbeats{tag}", [P, 2, NT, NE], F32, st)
        chosen = sb(f"fchosen{tag}", [P, NT, NE], BF16, st)
        run = [sb(f"frun{tag}{i}", [P, NT, NE], F32, st) for i in range(2)]
        base = [sb(f"fbase{tag}{i}", [P, NE], F32, st) for i in range(2)]
        base_slot = sb(f"fbase_slot{tag}", [P, NE], F32, st)
        tiles_of = sb(f"ftiles{tag}", [P, NE], F32, st)
        edge = sb(f"fedge{tag}", [P, NT], F32, st)
        over = sb(f"fover{tag}", [P, NE, NT], F32, st)
        TP = [pb(f"rTP{tag}{i}", [P, G], st) for i in range(4)]
        LP = [pb(f"rLP{tag}{i}", [P, G], st) for i in range(2)]
        rows = [sb(f"frows{tag}{i}", [P, G], F32, st) for i in range(2)]
        PP = [pb(f"rPP{tag}{i}", [P, G], st) for i in range(2)]
        s = {n: sem(f"r_{n}{tag}") for n in (
            "root_done", "rstd_done", "xn_ready", "turned", "xT_ready", "rows_ready", "rows_read",
            "lg_ready", "link", "ls_ready",
            "e_done", "chosen_ready", "prefix_ready", "numbers", "preset")}
        block = st.enter_context(nc.Block())

        @block.gpsimd
        def _(pool):
            pool.iota(edge[:, :], pattern=[[P, NT]], base=0, channel_multiplier=0,
                      allow_small_or_imprecise_dtypes=True).then_inc(s["numbers"], 1)
            pool.iota(tile_no[:, :], pattern=[[1, ST]], base=0, channel_multiplier=0,
                      allow_small_or_imprecise_dtypes=True).then_inc(s["numbers"], 1)

        @block.vector
        def _(dve):
            nc.vector.memset(wt[:, :, SH:], 1.0).then_inc(s["preset"], 1)
            nc.vector.memset(rank[:, :, :], 0.0).then_inc(s["preset"], 1)
            dve.wait_ge(s["root_done"], 1)
            nc.vector.reciprocal(big["rstd"][:, :], big["std"][:, :]).then_inc(s["rstd_done"], 1)
            dve.wait_ge(s["rstd_done"], 1)
            for t in range(NT):
                nc.vector.tensor_scalar(XN[:, t, :], X[:, t * D:(t + 1) * D], big["mv"][:, t, 0:1],
                                        big["rstd"][:, t:t + 1], ALU.subtract, ALU.mult).then_inc(s["xn_ready"], 1)
            dve.wait_ge(s["lg_ready"], 2)
            dve.wait_ge(s["numbers"], 2)
            dve.wait_ge(s["preset"], 2)
            link = chain(dve, s["link"])

            def per_token(v):
                return v.unsqueeze(2).to_broadcast([P, NT, NE])

            for b in range(2):
                last = nc.vector.tensor_tensor(
                    lg[:, b * NT // 2:(b + 1) * NT // 2, :].rearrange("p (j t) e -> p j t e", t=GT),
                    TP[b][:, :].rearrange("p (t j r) -> p j t r", t=GT, j=4)[:, :, :, 0:NE],
                    big["rb"][:, :].unsqueeze(1).unsqueeze(1).to_broadcast([P, 4, GT, NE]), ALU.add)
            link(last)
            link(nc.vector.tensor_reduce(m1[:, :], lg[:, :, :], AX.X, ALU.max))
            nc.vector.tensor_tensor(lg[:, :, :], lg[:, :, :], per_token(m1[:, :]), ALU.subtract).then_inc(s["ls_ready"], 1)
            dve.wait_ge(s["e_done"], 1)
            link(nc.vector.tensor_reduce(m1[:, :], pr[:, :, :], AX.X, ALU.add))
            link(nc.vector.reciprocal(m1[:, :], m1[:, :]))
            link(nc.vector.tensor_tensor(pr[:, :, :], pr[:, :, :], per_token(m1[:, :]), ALU.mult))
            for j in range(NE):
                bt = beats[:, j % 2, :, :]
                if j + 1 < NE:
                    last = nc.vector.tensor_tensor(bt[:, :, j + 1:], pr[:, :, j:j + 1].to_broadcast([P, NT, NE - 1 - j]),
                                                   pr[:, :, j + 1:], ALU.is_ge)
                if j > 0:
                    last = nc.vector.tensor_tensor(bt[:, :, 0:j], pr[:, :, j:j + 1].to_broadcast([P, NT, j]),
                                                   pr[:, :, 0:j], ALU.is_gt)
                link(last)
                if j + 1 < NE:
                    last = nc.vector.tensor_tensor(rank[:, :, j + 1:], rank[:, :, j + 1:], bt[:, :, j + 1:], ALU.add)
                if j > 0:
                    last = nc.vector.tensor_tensor(rank[:, :, 0:j], rank[:, :, 0:j], bt[:, :, 0:j], ALU.add)
                link(last)
            nc.vector.tensor_scalar(chosen[:, :, :], rank[:, :, :], float(TOP), None, ALU.is_lt).then_inc(s["chosen_ready"], 1)
            nc.vector.scalar_tensor_tensor(wt[:, :, 0:NE], rank[:, :, :], float(TOP), pr[:, :, :], ALU.is_lt, ALU.mult)\
                .then_inc(s["preset"], 1)
            dve.wait_ge(s["prefix_ready"], 2)
            link(nc.vector.tensor_copy(run[0][:, :, :], PP[1][:, 0:NT * NE].rearrange("p (t e) -> p t e", e=NE)))
            a, k = 0, 1
            while k < NT:
                nc.vector.tensor_copy(run[1 - a][:, 0:k, :], run[a][:, 0:k, :])
                link(nc.vector.tensor_tensor(run[1 - a][:, k:, :], run[a][:, k:, :], run[a][:, 0:NT - k, :], ALU.add))
                a, k = 1 - a, 2 * k
            link(nc.vector.tensor_tensor(over[:, :, :], run[a][:, NT - 1, :].unsqueeze(2).to_broadcast([P, NE, NT]),
                                         edge[:, :].unsqueeze(1).to_broadcast([P, NE, NT]), ALU.is_gt))
            link(nc.vector.tensor_reduce(tiles_of[:, :], over[:, :, :], AX.X, ALU.add))
            link(nc.vector.memset(base[0][:, 0:1], 0.0))
            link(nc.vector.tensor_copy(base[0][:, 1:], tiles_of[:, 0:NE - 1]))
            b, k = 0, 1
            while k < NE:
                nc.vector.tensor_copy(base[1 - b][:, 0:k], base[b][:, 0:k])
                link(nc.vector.tensor_tensor(base[1 - b][:, k:], base[b][:, k:], base[b][:, 0:NE - k], ALU.add))
                b, k = 1 - b, 2 * k
            link(nc.vector.tensor_tensor(run[a][:, :, :], run[a][:, :, :],
                                         PP[1][:, 0:NT * NE].rearrange("p (t e) -> p t e", e=NE), ALU.subtract))
            link(nc.vector.tensor_tensor(run[a][:, :, :], run[a][:, :, :],
                                         PP[0][:, 0:NT * NE].rearrange("p (t e) -> p t e", e=NE), ALU.add))
            nc.vector.tensor_copy(r["base"][:, :], base[b][:, :]).then_inc(s["preset"], 1)
            link(nc.vector.tensor_scalar(base_slot[:, :], base[b][:, :], float(P), None, ALU.mult))
            link(nc.vector.tensor_tensor(run[a][:, :, :], run[a][:, :, :],
                                         base_slot[:, :].unsqueeze(1).to_broadcast([P, NT, NE]), ALU.add))
            for k in range(TOP):
                part = (run[1 - a], beats[:, 0, :, :])[k]
                last = nc.vector.scalar_tensor_tensor(part[:, :, :], rank[:, :, :], float(k), run[a][:, :, :],
                                                      ALU.is_equal, ALU.mult)
            link(last)
            for k in range(TOP):
                part = (run[1 - a], beats[:, 0, :, :])[k]
                last = nc.vector.tensor_reduce(slot_f[:, k, :], part[:, :, :], AX.X, ALU.add)
            link(last)
            for k in range(TOP):
                nc.vector.tensor_copy(r["slot"][k][:, :], slot_f[:, k, :]).then_inc(s["preset"], 1)

        @block.scalar
        def _(act):
            nc.scalar.activation(big["std"][:, :], big["mv"][:, :, 1], ACT.Sqrt, bias=big["eps"][:, :])\
                .then_inc(s["root_done"], 1)
            act.sem_inc(s["xT_ready"], 2 * KD)
            for g in range(NG):
                for kk in range(KD):
                    act.wait_ge(s["turned"], KD * g + kk + 1)
                    nc.scalar.copy(xT[:, kk, g * G:(g + 1) * G], TP[(g % 2) * KD + kk][:, :]).then_inc(s["xT_ready"], 1)
                if g % 4 == 3:
                    act.wait_ge(s["rows_ready"], g // 4 + 1)
                    nc.scalar.copy(rows[g // 4][:, :], LP[g // 4][:, :]).then_inc(s["rows_read"], 1)
            act.wait_ge(s["ls_ready"], 1)
            nc.scalar.activation(pr[:, :, :], lg[:, :, :], ACT.Exp).then_inc(s["e_done"], 1)

        @block.tensor
        def _(pe):
            for g in range(NG):
                for kk in range(KD):
                    pe.wait_ge(s["xT_ready"], KD * g + kk + 1)
                    for t in range(GT):
                        if kk == 0:
                            pe.wait_ge(s["xn_ready"], GT * g + t + 1)
                        last = nc.tensor.transpose(TP[(g % 2) * KD + kk][:, t * P:(t + 1) * P],
                                                   XN[:, g * GT + t, kk * P:(kk + 1) * P], big["identF"][:, :])
                    last.then_inc(s["turned"], 1)
                if g % 4 == 3:
                    pe.wait_ge(s["xT_ready"], KD * (g + 1) + 2 * KD)
                    for kk in range(KD):
                        for j in range(4):
                            last = nc.tensor.matmul(LP[g // 4][32 * j:32 * j + 32, :], big["rw"][:, kk, :],
                                                    xT[:, kk, (g - 3 + j) * G:(g - 2 + j) * G],
                                                    start=kk == 0, stop=kk == KD - 1)
                    last.then_inc(s["rows_ready"], 1)
            for b in range(2):
                pe.wait_ge(s["rows_read"], b + 1)
                for t in range(GT):
                    last = nc.tensor.transpose(TP[b][:, t * P:(t + 1) * P], rows[b][:, t * P:(t + 1) * P],
                                               big["identF"][:, :])
                last.then_inc(s["lg_ready"], 1)
            pe.wait_ge(s["chosen_ready"], 1)
            flat = chosen[:, :, :].rearrange("p t e -> p (t e)")
            for j, m in enumerate(("before", "all1")):
                nc.tensor.matmul(PP[j][:, 0:NT * NE], big[m][:, :], flat, start=True, stop=True)\
                    .then_inc(s["prefix_ready"], 1)


def apply_experts(nc, tag, big, scratch, out, r, sb, pb, sem, ffn_loaded, slots_zeroed):
    X, XN, xT, wt = big["X"], r["XN"], r["xT"], r["wt"]
    again = out is None
    HALVES = (range(0, NG // 2), range(NG // 2, NG))
    TURN = 4
    YG = 8
    with ExitStack() as st:
        flat = XN[:, :, :].rearrange("p t d -> p (t d)")
        at = [0]

        def carve(shape):
            n = 1
            for x in shape:
                n *= x
            v = flat[:, at[0]:at[0] + n]
            at[0] += n
            return v.rearrange("p (a b) -> p a b", b=shape[1]) if len(shape) == 2 else v

        xg = [carve([D]) for _ in range(4)]
        xgT = [carve([KD, P]) for _ in range(2)]
        hs = [carve([HID]) for _ in range(2)]
        hT = [carve([HT, P]) for _ in range(2)]
        ys = [carve([D]) for _ in range(2)]
        yg = [[carve([D]) for _ in range(TOP)] for _ in range(YG)]
        hTs = [sb(f"hTs{tag}{i}", [P, HT, G], F32, st) for i in range(2)]
        wT = sb(f"fwT{tag}", [EX, G], F32, st)
        picked = sb(f"fpicked{tag}", [P, TOP, NT, NE], F32, st)
        reach = sb(f"freach{tag}", [1, ST, NE - 1], F32, st)
        eid_f = sb(f"feid{tag}", [1, ST], F32, st)
        TX = [pb(f"eTX{tag}{i}", [P, G], st) for i in range(2)]
        UP = [pb(f"eUP{tag}{i}", [P, G], st) for i in range(2)]
        HP = pb(f"eHP{tag}", [P, G], st)
        YP = [pb(f"eYP{tag}{i}", [P, G], st) for i in range(2)]
        WP = pb(f"eWP{tag}", [P, G], st)
        s = {n: sem(f"e_{n}{tag}") for n in (
            "scattered", "sh_ready", "sh_gelu", "wT_turned", "wT_ready", "sh_y", "sh_added", "x_turned", "xgT_ready",
            "up_done", "hs_ready", "h_turned", "hT_ready", "y_done", "ys_ready", "combined", "mix", "measured", "choice",
            "written")}
        xg_in = [sem(f"e_xg_in{tag}{i}") for i in range(4)]
        stored = [sem(f"e_stored{tag}{i}") for i in range(2)]
        gathered = [sem(f"e_gathered{tag}{i}") for i in range(YG)]
        block = st.enter_context(nc.Block())

        def tile_loop(eng, emit, tail):
            with eng.Fori(0, ST // TURN - tail) as j:
                for k in range(TURN):
                    emit(TURN * j + k, k)
            for i in range(ST - TURN * tail, ST):
                emit(i, i % TURN)

        @block.gpsimd
        def _(pool):
            pool.wait_ge(slots_zeroed, 16 * TURNS)
            for t in range(NT):
                for k in range(TOP):
                    nc.gpsimd.indirect_dma_start(
                        scratch["slots_in"][:, :], bass.IndirectOffsetOnAxis(ap=r["slot"][k][:, t:t + 1], axis=0),
                        XN[:, t, :], None).then_inc(s["scattered"], 16)
            for par in range(2):
                pool.wait_ge(stored[par], 16 * (ST // 2 + 1))
            for t in range(NT):
                if t >= YG:
                    pool.wait_ge(s["combined"], t - YG + 1)
                for k in range(TOP):
                    nc.gpsimd.indirect_dma_start(
                        yg[t % YG][k], None, scratch["slots_out"][:, :],
                        bass.IndirectOffsetOnAxis(ap=r["slot"][k][:, t:t + 1], axis=0)).then_inc(gathered[t % YG], 16)

        @block.sync
        def _(sp):
            for par in range(2):
                sp.sem_inc(stored[par], 16)
            sp.wait_ge(s["scattered"], 16 * TOP * NT)

            def load(i, k):
                sp.wait_ge(s["x_turned"], i + 1)
                sp.dma_start(xg[k % 4], scratch["slots_in"][bass.ds(i * P, P), :]).then_inc(xg_in[k % 4], 16)

            def emit(i, k, more=True):
                if not (isinstance(i, int) and i + 4 >= ST):
                    load(i + 4, k)
                sp.wait_ge(s["ys_ready"], i + 1 + 2)
                sp.dma_start(scratch["slots_out"][bass.ds(i * P, P), :], ys[k % 2]).then_inc(stored[k % 2], 16)

            for i in range(4):
                load(i, i)
            tile_loop(sp, emit, 1)
            for par in range(2):
                sp.wait_ge(stored[par], 16 * (ST // 2 + 1))
            if not again:
                view = out.rearrange("b (t p) d -> p (b t) d", p=P)
                X3 = X[:, :].rearrange("p (t d) -> p t d", d=D)
                for g in range(NG):
                    sp.wait_ge(s["combined"], (g + 1) * GT)
                    sp.dma_start(view[:, g * GT:(g + 1) * GT, :], X3[:, g * GT:(g + 1) * GT, :]).then_inc(s["written"], 16)
                sp.wait_ge(s["written"], 16 * NG)

        @block.tensor
        def _(pe):
            pe.sem_inc(s["x_turned"], 4)
            pe.sem_inc(s["up_done"], 2)
            pe.sem_inc(s["h_turned"], 2)
            pe.sem_inc(s["y_done"], 2)
            pe.wait_ge(ffn_loaded, 16 * (4 + 2 * TURNS))

            def shared_up(g):
                for m in range(HT):
                    k = g * HT + m
                    if k >= 2:
                        pe.wait_ge(s["sh_gelu"], k - 1)
                    for kk in range(KD):
                        last = nc.tensor.matmul(UP[k % 2][:, :], big["w1"][:, SH, kk, m * P:(m + 1) * P],
                                                xT[:, kk, g * G:(g + 1) * G], start=kk == 0, stop=kk == KD - 1)
                    last.then_inc(s["sh_ready"], 1)

            def shared_down(g):
                if g:
                    pe.wait_ge(s["wT_ready"], g)
                for t in range(GT):
                    last = nc.tensor.transpose(WP[0:EX, t * P:(t + 1) * P], wt[:, g * GT + t, :], big["identF"][:, :])
                last.then_inc(s["wT_turned"], 1)
                pe.wait_ge(s["wT_ready"], g + 1)
                pe.wait_ge(s["sh_gelu"], (g + 1) * HT)
                for t in range(GT):
                    k = g * GT + t
                    if k >= 2:
                        pe.wait_ge(s["sh_added"], k - 1)
                    nc.tensor.matmul(YP[k % 2][:, 0:D], wT[:, t * P:(t + 1) * P], big["b2"][:, :], start=True, stop=False)
                    for m in range(HT):
                        last = nc.tensor.matmul(YP[k % 2][:, 0:D], hTs[g % 2][:, m, t * P:(t + 1) * P],
                                                big["w2"][:, SH, m, :], start=False, stop=m == HT - 1)
                    last.then_inc(s["sh_y"], 1)

            def shared(groups):
                shared_up(groups[0])
                for g in groups:
                    if g + 1 in groups:
                        shared_up(g + 1)
                    shared_down(g)

            def turn_x(i, k):
                pe.wait_ge(xg_in[k % 4], 16 * (i // 4 + 1))
                pe.wait_ge(s["xgT_ready"], i + 1)
                for kk in range(KD):
                    last = nc.tensor.transpose(TX[k % 2][:, kk * P:(kk + 1) * P], xg[k % 4][:, kk * P:(kk + 1) * P],
                                               big["identF"][:, :])
                last.then_inc(s["x_turned"], 1)

            def up(i, k):
                e = pe.value_load(r["eid"][0:1, bass.ds(i, 1)], min_val=0, max_val=NE - 1)
                pe.wait_ge(s["xgT_ready"], i + 1 + 2)
                pe.wait_ge(s["hs_ready"], i + 1)
                w = big["w1"][:, bass.ds(e, 1), :, :].rearrange("p e k h -> p (e k) h")
                for kk in range(KD):
                    last = nc.tensor.matmul(UP[k % 2][:, :], xgT[k % 2][:, kk, :], w[:, kk, :], start=kk == 0,
                                            stop=kk == KD - 1)
                last.then_inc(s["up_done"], 1)

            def turn_h(i, k):
                pe.wait_ge(s["hs_ready"], i + 1 + 2)
                pe.wait_ge(s["hT_ready"], i + 1)
                for m in range(HT):
                    last = nc.tensor.transpose(HP[:, m * P:(m + 1) * P], hs[k % 2][:, m * P:(m + 1) * P],
                                               big["identF"][:, :])
                last.then_inc(s["h_turned"], 1)

            def down(i, k):
                e = pe.value_load(r["eid"][0:1, bass.ds(i, 1)], min_val=0, max_val=NE - 1)
                pe.wait_ge(s["hT_ready"], i + 1 + 1)
                pe.wait_ge(s["ys_ready"], i + 1)
                w = big["w2"][:, bass.ds(e, 1), :, :].rearrange("p e k d -> p (e k) d")
                for m in range(HT):
                    last = nc.tensor.matmul(YP[k % 2][:, 0:D], hT[k % 2][:, m, :], w[:, m, :], start=m == 0,
                                            stop=m == HT - 1)
                last.then_inc(s["y_done"], 1)

            shared(HALVES[0])
            pe.wait_ge(s["choice"], 3)
            pe.wait_ge(s["sh_added"], len(HALVES[0]) * GT)
            turn_x(0, 0)
            turn_x(1, 1)
            up(0, 0)
            turn_h(0, 0)

            def emit(i, k):
                static = isinstance(i, int)
                if not static or i + 2 < ST:
                    turn_x(i + 2, k + 2)
                if not static or i + 1 < ST:
                    up(i + 1, k + 1)
                down(i, k)
                if not static or i + 1 < ST:
                    turn_h(i + 1, k + 1)

            tile_loop(pe, emit, 1)
            pe.wait_ge(s["ys_ready"], ST + 2)
            shared(HALVES[1])

        @block.scalar
        def _(act):
            act.sem_inc(s["xgT_ready"], 2)
            act.sem_inc(s["hT_ready"], 1)

            def shared(groups):
                for g in groups:
                    for m in range(HT):
                        act.wait_ge(s["sh_ready"], g * HT + m + 1)
                        if m == 0 and g >= 2:
                            act.wait_ge(s["sh_y"], (g - 1) * GT)
                        nc.scalar.activation(hTs[g % 2][:, m, :], UP[(g * HT + m) % 2][:, :], ACT.Gelu,
                                             bias=big["b1"][:, SH, m:m + 1]).then_inc(s["sh_gelu"], 1)

            def copy_x(i, k):
                act.wait_ge(s["x_turned"], i + 1 + 4)
                act.wait_ge(s["up_done"], i + 1)
                nc.scalar.copy(xgT[k % 2].rearrange("p a b -> p (a b)"), TX[k % 2][:, 0:D]).then_inc(s["xgT_ready"], 1)

            def gelus(i, k):
                e = act.value_load(r["eid"][0:1, bass.ds(i, 1)], min_val=0, max_val=NE - 1)
                act.wait_ge(s["h_turned"], i + 1 + 2)
                act.wait_ge(s["y_done"], i + 1)
                for m in range(HT):
                    last = nc.scalar.activation(hT[k % 2][:, m, :], HP[:, m * P:(m + 1) * P], ACT.Gelu,
                                                bias=big["b1"][:, bass.ds(e, 1), m:m + 1].rearrange("p a b -> p (a b)"))
                last.then_inc(s["hT_ready"], 1)

            shared(HALVES[0])
            act.wait_ge(s["choice"], 3)
            copy_x(0, 0)
            copy_x(1, 1)

            def emit(i, k):
                gelus(i, k)
                if not isinstance(i, int) or i + 2 < ST:
                    copy_x(i + 2, k + 2)

            tile_loop(act, emit, 1)
            shared(HALVES[1])

        @block.vector
        def _(dve):
            dve.sem_inc(s["hs_ready"], 2)
            dve.sem_inc(s["ys_ready"], 2)
            for k in range(TOP):
                last = nc.vector.scalar_tensor_tensor(picked[:, k, :, :], r["rank"][:, :, :], float(k), r["pr"][:, :, :],
                                                      ALU.is_equal, ALU.mult)
            nc.vector.tensor_tensor(reach[:, :, :], r["tile_no"][:, :].unsqueeze(2).to_broadcast([1, ST, NE - 1]),
                                    r["base"][0:1, 1:].unsqueeze(1).to_broadcast([1, ST, NE - 1]), ALU.is_ge)\
                .then_inc(s["choice"], 1)
            dve.wait_ge(s["choice"], 1)
            for k in range(TOP):
                nc.vector.tensor_reduce(r["w"][k][:, :], picked[:, k, :, :], AX.X, ALU.add)
            nc.vector.tensor_reduce(eid_f[:, :], reach[:, :, :], AX.X, ALU.add).then_inc(s["choice"], 1)
            dve.wait_ge(s["choice"], 2)
            nc.vector.tensor_copy(r["eid"][:, :], eid_f[:, :]).then_inc(s["choice"], 1)

            def shared(g, after_tile=None):
                dve.wait_ge(s["wT_turned"], g + 1)
                if g:
                    dve.wait_ge(s["sh_y"], g * GT)
                nc.vector.tensor_copy(wT[:, :], WP[0:EX, :]).then_inc(s["wT_ready"], 1)
                for t in range(GT):
                    k = g * GT + t
                    dve.wait_ge(s["sh_y"], k + 1)
                    xs = X[:, k * D:(k + 1) * D]
                    nc.vector.tensor_tensor(xs, YP[k % 2][:, 0:D], xs, ALU.add).then_inc(s["sh_added"], 1)
                    if after_tile:
                        after_tile(k)

            def combine_tile(t):
                dve.wait_ge(gathered[t % YG], 16 * TOP * (t // YG + 1))
                xs = X[:, t * D:(t + 1) * D]
                nc.vector.scalar_tensor_tensor(xs, yg[t % YG][0], r["w"][0][:, t:t + 1], xs, ALU.mult, ALU.add)\
                    .then_inc(s["mix"], 1)
                dve.wait_ge(s["mix"], t + 1)
                nc.vector.scalar_tensor_tensor(xs, yg[t % YG][1], r["w"][1][:, t:t + 1], xs, ALU.mult, ALU.add)\
                    .then_inc(s["combined"], 1)

            def copy_h(i, k):
                dve.wait_ge(s["up_done"], i + 1 + 2)
                dve.wait_ge(s["h_turned"], i + 1)
                nc.vector.tensor_copy(hs[k % 2], UP[k % 2][:, :]).then_inc(s["hs_ready"], 1)

            def copy_y(i, k):
                dve.wait_ge(s["y_done"], i + 1 + 2)
                dve.wait_ge(stored[k % 2], 16 * (i // 2 + 1))
                nc.vector.tensor_copy(ys[k % 2], YP[k % 2][:, 0:D]).then_inc(s["ys_ready"], 1)

            for g in HALVES[0]:
                shared(g)
            copy_h(0, 0)

            def emit(i, k):
                if not isinstance(i, int) or i + 1 < ST:
                    copy_h(i + 1, k + 1)
                copy_y(i, k)

            tile_loop(dve, emit, 1)
            def measure(t):
                if again:
                    dve.wait_ge(s["combined"], t + 1)
                    nc.vector.bn_stats(big["stats"][:, t, :], X[:, t * D:(t + 1) * D]).then_inc(s["measured"], 1)

            first = HALVES[1][0] * GT

            def join(k):
                for t in range(2 * (k - 1 - first), 2 * (k - first)):
                    if t >= 0:
                        if t >= first:
                            dve.wait_ge(s["sh_added"], t + 1)
                        combine_tile(t)
                    if t >= 2:
                        measure(t - 2)

            for g in HALVES[1]:
                shared(g, join)
            dve.wait_ge(s["sh_added"], NT)
            for t in range(2 * (NT - 1 - first), NT):
                combine_tile(t)
                measure(t - 2)
            measure(NT - 2)
            measure(NT - 1)
            if again:
                dve.wait_ge(s["measured"], NT)
                for t in range(NT):
                    nc.vector.bn_aggr(big["mv"][:, t, :], big["stats"][:, t, :])


NAMES = """L0_attn_a_hidden_states L0_attn_a_c_attn_kernel L0_attn_a_c_attn_bias L0_attn_a_c_proj_kernel
L0_attn_a_c_proj_bias L0_attn_b_Wq L0_attn_b_bq L0_attn_b_Wk L0_attn_b_bk L0_attn_b_Wv L0_attn_b_bv L0_attn_b_Wo
L0_attn_b_bo L0_attn_b_Wqs L0_attn_b_bqs L0_attn_b_Wks L0_attn_b_bks L0_attn_b_Wvs L0_attn_b_bvs L0_attn_b_temp
L0_ffn_router_w L0_ffn_router_b L0_ffn_sw1 L0_ffn_sb1 L0_ffn_sw2 L0_ffn_sb2 L0_ffn_rw1 L0_ffn_rb1 L0_ffn_rw2
L0_ffn_rb2""".split()


def kernel(**inputs):
    import numpy as np
    import concourse.bacc as bacc
    from concourse.bass_utils import run_bass_kernel_spmd

    nc = bacc.Bacc("TRN2", target_bir_lowering=False, num_devices=1)
    arrays, io = {}, {}
    for name in NAMES:
        a = np.ascontiguousarray(inputs[name])
        if a.ndim == 0:
            a = a.reshape(1)
        arrays[name] = a
        io[name] = nc.dram_tensor(name, a.shape, mybir.dt.from_np(a.dtype), kind="ExternalInput").ap()
    out = nc.dram_tensor("out", (B, S, D), F32, kind="ExternalOutput").ap()
    build(nc, io, out)
    r = run_bass_kernel_spmd(nc, [arrays], core_ids=[0])
    return r.results[0]["out"]
```
